# Optimizing a Trainium2 kernel written in Bass

```python
import numpy as np
import jax
import jax.numpy as jnp

def _softmax(x, axis=-1):
    return jax.nn.softmax(x, axis=axis)
def _gelu(x):
    return jax.nn.gelu(x, approximate=True)
def _silu(x):
    return jax.nn.silu(x)
def _sigmoid(x):
    return jax.nn.sigmoid(x)
def _layernorm(x, axis=-1, eps=1e-5):
    m = jnp.mean(x, axis=axis, keepdims=True)
    v = jnp.var(x, axis=axis, keepdims=True)
    return (x - m) / jnp.sqrt(v + eps)
def _scatter_add(tgt, idx, src, axis=0):
    return tgt.at[idx].add(src)
def _segment_sum(src, seg, n):
    return jax.ops.segment_sum(src, seg, n)

kernel_name = 'mk_conv_seq_d4_conv_nhwc256_c668d7'

def setup_inputs(seed: int = 0):
    np.random.seed(seed)
    _w = jnp.asarray
    def _rec_inputs():
        import jax
        import jax.numpy as jnp
        _gk = jax.random.key(seed)
        x = -0.0005207 + 1.001 * jax.random.normal(jax.random.fold_in(_gk, 1), (2, 64, 64, 256), jnp.float32)
        return x
    x = _rec_inputs()
    def _L0_conv_setup():
        import jax, jax.numpy as jnp
        import numpy as np
        B, H, W, C = (2, 64, 64, 256)
        NH, K = (8, 7)
        HD = C // NH

        def _ln(x, w, b, eps=1e-05):
            m = x.mean(-1, keepdims=True)
            v = ((x - m) ** 2).mean(-1, keepdims=True)
            return (x - m) * jax.lax.rsqrt(v + eps) * w + b

        def _nbr_idx(n, k):
            half = k // 2
            start = np.clip(np.arange(n) - half, 0, n - k)
            return jnp.asarray(start[:, None] + np.arange(k)[None, :])
        key = jax.random.key(seed)
        ks = jax.random.split(key, 5)
        s = lambda fan: 1.0 / np.sqrt(fan)
        return {'x': jax.random.normal(ks[0], (B, H, W, C), jnp.float32), 'ln1_w': jnp.ones((C,), jnp.float32), 'ln1_b': jnp.zeros((C,), jnp.float32), 'qkv_w': jax.random.normal(ks[1], (3 * C, C), jnp.float32) * s(C), 'qkv_b': jnp.zeros((3 * C,), jnp.float32), 'proj_w': jax.random.normal(ks[2], (C, C), jnp.float32) * s(C), 'proj_b': jnp.zeros((C,), jnp.float32), 'ln2_w': jnp.ones((C,), jnp.float32), 'ln2_b': jnp.zeros((C,), jnp.float32), 'fc1_w': jax.random.normal(ks[3], (4 * C, C), jnp.float32) * s(C), 'fc1_b': jnp.zeros((4 * C,), jnp.float32), 'fc2_w': jax.random.normal(ks[4], (C, 4 * C), jnp.float32) * s(4 * C), 'fc2_b': jnp.zeros((C,), jnp.float32)}
    _L0_conv_all = _L0_conv_setup()
    _L0_conv_in = {k: v for k, v in _L0_conv_all.items() if k in ('ln1_w', 'ln1_b', 'qkv_w', 'qkv_b', 'proj_w', 'proj_b', 'ln2_w', 'ln2_b', 'fc1_w', 'fc1_b', 'fc2_w', 'fc2_b', )}
    del _L0_conv_all

    def _L1_conv_setup():
        import jax, jax.numpy as jnp
        import numpy as np
        NUM_BLOCKS = 8
        HSF = 1
        LAMBDA = 0.01
        HTF = 1.0
        SCALE = 0.02

        def softshrink(v, lam):
            return jnp.where(v > lam, v - lam, jnp.where(v < -lam, v + lam, jnp.zeros_like(v)))
        key = jax.random.key(seed)
        ks = jax.random.split(key, 5)
        B, H, W, C = (1, 360, 720, 256)
        bs = C // NUM_BLOCKS
        x = jax.random.normal(ks[0], (B, H, W, C), dtype=jnp.float32)
        w1 = SCALE * jax.random.normal(ks[1], (2, NUM_BLOCKS, bs, bs * HSF), dtype=jnp.float32)
        b1 = SCALE * jax.random.normal(ks[2], (2, NUM_BLOCKS, bs * HSF), dtype=jnp.float32)
        w2 = SCALE * jax.random.normal(ks[3], (2, NUM_BLOCKS, bs * HSF, bs), dtype=jnp.float32)
        b2 = SCALE * jax.random.normal(ks[4], (2, NUM_BLOCKS, bs), dtype=jnp.float32)
        return {'x': x, 'w1': w1, 'b1': b1, 'w2': w2, 'b2': b2}
    _L1_conv_all = _L1_conv_setup()
    _L1_conv_in = {k: v for k, v in _L1_conv_all.items() if k in ('w1', 'b1', 'w2', 'b2', )}
    del _L1_conv_all

    def _L2_conv_setup():
        import jax, jax.numpy as jnp
        import numpy as np
        NUM_HEADS = 8
        KERNEL = 3

        def _arsinh_norm(x, w, b):
            return w * jnp.arcsinh(x) + b

        def _nbr_idx(L, k):
            start = jnp.clip(jnp.arange(L) - k // 2, 0, L - k)
            return start[:, None] + jnp.arange(k)

        def _na2d(x, qkv_w, qkv_b, proj_w, proj_b, num_heads=NUM_HEADS, k=KERNEL):
            B, H, W, C = x.shape
            hd = C // num_heads
            qkv = x @ qkv_w + qkv_b
            q, kk, v = jnp.split(qkv, 3, axis=-1)
            q = q.reshape(B, H, W, num_heads, hd) * hd ** (-0.5)
            kk = kk.reshape(B, H, W, num_heads, hd)
            v = v.reshape(B, H, W, num_heads, hd)
            ri = _nbr_idx(H, k)[:, None, :, None]
            ci = _nbr_idx(W, k)[None, :, None, :]
            nb_k = kk[:, ri, ci].reshape(B, H, W, k * k, num_heads, hd)
            nb_v = v[:, ri, ci].reshape(B, H, W, k * k, num_heads, hd)
            scores = jnp.einsum('bijnd,bijmnd->bijnm', q, nb_k)
            attn = jax.nn.softmax(scores, axis=-1)
            out = jnp.einsum('bijnm,bijmnd->bijnd', attn, nb_v).reshape(B, H, W, C)
            return out @ proj_w + proj_b
        key = jax.random.key(seed)
        ks = jax.random.split(key, 8)
        B, H, W, C = (16, 64, 64, 256)
        s = 0.02
        return {'h': jax.random.normal(ks[0], (B, H, W, C), dtype=jnp.float32), 'qkv_w': jax.random.normal(ks[1], (C, 3 * C), dtype=jnp.float32) * s, 'qkv_b': jnp.zeros((3 * C,), jnp.float32), 'proj_w': jax.random.normal(ks[2], (C, C), dtype=jnp.float32) * s, 'proj_b': jnp.zeros((C,), jnp.float32), 'n1_w': jnp.ones((C,), jnp.float32), 'n1_b': jnp.zeros((C,), jnp.float32), 'n2_w': jnp.ones((C,), jnp.float32), 'n2_b': jnp.zeros((C,), jnp.float32), 'mlp_w1': jax.random.normal(ks[3], (C, 2 * C), dtype=jnp.float32) * s, 'mlp_b1': jnp.zeros((2 * C,), jnp.float32), 'mlp_w2': jax.random.normal(ks[4], (2 * C, C), dtype=jnp.float32) * s, 'mlp_b2': jnp.zeros((C,), jnp.float32)}
    _L2_conv_all = _L2_conv_setup()
    _L2_conv_in = {k: v for k, v in _L2_conv_all.items() if k in ('qkv_w', 'qkv_b', 'proj_w', 'proj_b', 'n1_w', 'n1_b', 'n2_w', 'n2_b', 'mlp_w1', 'mlp_b1', 'mlp_w2', 'mlp_b2', )}
    del _L2_conv_all

    def _L3_conv_setup():
        import jax, jax.numpy as jnp
        import numpy as np
        N_GROUPS = 8
        N_HEADS = 4
        EPS = 1e-05

        def _group_norm(x, scale, bias):
            B, H, W, C = x.shape
            g = N_GROUPS
            xg = x.reshape(B, H, W, g, C // g)
            mean = xg.mean(axis=(1, 2, 4), keepdims=True)
            var = xg.var(axis=(1, 2, 4), keepdims=True)
            xn = ((xg - mean) * jax.lax.rsqrt(var + EPS)).reshape(B, H, W, C)
            return xn * scale + bias
        key = jax.random.key(seed)
        ks = jax.random.split(key, 4)
        B, H, W, C = (4, 64, 64, 256)
        x = jax.random.normal(ks[0], (B, H, W, C), dtype=jnp.float32)
        gn_scale = jnp.ones((C,), dtype=jnp.float32)
        gn_bias = jnp.zeros((C,), dtype=jnp.float32)
        w_qkv = jax.random.normal(ks[1], (C, 3 * C), dtype=jnp.float32) * C ** (-0.5)
        w_out = jax.random.normal(ks[2], (C, C), dtype=jnp.float32) * C ** (-0.5)
        b_out = jnp.zeros((C,), dtype=jnp.float32)
        return {'x': x, 'gn_scale': gn_scale, 'gn_bias': gn_bias, 'w_qkv': w_qkv, 'w_out': w_out, 'b_out': b_out}
    _L3_conv_all = _L3_conv_setup()
    _L3_conv_in = {k: v for k, v in _L3_conv_all.items() if k in ('gn_scale', 'gn_bias', 'w_qkv', 'w_out', 'b_out', )}
    del _L3_conv_all

    return {
        "x": x,
        "L0_conv_ln1_w": _L0_conv_in["ln1_w"],
        "L0_conv_ln1_b": _L0_conv_in["ln1_b"],
        "L0_conv_qkv_w": _L0_conv_in["qkv_w"],
        "L0_conv_qkv_b": _L0_conv_in["qkv_b"],
        "L0_conv_proj_w": _L0_conv_in["proj_w"],
        "L0_conv_proj_b": _L0_conv_in["proj_b"],
        "L0_conv_ln2_w": _L0_conv_in["ln2_w"],
        "L0_conv_ln2_b": _L0_conv_in["ln2_b"],
        "L0_conv_fc1_w": _L0_conv_in["fc1_w"],
        "L0_conv_fc1_b": _L0_conv_in["fc1_b"],
        "L0_conv_fc2_w": _L0_conv_in["fc2_w"],
        "L0_conv_fc2_b": _L0_conv_in["fc2_b"],
        "L1_conv_w1": _L1_conv_in["w1"],
        "L1_conv_b1": _L1_conv_in["b1"],
        "L1_conv_w2": _L1_conv_in["w2"],
        "L1_conv_b2": _L1_conv_in["b2"],
        "L2_conv_qkv_w": _L2_conv_in["qkv_w"],
        "L2_conv_qkv_b": _L2_conv_in["qkv_b"],
        "L2_conv_proj_w": _L2_conv_in["proj_w"],
        "L2_conv_proj_b": _L2_conv_in["proj_b"],
        "L2_conv_n1_w": _L2_conv_in["n1_w"],
        "L2_conv_n1_b": _L2_conv_in["n1_b"],
        "L2_conv_n2_w": _L2_conv_in["n2_w"],
        "L2_conv_n2_b": _L2_conv_in["n2_b"],
        "L2_conv_mlp_w1": _L2_conv_in["mlp_w1"],
        "L2_conv_mlp_b1": _L2_conv_in["mlp_b1"],
        "L2_conv_mlp_w2": _L2_conv_in["mlp_w2"],
        "L2_conv_mlp_b2": _L2_conv_in["mlp_b2"],
        "L3_conv_gn_scale": _L3_conv_in["gn_scale"],
        "L3_conv_gn_bias": _L3_conv_in["gn_bias"],
        "L3_conv_w_qkv": _L3_conv_in["w_qkv"],
        "L3_conv_w_out": _L3_conv_in["w_out"],
        "L3_conv_b_out": _L3_conv_in["b_out"],
    }

def reference(x, L0_conv_ln1_w, L0_conv_ln1_b, L0_conv_qkv_w, L0_conv_qkv_b, L0_conv_proj_w, L0_conv_proj_b, L0_conv_ln2_w, L0_conv_ln2_b, L0_conv_fc1_w, L0_conv_fc1_b, L0_conv_fc2_w, L0_conv_fc2_b, L1_conv_w1, L1_conv_b1, L1_conv_w2, L1_conv_b2, L2_conv_qkv_w, L2_conv_qkv_b, L2_conv_proj_w, L2_conv_proj_b, L2_conv_n1_w, L2_conv_n1_b, L2_conv_n2_w, L2_conv_n2_b, L2_conv_mlp_w1, L2_conv_mlp_b1, L2_conv_mlp_w2, L2_conv_mlp_b2, L3_conv_gn_scale, L3_conv_gn_bias, L3_conv_w_qkv, L3_conv_w_out, L3_conv_b_out):
    import jax
    import jax.numpy as jnp
    def _L0_conv_ref(x, ln1_w, ln1_b, qkv_w, qkv_b, proj_w, proj_b, ln2_w, ln2_b, fc1_w, fc1_b, fc2_w, fc2_b):
        import jax, jax.numpy as jnp
        import numpy as np
        B, H, W, C = (2, 64, 64, 256)
        NH, K = (8, 7)
        HD = C // NH

        def _ln(x, w, b, eps=1e-05):
            m = x.mean(-1, keepdims=True)
            v = ((x - m) ** 2).mean(-1, keepdims=True)
            return (x - m) * jax.lax.rsqrt(v + eps) * w + b

        def _nbr_idx(n, k):
            half = k // 2
            start = np.clip(np.arange(n) - half, 0, n - k)
            return jnp.asarray(start[:, None] + np.arange(k)[None, :])
        shortcut = x
        xn = _ln(x, ln1_w, ln1_b)
        qkv = (xn @ qkv_w.T + qkv_b).reshape(B, H, W, 3, NH, HD)
        qkv = jnp.transpose(qkv, (3, 0, 4, 1, 2, 5))
        q, k, v = (qkv[0], qkv[1], qkv[2])
        q = q * HD ** (-0.5)
        ih = _nbr_idx(H, K)[:, None, :, None]
        iw = _nbr_idx(W, K)[None, :, None, :]
        k_nb = k[:, :, ih, iw, :].reshape(B, NH, H, W, K * K, HD)
        v_nb = v[:, :, ih, iw, :].reshape(B, NH, H, W, K * K, HD)
        attn = jnp.einsum('bnijd,bnijkd->bnijk', q, k_nb)
        attn = jax.nn.softmax(attn, axis=-1)
        out = jnp.einsum('bnijk,bnijkd->bnijd', attn, v_nb)
        out = jnp.transpose(out, (0, 2, 3, 1, 4)).reshape(B, H, W, C)
        out = out @ proj_w.T + proj_b
        x = shortcut + out
        h = _ln(x, ln2_w, ln2_b)
        h = jax.nn.gelu(h @ fc1_w.T + fc1_b, approximate=False)
        h = h @ fc2_w.T + fc2_b
        return x + h

    def _L1_conv_ref(x, w1, b1, w2, b2):
        import jax, jax.numpy as jnp
        import numpy as np
        NUM_BLOCKS = 8
        HSF = 1
        LAMBDA = 0.01
        HTF = 1.0
        SCALE = 0.02

        def softshrink(v, lam):
            return jnp.where(v > lam, v - lam, jnp.where(v < -lam, v + lam, jnp.zeros_like(v)))
        B, H, W, C = x.shape
        nb = NUM_BLOCKS
        bs = C // nb
        Wf = W // 2 + 1
        bias = x
        xf = jnp.fft.rfft2(x.astype(jnp.float32), axes=(1, 2), norm='ortho')
        xf = xf.reshape(B, H, Wf, nb, bs)
        km = int((H // 2 + 1) * HTF)
        xk = xf[:, -km:, :km]
        xr, xi = (jnp.real(xk), jnp.imag(xk))
        o1r = jax.nn.relu(jnp.einsum('bhwni,nio->bhwno', xr, w1[0]) - jnp.einsum('bhwni,nio->bhwno', xi, w1[1]) + b1[0])
        o1i = jax.nn.relu(jnp.einsum('bhwni,nio->bhwno', xi, w1[0]) + jnp.einsum('bhwni,nio->bhwno', xr, w1[1]) + b1[1])
        o2r = jnp.einsum('bhwno,nok->bhwnk', o1r, w2[0]) - jnp.einsum('bhwno,nok->bhwnk', o1i, w2[1]) + b2[0]
        o2i = jnp.einsum('bhwno,nok->bhwnk', o1i, w2[0]) + jnp.einsum('bhwno,nok->bhwnk', o1r, w2[1]) + b2[1]
        o2r = softshrink(o2r, LAMBDA)
        o2i = softshrink(o2i, LAMBDA)
        full = jnp.zeros((B, H, Wf, nb, bs), dtype=jnp.complex64)
        full = full.at[:, -km:, :km].set(jax.lax.complex(o2r, o2i))
        full = full.reshape(B, H, Wf, C)
        out = jnp.fft.irfft2(full, s=(H, W), axes=(1, 2), norm='ortho').astype(x.dtype)
        return out + bias

    def _L2_conv_ref(h, qkv_w, qkv_b, proj_w, proj_b, n1_w, n1_b, n2_w, n2_b, mlp_w1, mlp_b1, mlp_w2, mlp_b2):
        import jax, jax.numpy as jnp
        import numpy as np
        NUM_HEADS = 8
        KERNEL = 3

        def _arsinh_norm(x, w, b):
            return w * jnp.arcsinh(x) + b

        def _nbr_idx(L, k):
            start = jnp.clip(jnp.arange(L) - k // 2, 0, L - k)
            return start[:, None] + jnp.arange(k)

        def _na2d(x, qkv_w, qkv_b, proj_w, proj_b, num_heads=NUM_HEADS, k=KERNEL):
            B, H, W, C = x.shape
            hd = C // num_heads
            qkv = x @ qkv_w + qkv_b
            q, kk, v = jnp.split(qkv, 3, axis=-1)
            q = q.reshape(B, H, W, num_heads, hd) * hd ** (-0.5)
            kk = kk.reshape(B, H, W, num_heads, hd)
            v = v.reshape(B, H, W, num_heads, hd)
            ri = _nbr_idx(H, k)[:, None, :, None]
            ci = _nbr_idx(W, k)[None, :, None, :]
            nb_k = kk[:, ri, ci].reshape(B, H, W, k * k, num_heads, hd)
            nb_v = v[:, ri, ci].reshape(B, H, W, k * k, num_heads, hd)
            scores = jnp.einsum('bijnd,bijmnd->bijnm', q, nb_k)
            attn = jax.nn.softmax(scores, axis=-1)
            out = jnp.einsum('bijnm,bijmnd->bijnd', attn, nb_v).reshape(B, H, W, C)
            return out @ proj_w + proj_b
        h1 = _arsinh_norm(h, n1_w, n1_b)
        h = h + _na2d(h1, qkv_w, qkv_b, proj_w, proj_b)
        h2 = _arsinh_norm(h, n2_w, n2_b)
        ff = jax.nn.gelu(h2 @ mlp_w1 + mlp_b1, approximate=False) @ mlp_w2 + mlp_b2
        return h + ff

    def _L3_conv_ref(x, gn_scale, gn_bias, w_qkv, w_out, b_out):
        import jax, jax.numpy as jnp
        import numpy as np
        N_GROUPS = 8
        N_HEADS = 4
        EPS = 1e-05

        def _group_norm(x, scale, bias):
            B, H, W, C = x.shape
            g = N_GROUPS
            xg = x.reshape(B, H, W, g, C // g)
            mean = xg.mean(axis=(1, 2, 4), keepdims=True)
            var = xg.var(axis=(1, 2, 4), keepdims=True)
            xn = ((xg - mean) * jax.lax.rsqrt(var + EPS)).reshape(B, H, W, C)
            return xn * scale + bias
        B, H, W, C = x.shape
        hd = C // N_HEADS
        scale = C ** (-0.5)
        xn = _group_norm(x, gn_scale, gn_bias)
        qkv = jnp.einsum('bhwc,cd->bhwd', xn, w_qkv)
        qkv = qkv.reshape(B, H * W, N_HEADS, 3 * hd)
        q, k, v = jnp.split(qkv, 3, axis=-1)
        atten = jnp.einsum('bihd,bjhd->bijh', q, k) * scale
        atten = jax.nn.softmax(atten, axis=2)
        res = jnp.einsum('bijh,bjhd->bihd', atten, v)
        res = res.reshape(B, H, W, C)
        res = jnp.einsum('bhwc,cd->bhwd', res, w_out) + b_out
        return res + xn

    def _gn(v, G=32, eps=1e-5):
        B_, H_, W_, C_ = v.shape
        g = v.reshape(B_, H_, W_, G, C_ // G)
        m = jnp.mean(g, axis=(1, 2, 4), keepdims=True)
        s = jnp.var(g, axis=(1, 2, 4), keepdims=True)
        return ((g - m) / jnp.sqrt(s + eps)).reshape(v.shape)

    def _ln_c(v, eps=1e-6):
        m = jnp.mean(v, axis=-1, keepdims=True)
        s = jnp.var(v, axis=-1, keepdims=True)
        return (v - m) / jnp.sqrt(s + eps)

    def _ln_t(v, eps=1e-5):
        m = jnp.mean(v, axis=-1, keepdims=True)
        s = jnp.var(v, axis=-1, keepdims=True)
        return (v - m) / jnp.sqrt(s + eps)

    def _to_tokens(v):
        B_, H_, W_, C_ = v.shape
        return v.reshape(B_, H_ * W_, C_)
    def _from_tokens(t, like):
        return t.reshape(like.shape)

    x = _L0_conv_ref(x, L0_conv_ln1_w, L0_conv_ln1_b, L0_conv_qkv_w, L0_conv_qkv_b, L0_conv_proj_w, L0_conv_proj_b, L0_conv_ln2_w, L0_conv_ln2_b, L0_conv_fc1_w, L0_conv_fc1_b, L0_conv_fc2_w, L0_conv_fc2_b)
    x = _L1_conv_ref(x, L1_conv_w1, L1_conv_b1, L1_conv_w2, L1_conv_b2)
    x = _L2_conv_ref(x, L2_conv_qkv_w, L2_conv_qkv_b, L2_conv_proj_w, L2_conv_proj_b, L2_conv_n1_w, L2_conv_n1_b, L2_conv_n2_w, L2_conv_n2_b, L2_conv_mlp_w1, L2_conv_mlp_b1, L2_conv_mlp_w2, L2_conv_mlp_b2)
    x = _L3_conv_ref(x, L3_conv_gn_scale, L3_conv_gn_bias, L3_conv_w_qkv, L3_conv_w_out, L3_conv_b_out)
    return x


_drawn_inputs = setup_inputs


def setup_inputs(seed=0):
    import zlib

    import numpy as np

    out = dict(_drawn_inputs(seed))
    spreads = {'L0_conv_ln1_w': (1.0, 0.2),
     'L0_conv_ln1_b': (0.0, 0.1),
     'L0_conv_qkv_b': (0.0, 0.1),
     'L0_conv_proj_b': (0.0, 0.1),
     'L0_conv_ln2_w': (1.0, 0.2),
     'L0_conv_ln2_b': (0.0, 0.1),
     'L0_conv_fc1_b': (0.0, 0.1),
     'L0_conv_fc2_b': (0.0, 0.1),
     'L2_conv_qkv_b': (0.0, 0.1),
     'L2_conv_proj_b': (0.0, 0.1),
     'L2_conv_n1_w': (1.0, 0.6),
     'L2_conv_n1_b': (0.0, 0.797),
     'L2_conv_n2_w': (1.0, 0.6),
     'L2_conv_n2_b': (0.0, 0.8),
     'L2_conv_mlp_b1': (0.0, 0.394),
     'L2_conv_mlp_b2': (0.0, 0.1),
     'L3_conv_gn_scale': (1.0, 0.2),
     'L3_conv_gn_bias': (0.0, 0.1),
     'L3_conv_b_out': (0.0, 0.1)}
    factors = {'L1_conv_w1': 7.91, 'L1_conv_b1': 8.0, 'L1_conv_w2': 6.51, 'L1_conv_b2': 5.312}
    for name, (base, spread) in spreads.items():
        noise = np.random.default_rng([zlib.crc32(name.encode()), seed]).standard_normal(out[name].shape)
        drawn = base * np.exp(spread * noise) if base else spread * noise
        out[name] = jnp.asarray(drawn.astype(out[name].dtype))
    for name, factor in factors.items():
        out[name] = (out[name] * factor).astype(out[name].dtype)
    return out
```

```python
import math
from contextlib import ExitStack

import numpy as np
import concourse.bass as bass
from concourse import mybir

F32 = mybir.dt.float32
F16 = mybir.dt.float16
BF16 = mybir.dt.bfloat16
ALU = mybir.AluOpType
ACT = mybir.ActivationFunctionType
AX = mybir.AxisListType

P = 128
B, H, W, C = 2, 64, 64, 256
T = B * H * W
GT = 512
GROUPS = T // GT
TPG = GT // P
CH = C // P
PR, PC = 8, 16
LN_EPS = 1e-5
OPERAND_SCALE = 16.0
PROB_SCALE = 1024.0
FREE = 1


class Phase:

    def __init__(self, nc, name):
        self.nc, self.name, self.stack = nc, name, ExitStack()
        self.used = []

    def __enter__(self):
        self.stack.__enter__()
        return self

    def __exit__(self, *e):
        self.blocks.__exit__(*e)
        for sem in self.used:
            self.nc.sync.sem_clear(sem)
        self.nc.all_engine_barrier()
        return self.stack.__exit__(*e)

    def sb(self, name, shape, dt=F32):
        return self.stack.enter_context(self.nc.sbuf_tensor(f"{self.name}_{name}", shape, dt))

    def ps(self, name, shape, dt=F32):
        return self.stack.enter_context(self.nc.psum_tensor(f"{self.name}_{name}", shape, dt))

    def sem(self, name):
        self.used.append(self.stack.enter_context(self.nc.semaphore(f"{self.name}_{name}")))
        return self.used[-1]

    def sems(self, name, n):
        return [self.sem(f"{name}{k}") for k in range(n)]

    def block(self):
        self.blocks = self.nc.Block()
        return self.blocks.__enter__()


def passed(eng, marker):
    eng.sem_inc(marker, 1)


class Chain:

    def __init__(self, eng, sem, start=0):
        self.eng, self.sem, self.start, self.n = eng, sem, start, 0

    def step(self, ins):
        ins.then_inc(self.sem, 1)
        self.n += 1

    def settle(self):
        self.eng.wait_ge(self.sem, self.start + self.n)

    def link(self, ins):
        self.step(ins)
        self.settle()


def row(ap):
    return ap.rearrange("(o n) -> o n", o=1).broadcast_to([P, ap.shape[0]])



def front_phase(nc, name, kind, x, ident, w_qkv, b_qk, b_v, gamma, beta, qk_out, v_out, heads,
                q_patches, group_affine=None, xn_out=None):
    hd = C // heads
    vw = 2 * hd + 1
    V_UNITS, QK_UNITS = 2, 4
    UNITS = V_UNITS + QK_UNITS
    with Phase(nc, name) as ph:
        idt = ph.sb("ident", [P, P])
        w = ph.sb("w", [P, CH, 3 * C])
        x_in = [ph.sb(f"x{u}", [P, TPG, C]) for u in range(2)]
        xn = [ph.sb(f"xn{u}", [P, TPG, C]) for u in range(2)]
        aux = ph.sb("aux", [P, TPG, C])
        root = ph.sb("root", [P, TPG, C])
        stats = ph.sb("stats", [P, TPG, 6])
        mv = ph.sb("mv", [P, TPG, 2])
        std = ph.sb("std", [P, TPG])
        rstd = ph.sb("rstd", [P, TPG])
        eps = ph.sb("eps", [P, 1])
        ab = [ph.sb(f"ab{u}", [P, 2, C]) for u in range(2)]
        gcol = ph.sb("gamma", [P, CH])
        bcol = ph.sb("beta", [P, CH])
        qkb = ph.sb("qkb", [P, 4])
        vb = ph.sb("vb", [P, C])
        xT = ph.sb("xT", [P, CH, GT])
        lin = ph.sb("lin", [P, QK_UNITS, 512])
        vlin = ph.sb("vlin", [P, V_UNITS, 512])
        qks = [ph.sb(f"qks{u}", [P, 4, 2, GT], F16) for u in range(2)]
        vs = [ph.sb(f"vs{u}", [P, TPG, heads * vw], F16) for u in range(2)]
        tp = [ph.ps(f"tp{c}", [P, GT]) for c in range(CH)]
        mm = [ph.ps(f"mm{k}", [P, 512]) for k in range(UNITS)]

        weights_in = ph.sem("weights_in")
        sp_marker = ph.sem("sp_marker")
        consts = ph.sem("consts")
        bias_ready = ph.sem("bias_ready")
        x_loaded = ph.sems("x_loaded", 2)
        x_used = ph.sems("x_used", 2)
        act_steps = ph.sem("act_steps")
        dve_steps = ph.sem("dve_steps")
        marker = ph.sem("marker")
        var_ready = ph.sem("var_ready")
        std_ready = ph.sem("std_ready")
        root_ready = ph.sem("root_ready")
        sum_ready = ph.sem("sum_ready")
        log_ready = ph.sem("log_ready")
        xn_ready = ph.sem("xn_ready")
        tp_ready = ph.sem("tp_ready")
        xt_ready = ph.sem("xt_ready")
        mm_ready = ph.sem("mm_ready")
        qk_hi = ph.sem("qk_hi")
        qk_lo = ph.sem("qk_lo")
        v_split = ph.sem("v_split")
        qk_stored = ph.sems("qk_stored", 2)
        v_stored = ph.sems("v_stored", 2)
        xn_stored = ph.sems("xn_stored", 2)
        block = ph.block()

        loads = [(idt[:, :], ident), (w[:, :, :], w_qkv.rearrange("(c p) n -> p c n", p=P))]
        if gamma is not None:
            loads += [(gcol[:, :], gamma), (bcol[:, :], beta)]
        if b_qk is not None:
            loads += [(qkb[:, :], b_qk), (vb[:, :], row(b_v))]
        per_x = 16 * (1 + (group_affine is not None))

        @block.sync
        def _(sp):
            def load(g, u):
                sp.dma_start(x_in[u][:, :, :],
                             x[bass.ds(g * GT, GT)].rearrange("(t p) c -> p t c", p=P)).then_inc(x_loaded[u], 16)
                if group_affine is not None:
                    sp.dma_start(ab[u][:, :, :], group_affine[bass.ds(g, 1)].broadcast_to([P, 2, C])).then_inc(x_loaded[u], 16)

            def store(g, u):
                if xn_out is not None:
                    sp.wait_ge(xn_ready, g + 1 + FREE)
                    sp.dma_start(xn_out[bass.ds(g * GT, GT)].rearrange("(t p) f -> p t f", p=P),
                                 xn[u][:, :, :]).then_inc(xn_stored[u], 16)
                sp.wait_ge(v_split, g + 1)
                sp.dma_start(v_out[bass.ds(g * GT, GT)].rearrange("(t p) f -> p t f", p=P),
                             vs[u][:, :, :]).then_inc(v_stored[u], 16)
                for m in range(QK_UNITS):
                    sp.wait_ge(qk_lo, QK_UNITS * g + m + 1 + FREE)
                    passed(sp, sp_marker)
                    some = slice((m % 2) * (heads // 2), (m % 2 + 1) * (heads // 2))
                    for s in range(2):
                        sp.dma_start(qk_out[m // 2, some, s, :, bass.ds(g * GT, GT)],
                                     qks[u][:, m, s, :]).then_inc(qk_stored[u], 16)

            for u in range(2):
                load(u, u)
            for dst, src in loads:
                sp.dma_start(dst, src).then_inc(weights_in, 16)
            with sp.Fori(0, GROUPS // 2 - 1) as i:
                for u in range(2):
                    store(2 * i + u, u)
                    sp.wait_ge(x_used[u], i + 1)
                    load(2 * i + 2 + u, u)
            for u in range(2):
                store(GROUPS - 2 + u, u)
            for u in range(2):
                sp.wait_ge(qk_stored[u], 32 * QK_UNITS * (GROUPS // 2) + FREE)
                sp.wait_ge(v_stored[u], 16 * (GROUPS // 2) + FREE)
                if xn_out is not None:
                    sp.wait_ge(xn_stored[u], 16 * (GROUPS // 2) + FREE)

        @block.gpsimd
        def _(pool):
            pool.sem_inc(qk_lo, FREE)
            pool.memset(eps[:, :], LN_EPS).then_inc(consts, 1)
            for u in range(2):
                v = vs[u][:, :, :].rearrange("p t (h f) -> p (t h) f", f=vw)
                pool.memset(v[:, :, hd:hd + 1], OPERAND_SCALE).then_inc(consts, 1)
            with pool.Fori(0, GROUPS // 2) as i:
                for u in range(2):
                    g = 2 * i + u
                    for m in range(QK_UNITS):
                        pool.wait_ge(qk_hi, QK_UNITS * g + m + 1)
                        pool.tensor_tensor(qks[u][:, m, 1, :], lin[:, m, :], qks[u][:, m, 0, :],
                                           ALU.subtract).then_inc(qk_lo, 1)

        @block.tensor
        def _(pe):
            pe.wait_ge(weights_in, 16 * len(loads))
            with pe.Fori(0, GROUPS // 2) as i:
                for u in range(2):
                    g = 2 * i + u
                    pe.wait_ge(xn_ready, g + 1 + FREE)
                    pe.wait_ge(xt_ready, CH * g + FREE)
                    for c in range(CH):
                        for t in range(TPG):
                            last = pe.transpose(tp[c][:, t * P:(t + 1) * P], xn[u][:, t, c * P:(c + 1) * P], idt[:, :])
                        last.then_inc(tp_ready, 1)
                    pe.wait_ge(xt_ready, CH * (g + 1) + FREE)
                    for k in range(UNITS):
                        bank = mm[k]
                        if k < V_UNITS:
                            for t in range(2):
                                for c in range(CH):
                                    tt = 2 * k + t
                                    last = pe.matmul(bank[:, t * C:(t + 1) * C], xT[:, c, tt * P:(tt + 1) * P],
                                                     w[:, c, 2 * C:3 * C], start=(c == 0), stop=(c == CH - 1))
                        else:
                            m = k - V_UNITS
                            for c in range(CH):
                                last = pe.matmul(bank[:, :], w[:, c, m * P:(m + 1) * P], xT[:, c, :],
                                                 start=(c == 0), stop=(c == CH - 1))
                        last.then_inc(mm_ready, 1)

        @block.scalar
        def _(act):
            act.sem_inc(xt_ready, FREE)
            for u in range(2):
                act.sem_inc(qk_stored[u], FREE)
            act.wait_ge(weights_in, 16 * len(loads))
            act.wait_ge(consts, 3)
            if b_qk is not None:
                act.mul(qkb[:, :], qkb[:, :], OPERAND_SCALE).then_inc(bias_ready, 1)
                act.mul(vb[:, :], vb[:, :], OPERAND_SCALE).then_inc(bias_ready, 1)
                act.wait_ge(bias_ready, 2)
            with act.Fori(0, GROUPS // 2) as i:
                for u in range(2):
                    g = 2 * i + u
                    if kind == "layer":
                        act.wait_ge(var_ready, g + 1)
                        act.activation(std[:, :], mv[:, :, 1], ACT.Sqrt, bias=eps[:, :]).then_inc(std_ready, 1)
                    if kind == "arsinh":
                        steps = Chain(act, act_steps, 2 * g)
                        act.wait_ge(x_loaded[u], per_x * (i + 1))
                        act.wait_ge(xn_ready, g + FREE)
                        steps.link(act.activation(root[:, :, :], x_in[u][:, :, :], ACT.Square))
                        act.activation(root[:, :, :], root[:, :, :], ACT.Sqrt, bias=1.0).then_inc(root_ready, 1)
                        act.wait_ge(sum_ready, g + 1)
                        steps.link(act.activation(aux[:, :, :], aux[:, :, :], ACT.Ln))
                        act.activation(root[:, :, :], x_in[u][:, :, :], ACT.Sign).then_inc(log_ready, 1)
                    for c in range(CH):
                        act.wait_ge(tp_ready, CH * g + c + 1)
                        if gamma is None:
                            ins = act.activation(xT[:, c, :], tp[c][:, :], ACT.Identity)
                        else:
                            ins = act.activation(xT[:, c, :], tp[c][:, :], ACT.Identity,
                                                 bias=bcol[:, c:c + 1], scale=gcol[:, c:c + 1])
                        ins.then_inc(xt_ready, 1)
                    act.wait_ge(qk_stored[u], 32 * QK_UNITS * i + FREE)
                    act.wait_ge(qk_lo, QK_UNITS * g + FREE)
                    for m in range(QK_UNITS):
                        act.wait_ge(mm_ready, UNITS * g + V_UNITS + m + 1)
                        bank = mm[V_UNITS + m]
                        bias = qkb[:, m:m + 1] if b_qk is not None else 0.0
                        src, whole, high = bank[:, :], lin[:, m, :], qks[u][:, m, 0, :]
                        if q_patches and m < 2:
                            src = src.rearrange("p (r t c) -> p t r c", r=PR, c=PC)
                            whole, high = (y.rearrange("p (t r c) -> p t r c", r=PR, c=PC) for y in (whole, high))
                        act.activation(whole, src, ACT.Identity, bias=bias, scale=OPERAND_SCALE)
                        act.activation(high, src, ACT.Identity, bias=bias, scale=OPERAND_SCALE).then_inc(qk_hi, 1)

        @block.vector
        def _(dve):
            dve.sem_inc(xn_ready, FREE)
            for u in range(2):
                dve.sem_inc(xn_stored[u], FREE)
            for u in range(2):
                dve.sem_inc(v_stored[u], FREE)
            if b_qk is not None:
                dve.wait_ge(bias_ready, 2)
            dve.wait_ge(consts, 3)
            own = {"layer": 2, "arsinh": 1, "group": 1}[kind] + 2 * V_UNITS
            with dve.Fori(0, GROUPS // 2) as i:
                for u in range(2):
                    g = 2 * i + u
                    steps = Chain(dve, dve_steps, own * g)
                    dve.wait_ge(x_loaded[u], per_x * (i + 1))
                    if xn_out is not None:
                        dve.wait_ge(xn_stored[u], 16 * i + FREE)
                    if kind == "layer":
                        for t in range(TPG):
                            last = dve.bn_stats(stats[:, t, :], x_in[u][:, t, :])
                        steps.link(last)
                        passed(dve, marker)
                        for t in range(TPG):
                            last = dve.bn_aggr(mv[:, t, :], stats[:, t, :])
                        last.then_inc(var_ready, 1)
                        dve.wait_ge(var_ready, g + 1)
                        dve.wait_ge(std_ready, g + 1)
                        steps.link(dve.reciprocal(rstd[:, :], std[:, :]))
                        for t in range(TPG):
                            last = dve.tensor_scalar(xn[u][:, t, :], x_in[u][:, t, :], mv[:, t, 0:1],
                                                     rstd[:, t:t + 1], ALU.subtract, ALU.mult)
                    if kind == "arsinh":
                        steps.link(dve.scalar_tensor_tensor(aux[:, :, :], x_in[u][:, :, :], -1.0, x_in[u][:, :, :],
                                                            ALU.mult, ALU.max))
                        dve.wait_ge(root_ready, g + 1)
                        dve.tensor_tensor(aux[:, :, :], aux[:, :, :], root[:, :, :], ALU.add).then_inc(sum_ready, 1)
                        dve.wait_ge(log_ready, g + 1)
                        last = dve.tensor_tensor(xn[u][:, :, :], aux[:, :, :], root[:, :, :], ALU.mult)
                    if kind == "group":
                        a = ab[u][:, 0:1, :].broadcast_to([P, TPG, C])
                        b = ab[u][:, 1:2, :].broadcast_to([P, TPG, C])
                        steps.link(dve.tensor_tensor(aux[:, :, :], x_in[u][:, :, :], a, ALU.mult))
                        last = dve.tensor_tensor(xn[u][:, :, :], aux[:, :, :], b, ALU.add)
                    last.then_inc(xn_ready, 1)
                    dve.wait_ge(xn_ready, g + 1 + FREE)
                    dve.sem_inc(x_used[u], 1)
                    dve.wait_ge(v_stored[u], 16 * i + FREE)
                    for k in range(V_UNITS):
                        dve.wait_ge(mm_ready, UNITS * g + k + 1)
                        src = mm[k][:, :].rearrange("p (t c) -> p t c", c=C)
                        dst = vlin[:, k, :].rearrange("p (t c) -> p t c", c=C)
                        if b_qk is not None:
                            bias = vb[:, :].rearrange("p (o c) -> p o c", o=1).broadcast_to([P, 2, C])
                            ins = dve.scalar_tensor_tensor(dst, src, OPERAND_SCALE, bias, ALU.mult, ALU.add)
                        else:
                            ins = dve.tensor_scalar(dst, src, OPERAND_SCALE, None, ALU.mult)
                        steps.link(ins)
                        whole = vlin[:, k, :].rearrange("p (h f) -> p h f", f=hd)
                        parts = vs[u][:, 2 * k:2 * k + 2, :].rearrange("p t (h f) -> p (t h) f", f=vw)
                        steps.link(dve.tensor_copy(parts[:, :, 0:hd], whole))
                        last = dve.tensor_tensor(parts[:, :, hd + 1:vw], whole, parts[:, :, 0:hd], ALU.subtract)
                    last.then_inc(v_split, 1)
                    dve.wait_ge(v_split, g + 1)
                    assert steps.n == own


def global_attention_phase(nc, name, qk, v, ident, out, heads, scale):
    S = H * W
    hd = C // heads
    vw = 2 * hd + 1
    assert 2 * hd == P
    QB = S // GT
    KT = S // P
    QT = GT // P
    KC = S // 512
    UNITS = QT * KC
    MAX_STEPS = 26
    MM_STEP, ROW_STEP, COPY_STEP = 26, 28, 29
    HEADS = B * heads
    STAT = 256.0
    exp_scale = scale / OPERAND_SCALE ** 2

    def units_of(kt):
        if kt >= MAX_STEPS:
            return range(0)
        return range(kt * UNITS // MAX_STEPS, (kt + 1) * UNITS // MAX_STEPS)

    def by_pool(kt):
        return kt % 4 == 3

    def lows(kt):
        n = sum(by_pool(x) for x in range(kt + 1))
        return kt + 1 - n, n

    D_LOWS, P_LOWS = lows(KT - 1)

    with Phase(nc, name) as ph:
        idf = ph.sb("ident", [P, P])
        id16 = ph.sb("ident16", [P, P], F16)
        q_hl = [ph.sb(f"q_hl{u}", [P, S], F16) for u in range(2)]
        q_hm = [ph.sb(f"q_hm{u}", [P, S], F16) for u in range(2)]
        k_hh = [ph.sb(f"k_hh{u}", [P, S], F16) for u in range(2)]
        k_ll = [ph.sb(f"k_ll{u}", [P, S], F16) for u in range(2)]
        k_lc = [ph.sb(f"k_lc{u}", [P, S], F16) for u in range(2)]
        vt = [ph.sb(f"v{u}", [P, KT, vw], F16) for u in range(2)]
        o_head = [ph.sb(f"o{u}", [P, S // P, hd]) for u in range(2)]
        part_max = ph.sb("part_max", [P, QT, KC])
        neg_max = ph.sb("neg_max", [P, QT])
        max_cols = ph.sb("max_cols", [P, QT, P], F16)
        shift = ph.sb("shift", [P, 1])
        p32 = [ph.sb(f"p32_{k}", [P, GT]) for k in range(2)]
        p_hi = [ph.sb(f"p_hi{k}", [P, GT], F16) for k in range(4)]
        p_lo = [ph.sb(f"p_lo{k}", [P, GT], F16) for k in range(4)]
        o_low = ph.sb("o_low", [P, QT, hd])
        o_sum = ph.sb("o_sum", [P, QT, hd])
        rden = ph.sb("rden", [P, QT])
        st = [ph.ps(f"st{k}", [P, GT]) for k in range(2)]
        mx = [ph.ps(f"mx{k}", [P, 512]) for k in range(2)]
        o_ps = ph.ps("o_ps", [P, 2, 512])
        row_ps = ph.ps("row_ps", [P, GT])

        consts_in = ph.sem("consts_in")
        zeroed = ph.sem("zeroed")
        consts = ph.sem("consts")
        head_loaded = ph.sems("head_loaded", 2)
        st_ready = ph.sem("st_ready")
        exp_done = ph.sem("exp_done")
        low_dve = ph.sem("low_dve")
        low_pool = ph.sem("low_pool")
        mx_ready = ph.sem("mx_ready")
        mx_read = ph.sem("mx_read")
        dve_steps = ph.sem("dve_steps")
        cols_ready = ph.sem("cols_ready")
        rows_ready = ph.sem("rows_ready")
        q_ready = ph.sem("q_ready")
        block_done = ph.sem("block_done")
        block_out = ph.sem("block_out")
        head_stored = ph.sems("head_stored", 2)
        block = ph.block()
        LOADS = 8

        @block.sync
        def _(sp):
            def load(n, u):
                b, h = n // heads % B, n % heads
                toks = slice(b * S, (b + 1) * S)
                parts = [(q_hl[u][:, :], qk[0, h, :, :, toks].rearrange("s d n -> (s d) n")),
                         (q_hm[u][0:hd, :], qk[0, h, 0, :, toks]),
                         (k_hh[u][0:hd, :], qk[1, h, 0, :, toks]), (k_hh[u][hd:P, :], qk[1, h, 0, :, toks]),
                         (k_ll[u][0:hd, :], qk[1, h, 1, :, toks]), (k_ll[u][hd:P, :], qk[1, h, 1, :, toks]),
                         (k_lc[u][0:hd, :], qk[1, h, 1, :, toks]),
                         (vt[u][:, :, :], v[toks, h * vw:(h + 1) * vw].rearrange("(t p) f -> p t f", p=P))]
                assert len(parts) == LOADS
                for dst, src in parts:
                    sp.dma_start(dst, src).then_inc(head_loaded[u], 16)

            sp.dma_start(idf[:, :], ident).then_inc(consts_in, 16)
            for n in range(2):
                load(n, n)
            for n in range(HEADS):
                u = n % 2
                b, h = n // heads, n % heads
                sp.wait_ge(block_out, QB * (n + 1) + FREE)
                sp.dma_start(out[b * S:(b + 1) * S, h * hd:(h + 1) * hd].rearrange("(t p) f -> p t f", p=P),
                             o_head[u][:, :, :]).then_inc(head_stored[u], 16)
                if n + 2 <= HEADS:
                    load(n + 2, u)
            for u in range(2):
                sp.wait_ge(head_stored[u], 16 * (HEADS // 2) + FREE)

        @block.gpsimd
        def _(pool):
            pool.sem_inc(low_pool, FREE)
            with pool.Fori(0, HEADS // 2) as a:
                for u in range(2):
                    with pool.Fori(0, QB) as qb:
                        j = a * (2 * QB) + u * QB + qb
                        for kt in range(KT):
                            if by_pool(kt):
                                pool.wait_ge(exp_done, j * KT + kt + 3)
                                pool.tensor_tensor(p_lo[kt % 4][:, :], p32[kt % 2][:, :], p_hi[kt % 4][:, :],
                                                   ALU.subtract).then_inc(low_pool, 1)

        @block.tensor
        def _(pe):
            def max_unit(base, k, u, q0):
                tq, c = k // KC, k % KC
                if not (isinstance(base, int) and base + k < 2):
                    pe.wait_ge(mx_read, base + k - 1)
                lhs = q_hl[u][:, bass.ds(q0 + tq * P, P)]
                pe.matmul(mx[k % 2][:, :], lhs, k_hh[u][:, c * 512:(c + 1) * 512], start=True, stop=False)
                pe.matmul(mx[k % 2][:, :], lhs, k_ll[u][:, c * 512:(c + 1) * 512], start=False,
                          stop=True).then_inc(mx_ready, 1)

            def max_rows(mj):
                pe.wait_ge(cols_ready, mj + 1)
                for tq in range(QT):
                    last = pe.matmul(row_ps[:, tq * P:(tq + 1) * P], max_cols[:, tq, :], id16[:, :],
                                     start=(tq == 0), stop=(tq == QT - 1), skip_group_check=True)
                last.then_inc(rows_ready, 1)

            def values(j, kt, u):
                d, p = lows(kt)
                if by_pool(kt):
                    pe.wait_ge(low_pool, j * P_LOWS + p + FREE)
                else:
                    pe.wait_ge(low_dve, j * D_LOWS + d + FREE)
                if kt == 0:
                    pe.wait_ge(block_out, j + FREE)
                for tq in range(QT):
                    o = o_ps[:, tq // 2, (tq % 2) * vw:(tq % 2 + 1) * vw]
                    pe.matmul(o, p_hi[kt % 4][:, tq * P:(tq + 1) * P], vt[u][:, kt, :],
                              start=(kt == 0 and tq % 2 == 0), stop=(kt == KT - 1), skip_group_check=True)
                    last = pe.matmul(o[:, 0:hd + 1], p_lo[kt % 4][:, tq * P:(tq + 1) * P], vt[u][:, kt, 0:hd + 1],
                                     start=False, stop=(kt == KT - 1), skip_group_check=True)
                if kt == KT - 1:
                    last.then_inc(block_done, 1)

            def attend(j, u, qb, u_next, q_next):
                pe.wait_ge(q_ready, j + 1)
                for kt in range(KT + 2):
                    if kt < KT:
                        pe.wait_ge(exp_done, j * KT + kt + 1)
                        pe.matmul(st[kt % 2][:, :], k_hh[u][:, kt * P:(kt + 1) * P],
                                  q_hl[u][:, bass.ds(qb * GT, GT)], start=True, stop=False)
                        pe.matmul(st[kt % 2][:, :], k_lc[u][:, kt * P:(kt + 1) * P],
                                  q_hm[u][:, bass.ds(qb * GT, GT)], start=False, stop=True).then_inc(st_ready, 1)
                        for k in units_of(kt):
                            max_unit((j + 1) * UNITS, k, u_next, q_next)
                        if kt == ROW_STEP:
                            max_rows(j + 1)
                    if kt >= 2:
                        values(j, kt - 2, u)

            pe.wait_ge(consts, 5)
            pe.wait_ge(head_loaded[0], 16 * LOADS)
            for k in range(UNITS):
                max_unit(0, k, 0, 0)
            max_rows(0)
            with pe.Fori(0, HEADS // 2) as a:
                for u in range(2):
                    with pe.Fori(0, QB - 1) as qb:
                        attend(a * (2 * QB) + u * QB + qb, u, qb, u, (qb + 1) * GT)
                    pe.wait_ge(head_loaded[1 - u], 16 * LOADS * (a + 1 + u))
                    attend(a * (2 * QB) + u * QB + QB - 1, u, QB - 1, 1 - u, 0)

        @block.scalar
        def _(act):
            act.sem_inc(exp_done, 2)
            act.wait_ge(consts_in, 16)
            act.activation(id16[:, :], idf[:, :], ACT.Copy).then_inc(consts, 1)
            act.wait_ge(consts, 5)
            with act.Fori(0, HEADS // 2) as a:
                for u in range(2):
                    with act.Fori(0, QB) as qb:
                        j = a * (2 * QB) + u * QB + qb
                        for kt in range(KT):
                            before = (kt - 2) % KT
                            d, p = lows(before)
                            if by_pool(before):
                                act.wait_ge(low_pool, j * P_LOWS + (p if kt >= 2 else 0) + FREE)
                            else:
                                act.wait_ge(low_dve, j * D_LOWS + (d if kt >= 2 else 0) + FREE)
                            act.wait_ge(st_ready, j * KT + kt + 1)
                            act.activation(p32[kt % 2][:, :], st[kt % 2][:, :], ACT.Exp, bias=shift[:, :],
                                           scale=exp_scale)
                            act.activation(p_hi[kt % 4][:, :], st[kt % 2][:, :], ACT.Exp, bias=shift[:, :],
                                           scale=exp_scale).then_inc(exp_done, 1)

        @block.vector
        def _(dve):
            dve.sem_inc(low_dve, FREE)
            for u in range(2):
                dve.sem_inc(head_stored[u], FREE)
            dve.sem_inc(block_out, FREE)
            OWN = 4

            def reduce_unit(base, k):
                dve.wait_ge(mx_ready, base + k + 1)
                dve.tensor_reduce(part_max[:, k // KC, k % KC:k % KC + 1], mx[k % 2][:, :], AX.X,
                                  ALU.max).then_inc(mx_read, 1)

            def max_to_cols(mj, steps):
                dve.wait_ge(mx_read, (mj + 1) * UNITS)
                steps.link(dve.tensor_reduce(neg_max[:, :], part_max[:, :, :], AX.X, ALU.max, negate=True))
                steps.link(dve.tensor_scalar(max_cols[:, :, hd], neg_max[:, :], 1.0 / STAT, None, ALU.mult))
                dve.scalar_tensor_tensor(max_cols[:, :, hd + 1], neg_max[:, :], 1.0 / STAT, max_cols[:, :, hd],
                                         ALU.mult, ALU.subtract).then_inc(cols_ready, 1)

            def rows_to_q(mj, u, q0):
                dve.wait_ge(rows_ready, mj + 1)
                dve.tensor_copy(q_hm[u][hd:P, bass.ds(q0, GT)], row_ps[hd:P, :]).then_inc(q_ready, 1)

            def low(j, kt):
                if by_pool(kt):
                    return
                dve.wait_ge(exp_done, j * KT + kt + 3)
                dve.tensor_tensor(p_lo[kt % 4][:, :], p32[kt % 2][:, :], p_hi[kt % 4][:, :],
                                  ALU.subtract).then_inc(low_dve, 1)

            def attend(a, j, u, qb, u_next, q_next):
                steps = Chain(dve, dve_steps, 2 + OWN * j)
                for kt in range(KT + 1):
                    for k in units_of(kt):
                        reduce_unit((j + 1) * UNITS, k)
                    if kt >= 1:
                        low(j, kt - 1)
                    if kt == MM_STEP:
                        max_to_cols(j + 1, steps)
                    if kt == COPY_STEP:
                        rows_to_q(j + 1, u_next, q_next)
                dve.wait_ge(block_done, j + 1)
                sums = o_ps[:, :, 0:2 * vw].rearrange("p b (t f) -> p b t f", f=vw)
                four = lambda x: x[:, :, :].rearrange("p (b t) f -> p b t f", t=2)
                dve.tensor_copy(four(o_low), sums[:, :, :, hd + 1:vw])
                steps.link(dve.reciprocal(rden[:, :].rearrange("p (b t) -> p b t", t=2), sums[:, :, :, hd]))
                steps.link(dve.tensor_tensor(four(o_sum), sums[:, :, :, 0:hd], four(o_low), ALU.add))
                den = rden[:, :].rearrange("p (t o) -> p t o", o=1).broadcast_to([P, QT, hd])
                dve.wait_ge(head_stored[u], 16 * a + FREE)
                dve.tensor_tensor(o_head[u][:, bass.ds(qb * QT, QT), :], o_sum[:, :, :], den,
                                  ALU.mult).then_inc(block_out, 1)
                assert steps.n == OWN

            for u in range(2):
                dve.memset(k_lc[u][hd:P, :], 0.0).then_inc(zeroed, 1)
            dve.memset(max_cols[:, :, :], 0.0).then_inc(consts, 1)
            dve.memset(shift[:, :], math.log(PROB_SCALE)).then_inc(consts, 1)
            dve.wait_ge(zeroed, 2)
            for u in range(2):
                dve.memset(k_lc[u][hd:hd + 2, :], STAT).then_inc(consts, 1)
            dve.wait_ge(consts, 5)
            for k in range(UNITS):
                reduce_unit(0, k)
            max_to_cols(0, Chain(dve, dve_steps, 0))
            rows_to_q(0, 0, 0)
            with dve.Fori(0, HEADS // 2) as a:
                for u in range(2):
                    with dve.Fori(0, QB - 1) as qb:
                        attend(a, a * (2 * QB) + u * QB + qb, u, qb, u, (qb + 1) * GT)
                    attend(a, a * (2 * QB) + u * QB + QB - 1, u, QB - 1, 1 - u, 0)


PATCHES = (H // PR) * (W // PC)
MASKED = -1e30


def window(k):
    wr, wc = PR + k - 1, PC + k - 1
    rows = P // wc
    return wr, wc, rows, -(-wr // rows)


def patch_origin(t, k):
    half = k // 2
    r, c = PR * (t // (W // PC)), PC * (t % (W // PC))
    wr, wc, _, _ = window(k)
    return r, c, min(max(r - half, 0), H - wr), min(max(c - half, 0), W - wc)


def neighbour_masks(k):
    wr, wc, _, _ = window(k)
    out = np.full((3, 3, PR, PC, wr, wc), MASKED, np.float32)
    for vr, tr in enumerate((0, 1, H // PR - 1)):
        for vc, tc in enumerate((0, 1, W // PC - 1)):
            r0, c0, kr0, kc0 = patch_origin(tr * (W // PC) + tc, k)
            for r in range(PR):
                a = min(max(r0 + r - k // 2, 0), H - k) - kr0
                for c in range(PC):
                    b = min(max(c0 + c - k // 2, 0), W - k) - kc0
                    out[vr, vc, r, c, a:a + k, b:b + k] = 0.0
    return (out.reshape(9, P, wr * wc).view(np.uint32) >> 16).astype(np.uint16)


def local_attention_phase(nc, name, qk, v, ident, masks, out, heads, k, scale):
    S = H * W
    hd = C // heads
    vw = 2 * hd + 1
    assert 4 * hd == P
    wr, wc, cr, NC = window(k)
    keys, ck = wr * wc, cr * wc
    HG = 4
    NHG = heads // HG
    UN = PATCHES // 2
    N = 2 * UN
    exp_scale = scale / OPERAND_SCALE ** 2

    def rows_of(ch):
        return min(cr, wr - cr * ch)

    with Phase(nc, name) as ph:
        idt = ph.sb("ident", [P, P])
        idb = ph.sb("identb", [P, P], BF16)
        mask = ph.sb("mask", [P, 9, keys], BF16)
        q4 = [ph.sb(f"q{u}", [P, S], F16) for u in range(2)]
        k4 = [ph.sb(f"k{u}", [P, H, W], F16) for u in range(2)]
        vwin = [ph.sb(f"v{x}", [P, PATCHES * NC, HG * vw], F16) for x in range(NHG)]
        o_head = [ph.sb(f"o{u}", [P, PATCHES, hd]) for u in range(2)]
        neg_max = ph.sb("neg_max", [P, 2, 2])
        bias = ph.sb("bias", [P, 2, 2])
        p32 = [ph.sb(f"p{x}", [P, 2, NC * ck]) for x in range(2)]
        p_hi = [ph.sb(f"ph{x}", [P, 2, NC * P], F16) for x in range(2)]
        p_lo = [ph.sb(f"pl{x}", [P, 2, NC * P], F16) for x in range(2)]
        o_low = ph.sb("o_low", [P, 4, hd])
        o_sum = ph.sb("o_sum", [P, 4, hd])
        rden = ph.sb("rden", [P, 4])
        sc = [ph.ps(f"sc{x}", [P, 2, 512]) for x in range(2)]
        pt = ph.ps("pt", [P, 2, 512])
        ov = [ph.ps(f"ov{x}", [P, 512]) for x in range(2)]

        consts_in = ph.sem("consts_in")
        consts = ph.sem("consts")
        head_loaded = ph.sems("head_loaded", 2)
        v_loaded = ph.sems("v_loaded", NHG)
        sc_ready = ph.sem("sc_ready")
        max_ready = ph.sem("max_ready")
        bias_ready = ph.sem("bias_ready")
        exp_done = ph.sem("exp_done")
        pt_ready = ph.sem("pt_ready")
        hi_ready = ph.sem("hi_ready")
        lo_ready = ph.sem("lo_ready")
        pv_done = ph.sem("pv_done")
        norm_steps = ph.sem("norm_steps")
        out_ready = ph.sem("out_ready")
        head_stored = ph.sems("head_stored", 2)
        block = ph.block()
        BODIES = B * heads // 2
        PAIRS = HG // 2

        @block.sync
        def _(sp):
            def load_head(n, u):
                b, h = n // heads, n % heads
                toks = slice(b * S, (b + 1) * S)
                flat = lambda x: x[:, :, :].rearrange("p r c -> p (r c)")
                for x in range(2):
                    sp.dma_start(q4[u][2 * hd * x:2 * hd * (x + 1), :],
                                 qk[0, h, :, :, toks].rearrange("s d n -> (s d) n")).then_inc(head_loaded[u], 16)
                for x in range(4):
                    sp.dma_start(flat(k4[u])[hd * x:hd * (x + 1), :],
                                 qk[1, h, x // 2, :, toks]).then_inc(head_loaded[u], 16)

            def load_v(b, x):
                img = v[b * S:(b + 1) * S, x * HG * vw:(x + 1) * HG * vw].rearrange("(r c) f -> r c f", c=W)
                for t in range(PATCHES):
                    _, _, r0, c0 = patch_origin(t, k)
                    for ch in range(NC):
                        n = rows_of(ch)
                        a = r0 + cr * ch
                        sp.dma_start(vwin[x][0:n * wc, t * NC + ch, :],
                                     img[a:a + n, c0:c0 + wc, :]).then_inc(v_loaded[x], 16)

            sp.dma_start(idt[:, :], ident).then_inc(consts_in, 16)
            sp.dma_start(mask[:, :, :], masks.rearrange("v p n -> p v n").bitcast(BF16)).then_inc(consts_in, 16)
            for u in range(2):
                load_head(u, u)
            sp.wait_ge(consts, 5)
            for x in range(NHG):
                load_v(0, x)
            for n in range(B * heads):
                u = n % 2
                sp.wait_ge(out_ready, (n + 1) * UN // 2 + FREE)
                sp.dma_start(out[n // heads, :, :, n % heads * hd:(n % heads + 1) * hd].rearrange("t p f -> p t f"),
                             o_head[u][:, :, :]).then_inc(head_stored[u], 16)
                if n + 2 < B * heads:
                    load_head(n + 2, u)
                if (n + 1) % HG == 0 and n + 1 + heads - HG < B * heads:
                    load_v(n // heads + 1, n % heads // HG)
            for u in range(2):
                sp.wait_ge(head_stored[u], 16 * (B * heads // 2) + FREE)

        def bodies(eng):
            with eng.Fori(0, B) as b:
                for x in range(NHG):
                    with eng.Fori(0, PAIRS) as a:
                        yield b * (NHG * PAIRS) + x * PAIRS + a, b, x, a

        def place(n):
            return n // UN, n % UN

        @block.tensor
        def _(pe):
            pe.wait_ge(consts_in, 32)
            pe.wait_ge(consts, 5)

            def scores(pair, n):
                u, un = place(n)
                if un == 0:
                    pe.wait_ge(head_loaded[u], 96 * (pair + 1))
                pe.wait_ge(exp_done, pair * N + n + 1)
                for j in range(2):
                    t = 2 * un + j
                    r, c, kr, kc = patch_origin(t, k)
                    vr = 0 if r == 0 else 2 if r == H - PR else 1
                    vc = 0 if c == 0 else 2 if c == W - PC else 1
                    dst = sc[n % 2][:, j, 0:keys]
                    pe.matmul(dst, q4[u][:, t * P:(t + 1) * P], k4[u][:, kr:kr + wr, kc:kc + wc],
                              start=True, stop=False)
                    last = pe.matmul(dst, idb[:, :], mask[:, 3 * vr + vc, :], start=False, stop=True)
                last.then_inc(sc_ready, 1)

            def turn(pair, n):
                pe.wait_ge(exp_done, pair * N + n + 3)
                pe.wait_ge(lo_ready, pair * N + n + FREE)
                for j in range(2):
                    for ch in range(NC):
                        last = pe.transpose(pt[0:ck, j, ch * P:(ch + 1) * P], p32[n % 2][:, j, ch * ck:(ch + 1) * ck],
                                            idt[:, :])
                last.then_inc(pt_ready, 1)

            def values(pair, n, x, a):
                u, un = place(n)
                pe.wait_ge(lo_ready, pair * N + n + 1 + FREE)
                quad = n // 2
                if n % 2 == 0 and quad >= 2:
                    pe.wait_ge(out_ready, pair * (N // 2) + quad - 1 + FREE)
                elif n % 2 == 0:
                    pe.wait_ge(out_ready, pair * (N // 2) + FREE)
                for j in range(2):
                    t = 2 * un + j
                    o = ov[quad % 2][:, (2 * (n % 2) + j) * vw:(2 * (n % 2) + j + 1) * vw]
                    for ch in range(NC):
                        vv = vwin[x][0:ck, t * NC + ch, bass.ds(a * (2 * vw) + u * vw, vw)]
                        first = n % 2 == 0 and j == 0 and ch == 0
                        pe.matmul(o, p_hi[n % 2][0:ck, j, ch * P:(ch + 1) * P], vv,
                                  start=first, stop=(ch == NC - 1), skip_group_check=True)
                        vv = vwin[x][0:ck, t * NC + ch, bass.ds(a * (2 * vw) + u * vw, hd + 1)]
                        last = pe.matmul(o[:, 0:hd + 1], p_lo[n % 2][0:ck, j, ch * P:(ch + 1) * P], vv,
                                         start=False, stop=(ch == NC - 1), skip_group_check=True)
                last.then_inc(pv_done, 1)

            for pair, b, x, a in bodies(pe):
                pe.wait_ge(v_loaded[x], 16 * PATCHES * NC * (b + 1))
                for n in range(-2, N + 1):
                    if 0 <= n < N:
                        turn(pair, n)
                    if n + 2 < N:
                        scores(pair, n + 2)
                    if n >= 1:
                        values(pair, n - 1, x, a)

        @block.scalar
        def _(act):
            act.sem_inc(exp_done, 2)
            act.wait_ge(consts_in, 32)
            act.activation(idb[:, :], idt[:, :], ACT.Copy).then_inc(consts, 1)
            for pair, b, x, a in bodies(act):
                for n in range(N + 1):
                    if n < N:
                        act.wait_ge(bias_ready, pair * N + n + 1)
                        for j in range(2):
                            last = act.activation(p32[n % 2][:, j, 0:keys], sc[n % 2][:, j, 0:keys], ACT.Exp,
                                                  bias=bias[:, n % 2, j:j + 1], scale=exp_scale)
                        last.then_inc(exp_done, 1)
                    if n >= 1:
                        m = n - 1
                        act.wait_ge(pt_ready, pair * N + m + 1)
                        act.activation(p_hi[m % 2][0:ck, :, :], pt[0:ck, :, 0:NC * P], ACT.Copy).then_inc(hi_ready, 1)

        @block.vector
        def _(dve):
            dve.sem_inc(lo_ready, FREE)
            dve.sem_inc(out_ready, FREE)
            for u in range(2):
                dve.sem_inc(head_stored[u], FREE)
            for x in range(2):
                dve.memset(p32[x][:, :, :], 0.0).then_inc(consts, 1)
            for x in range(NHG):
                dve.memset(vwin[x][:, :, :], 0.0).then_inc(consts, 1)
            dve.wait_ge(consts, 5)

            def maxima(pair, n):
                dve.wait_ge(sc_ready, pair * N + n + 1)
                dve.tensor_reduce(neg_max[:, n % 2, :], sc[n % 2][:, :, 0:keys], AX.X, ALU.max,
                                  negate=True).then_inc(max_ready, 1)
                dve.wait_ge(max_ready, pair * N + n + 1)
                dve.tensor_scalar(bias[:, n % 2, :], neg_max[:, n % 2, :], exp_scale, math.log(PROB_SCALE),
                                  ALU.mult, ALU.add).then_inc(bias_ready, 1)

            def low(pair, n):
                dve.wait_ge(hi_ready, pair * N + n + 1)
                dve.tensor_tensor(p_lo[n % 2][0:ck, :, :], pt[0:ck, :, 0:NC * P], p_hi[n % 2][0:ck, :, :],
                                  ALU.subtract).then_inc(lo_ready, 1)

            def normalise(pair, n):
                u, un = place(n)
                quad = n // 2
                steps = Chain(dve, norm_steps, (pair * (N // 2) + quad) * 3)
                dve.wait_ge(pv_done, pair * N + n + 1)
                sums = ov[quad % 2][:, 0:4 * vw].rearrange("p (t f) -> p t f", f=vw)
                steps.step(dve.tensor_copy(o_low[:, :, :], sums[:, :, hd + 1:vw]))
                steps.link(dve.reciprocal(rden[:, :], sums[:, :, hd]))
                steps.link(dve.tensor_tensor(o_sum[:, :, :], sums[:, :, 0:hd], o_low[:, :, :], ALU.add))
                den = rden[:, :].rearrange("p (t o) -> p t o", o=1).broadcast_to([P, 4, hd])
                dve.tensor_tensor(o_head[u][:, 2 * un - 2:2 * un + 2, :], o_sum[:, :, :], den,
                                  ALU.mult).then_inc(out_ready, 1)

            for pair, b, x, a in bodies(dve):
                for u in range(2):
                    dve.wait_ge(head_stored[u], 16 * pair + FREE)
                for n in range(N + 3):
                    if n < N:
                        maxima(pair, n)
                    if 2 <= n < N + 2:
                        low(pair, n - 2)
                    if n >= 4 and n % 2 == 0:
                        normalise(pair, n - 3)


def tail_phase(nc, name, kind, att, x, ident, w_proj, b_proj, out, patches,
               gamma=None, beta=None, w1=None, b1=None, w2=None, b2=None):
    mlp = kind != "none"
    FT = w1.shape[1] // P if mlp else 0
    with Phase(nc, name) as ph:
        idt = ph.sb("ident", [P, P])
        wp = ph.sb("wp", [P, CH, C])
        bp = ph.sb("bp", [P, C])
        a_in = [ph.sb(f"a{u}", [P, TPG, C]) for u in range(2)]
        x_in = [ph.sb(f"x{u}", [P, TPG, C]) for u in range(2)]
        res = ph.sb("res", [P, TPG, C])
        y = [ph.sb(f"y{u}", [P, TPG, C]) for u in range(2)]
        aT = ph.sb("aT", [P, CH, GT])
        xn = ph.sb("xn", [P, TPG, C])
        aux = ph.sb("aux", [P, TPG, C])
        root = ph.sb("root", [P, TPG, C])
        res2 = ph.sb("res2", [P, TPG, C])
        stats = ph.sb("stats", [P, TPG, 6])
        mv = ph.sb("mv", [P, TPG, 2])
        std = ph.sb("std", [P, TPG])
        rstd = ph.sb("rstd", [P, TPG])
        eps = ph.sb("eps", [P, 1])
        tp = [ph.ps(f"tp{c}", [P, GT]) for c in range(CH)]
        op = [ph.ps(f"op{c}", [P, 512]) for c in range(2)]
        fp = [ph.ps(f"fp{c}", [P, 512]) for c in range(2)]
        if mlp:
            gcol, bcol = ph.sb("gamma", [P, CH]), ph.sb("beta", [P, CH])
            w1s, b1s = ph.sb("w1", [P, CH, FT * P]), ph.sb("b1", [P, FT])
            w2s, b2s = ph.sb("w2", [P, FT, C]), ph.sb("b2", [P, C])
            xT = ph.sb("xT", [P, CH, GT])
            hT = ph.sb("hT", [P, FT, GT])

        weights_in = ph.sem("weights_in")
        consts = ph.sem("consts")
        loaded = ph.sems("loaded", 2)
        a_turned = ph.sem("a_turned")
        at_ready = ph.sem("at_ready")
        proj_ready = ph.sem("proj_ready")
        res_ready = ph.sem("res_ready")
        y_ready = ph.sem("y_ready")
        dve_steps = ph.sem("dve_steps")
        act_steps = ph.sem("act_steps")
        marker = ph.sem("marker")
        var_ready = ph.sem("var_ready")
        std_ready = ph.sem("std_ready")
        root_ready = ph.sem("root_ready")
        sum_ready = ph.sem("sum_ready")
        log_ready = ph.sem("log_ready")
        xn_ready = ph.sem("xn_ready")
        x_turned = ph.sem("x_turned")
        xt_ready = ph.sem("xt_ready")
        fc1_ready = ph.sem("fc1_ready")
        h_ready = ph.sem("h_ready")
        fc2_ready = ph.sem("fc2_ready")
        res2_ready = ph.sem("res2_ready")
        out_ready = ph.sem("out_ready")
        stored = ph.sems("stored", 2)
        block = ph.block()

        loads = [(idt[:, :], ident), (wp[:, :, :], w_proj.rearrange("(c p) n -> p c n", p=P)), (bp[:, :], row(b_proj))]
        if mlp:
            loads += [(gcol[:, :], gamma), (bcol[:, :], beta), (w1s[:, :, :], w1.rearrange("(c p) n -> p c n", p=P)),
                      (b1s[:, :], b1), (w2s[:, :, :], w2.rearrange("(c p) n -> p c n", p=P)), (b2s[:, :], row(b2))]
        n_x = TPG if patches else 1

        def token_parts(dram, g, tile):
            if not patches:
                return [(dram[bass.ds(g * GT, GT)].rearrange("(t p) c -> p t c", p=P), tile[:, :, :])]
            band = dram.rearrange("(g r t c) f -> g r t c f", r=PR, t=TPG, c=PC)[bass.ds(g, 1)]
            return [(band[:, :, t, :, :].rearrange("g r c f -> (g r) c f"), tile[:, t, :]) for t in range(TPG)]

        @block.sync
        def _(sp):
            def load(g, u):
                if patches:
                    src = att.rearrange("b t p f -> (b t) p f")[bass.ds(g * TPG, TPG)].rearrange("t p f -> p t f")
                else:
                    src = att[bass.ds(g * GT, GT)].rearrange("(t p) c -> p t c", p=P)
                sp.dma_start(a_in[u][:, :, :], src).then_inc(loaded[u], 16)
                for dram, tile in token_parts(x, g, x_in[u]):
                    sp.dma_start(tile, dram).then_inc(loaded[u], 16)

            def store(g, u):
                sp.wait_ge(out_ready, g + 1 + FREE)
                for dram, tile in token_parts(out, g, y[u]):
                    sp.dma_start(dram, tile).then_inc(stored[u], 16)

            for u in range(2):
                load(u, u)
            for dst, src in loads:
                sp.dma_start(dst, src).then_inc(weights_in, 16)
            with sp.Fori(0, GROUPS // 2 - 1) as i:
                for u in range(2):
                    g = 2 * i + u
                    sp.wait_ge(a_turned, CH * (g + 1))
                    sp.wait_ge(res_ready, g + 1)
                    load(g + 2, u)
                    store(g, u)
            for u in range(2):
                store(GROUPS - 2 + u, u)
            for u in range(2):
                sp.wait_ge(stored[u], 16 * n_x * (GROUPS // 2) + FREE)

        def groups(eng):
            with eng.Fori(0, GROUPS // 2) as i:
                for u in range(2):
                    yield i, u, 2 * i + u

        @block.gpsimd
        def _(pool):
            pool.wait_ge(weights_in, 16 * len(loads))
            pool.memset(eps[:, :], LN_EPS).then_inc(consts, 1)
            for i, u, g in groups(pool):
                pool.wait_ge(loaded[u], 16 * (1 + n_x) * (i + 1))
                pool.wait_ge(y_ready, g + FREE)
                pool.tensor_tensor(res[:, :, :], x_in[u][:, :, :],
                                   bp[:, :].rearrange("p (o c) -> p o c", o=1).broadcast_to([P, TPG, C]),
                                   ALU.add).then_inc(res_ready, 1)
                if mlp:
                    pool.wait_ge(y_ready, g + 1 + FREE)
                    pool.wait_ge(out_ready, g + FREE)
                    pool.tensor_tensor(res2[:, :, :], y[u][:, :, :],
                                       b2s[:, :].rearrange("p (o c) -> p o c", o=1).broadcast_to([P, TPG, C]),
                                       ALU.add).then_inc(res2_ready, 1)

        @block.tensor
        def _(pe):
            pe.wait_ge(weights_in, 16 * len(loads))

            def turn(src, done):
                for c in range(CH):
                    for t in range(TPG):
                        last = pe.transpose(tp[c][:, t * P:(t + 1) * P], src[:, t, c * P:(c + 1) * P], idt[:, :])
                    last.then_inc(done, 1)

            def token_major(lhs, w, tiles, done):
                for half in range(2):
                    for t in range(2):
                        tt = 2 * half + t
                        for c in range(tiles):
                            last = pe.matmul(op[half][:, t * C:(t + 1) * C], lhs[:, c, tt * P:(tt + 1) * P],
                                             w[:, c, :], start=(c == 0), stop=(c == tiles - 1))
                    last.then_inc(done, 1)

            for i, u, g in groups(pe):
                pe.wait_ge(loaded[u], 16 * (1 + n_x) * (i + 1))
                pe.wait_ge(xt_ready if mlp else at_ready, CH * g + FREE)
                turn(a_in[u], a_turned)
                pe.wait_ge(at_ready, CH * (g + 1) + (0 if mlp else FREE))
                pe.wait_ge(out_ready, g + FREE)
                token_major(aT, wp, CH, proj_ready)
                if not mlp:
                    continue
                pe.wait_ge(xn_ready, g + 1)
                turn(xn, x_turned)
                pe.wait_ge(xt_ready, CH * (g + 1) + FREE)
                for m in range(FT):
                    if m >= 2:
                        pe.wait_ge(h_ready, FT * g + m - 1)
                    for c in range(CH):
                        last = pe.matmul(fp[m % 2][:, :], w1s[:, c, m * P:(m + 1) * P], xT[:, c, :],
                                         start=(c == 0), stop=(c == CH - 1))
                    last.then_inc(fc1_ready, 1)
                pe.wait_ge(h_ready, FT * (g + 1))
                token_major(hT, w2s, FT, fc2_ready)

        @block.scalar
        def _(act):
            act.sem_inc(xt_ready if mlp else at_ready, FREE)
            act.wait_ge(weights_in, 16 * len(loads))
            act.wait_ge(consts, 1)
            for i, u, g in groups(act):
                for c in range(CH):
                    act.wait_ge(a_turned, CH * g + c + 1)
                    act.activation(aT[:, c, :], tp[c][:, :], ACT.Copy).then_inc(at_ready, 1)
                if not mlp:
                    continue
                if kind == "layer":
                    act.wait_ge(var_ready, g + 1)
                    act.activation(std[:, :], mv[:, :, 1], ACT.Sqrt, bias=eps[:, :]).then_inc(std_ready, 1)
                else:
                    steps = Chain(act, act_steps, 2 * g)
                    act.wait_ge(y_ready, g + 1 + FREE)
                    steps.link(act.activation(root[:, :, :], y[u][:, :, :], ACT.Square))
                    act.activation(root[:, :, :], root[:, :, :], ACT.Sqrt, bias=1.0).then_inc(root_ready, 1)
                    act.wait_ge(sum_ready, g + 1)
                    steps.link(act.activation(aux[:, :, :], aux[:, :, :], ACT.Ln))
                    act.activation(root[:, :, :], y[u][:, :, :], ACT.Sign).then_inc(log_ready, 1)
                for c in range(CH):
                    act.wait_ge(x_turned, CH * g + c + 1)
                    act.activation(xT[:, c, :], tp[c][:, :], ACT.Identity, bias=bcol[:, c:c + 1],
                                   scale=gcol[:, c:c + 1]).then_inc(xt_ready, 1)
                for m in range(FT):
                    act.wait_ge(fc1_ready, FT * g + m + 1)
                    act.activation(hT[:, m, :], fp[m % 2][:, :], ACT.Gelu, bias=b1s[:, m:m + 1]).then_inc(h_ready, 1)

        @block.vector
        def _(dve):
            dve.sem_inc(y_ready, FREE)
            dve.sem_inc(out_ready, FREE)
            for u in range(2):
                dve.sem_inc(stored[u], FREE)
            own = {"layer": 2, "arsinh": 1, "none": 0}[kind]
            flat = lambda x, half: x[:, 2 * half:2 * half + 2, :].rearrange("p t c -> p (t c)")
            for i, u, g in groups(dve):
                steps = Chain(dve, dve_steps, own * g)
                dve.wait_ge(stored[u], 16 * n_x * i + FREE)
                dve.wait_ge(res_ready, g + 1)
                for half in range(2):
                    dve.wait_ge(proj_ready, 2 * g + half + 1)
                    last = dve.tensor_tensor(flat(y[u], half), op[half][:, :], flat(res, half), ALU.add)
                last.then_inc(y_ready, 1)
                dve.wait_ge(y_ready, g + 1 + FREE)
                if not mlp:
                    dve.sem_inc(out_ready, 1)
                    continue
                if kind == "layer":
                    for t in range(TPG):
                        last = dve.bn_stats(stats[:, t, :], y[u][:, t, :])
                    steps.link(last)
                    passed(dve, marker)
                    for t in range(TPG):
                        last = dve.bn_aggr(mv[:, t, :], stats[:, t, :])
                    last.then_inc(var_ready, 1)
                    dve.wait_ge(var_ready, g + 1)
                    dve.wait_ge(std_ready, g + 1)
                    steps.link(dve.reciprocal(rstd[:, :], std[:, :]))
                    for t in range(TPG):
                        last = dve.tensor_scalar(xn[:, t, :], y[u][:, t, :], mv[:, t, 0:1], rstd[:, t:t + 1],
                                                 ALU.subtract, ALU.mult)
                else:
                    steps.link(dve.scalar_tensor_tensor(aux[:, :, :], y[u][:, :, :], -1.0, y[u][:, :, :],
                                                        ALU.mult, ALU.max))
                    dve.wait_ge(root_ready, g + 1)
                    dve.tensor_tensor(aux[:, :, :], aux[:, :, :], root[:, :, :], ALU.add).then_inc(sum_ready, 1)
                    dve.wait_ge(log_ready, g + 1)
                    last = dve.tensor_tensor(xn[:, :, :], aux[:, :, :], root[:, :, :], ALU.mult)
                last.then_inc(xn_ready, 1)
                dve.wait_ge(res2_ready, g + 1)
                for half in range(2):
                    dve.wait_ge(fc2_ready, 2 * g + half + 1)
                    last = dve.tensor_tensor(flat(y[u], half), op[half][:, :], flat(res2, half), ALU.add)
                last.then_inc(out_ready, 1)
                assert steps.n == own


GN_GROUPS = 8


def group_stats_phase(nc, name, x, ident, ones_blocks, scale, bias, affine):
    PER = GROUPS // B
    with Phase(nc, name) as ph:
        idt = ph.sb("ident", [P, P])
        ones = ph.sb("ones", [P, P])
        sc = ph.sb("scale", [P, CH])
        bi = ph.sb("bias", [P, CH])
        x_in = [ph.sb(f"x{u}", [P, TPG, C]) for u in range(2)]
        stats = ph.sb("stats", [P, B, CH, PER, 6])
        mv = ph.sb("mv", [P, B, CH, 2])
        mean = ph.sb("mean", [P, B, CH])
        dev = ph.sb("dev", [P, B, CH])
        var = ph.sb("var", [P, B, CH])
        eps = ph.sb("eps", [P, 1])
        ab = ph.sb("ab", [P, B, CH, 2])
        tmp = ph.sb("tmp", [P, B, CH])
        tp = [ph.ps(f"tp{c}", [P, GT]) for c in range(2 * CH)]
        sums = ph.ps("sums", [P, 512])

        consts_in = ph.sem("consts_in")
        consts = ph.sem("consts")
        loaded = ph.sems("loaded", 2)
        turned = ph.sem("turned")
        counted = ph.sem("counted")
        steps_done = ph.sem("steps_done")
        to_sum = ph.sem("to_sum")
        summed = ph.sem("summed")
        std_ready = ph.sem("std_ready")
        ab_ready = ph.sem("ab_ready")
        stored = ph.sem("stored")
        block = ph.block()

        @block.sync
        def _(sp):
            for dst, src in ((idt[:, :], ident), (ones[:, :], ones_blocks), (sc[:, :], scale), (bi[:, :], bias)):
                sp.dma_start(dst, src).then_inc(consts_in, 16)
            for g in range(GROUPS):
                u = g % 2
                if g >= 2:
                    sp.wait_ge(turned, CH * (g - 1))
                sp.dma_start(x_in[u][:, :, :], x[g * GT:(g + 1) * GT].rearrange("(t p) c -> p t c", p=P)).then_inc(loaded[u], 16)
            sp.wait_ge(ab_ready, 1)
            with nc.allow_non_contiguous_dma(reason="512 values a token group"):
                for g in range(GROUPS):
                    for k in range(2):
                        for c in range(CH):
                            sp.dma_start(affine[g, k, c * P:(c + 1) * P].rearrange("(p o) -> p o", o=1),
                                         ab[:, g // PER, c, k:k + 1]).then_inc(stored, 16)
            sp.wait_ge(stored, 16 * 2 * CH * GROUPS)

        @block.gpsimd
        def _(pool):
            pool.memset(eps[:, :], LN_EPS).then_inc(consts, 1)

        @block.tensor
        def _(pe):
            pe.wait_ge(consts_in, 64)
            for g in range(GROUPS):
                u = g % 2
                pe.wait_ge(loaded[u], 16 * (g // 2 + 1))
                if g >= 2:
                    pe.wait_ge(counted, CH * (g - 1))
                for c in range(CH):
                    for t in range(TPG):
                        last = pe.transpose(tp[CH * u + c][:, t * P:(t + 1) * P], x_in[u][:, t, c * P:(c + 1) * P], idt[:, :])
                    last.then_inc(turned, 1)
            n = B * CH
            flat = lambda v: v[:, :, :].rearrange("p b c -> p (b c)")
            for k, src in enumerate((mean, dev)):
                pe.wait_ge(to_sum, k + 1)
                pe.matmul(sums[:, k * n:(k + 1) * n], ones[:, :], flat(src), start=True, stop=True).then_inc(summed, 1)

        @block.scalar
        def _(act):
            act.wait_ge(consts, 1)
            act.wait_ge(to_sum, 3)
            act.activation(var[:, :, :], var[:, :, :], ACT.Sqrt, bias=eps[:, :]).then_inc(std_ready, 1)

        @block.vector
        def _(dve):
            steps = Chain(dve, steps_done)
            dve.wait_ge(consts_in, 64)
            for g in range(GROUPS):
                for c in range(CH):
                    dve.wait_ge(turned, CH * g + c + 1)
                    dve.bn_stats(stats[:, g // PER, c, g % PER, :], tp[CH * (g % 2) + c][:, :]).then_inc(counted, 1)
            dve.wait_ge(counted, CH * GROUPS)
            for b in range(B):
                for c in range(CH):
                    steps.step(dve.bn_aggr(mv[:, b, c, :], stats[:, b, c, :, :]))
            steps.settle()
            n = B * CH
            shaped = lambda k: sums[:, k * n:(k + 1) * n].rearrange("p (b c) -> p b c", b=B)
            dve.tensor_copy(mean[:, :, :], mv[:, :, :, 0]).then_inc(to_sum, 1)
            dve.wait_ge(summed, 1)
            steps.link(dve.tensor_copy(mean[:, :, :], shaped(0)))
            steps.link(dve.tensor_tensor(dev[:, :, :], mv[:, :, :, 0], mean[:, :, :], ALU.subtract))
            steps.link(dve.tensor_tensor(dev[:, :, :], dev[:, :, :], dev[:, :, :], ALU.mult))
            dve.tensor_tensor(dev[:, :, :], dev[:, :, :], mv[:, :, :, 1], ALU.add).then_inc(to_sum, 1)
            dve.wait_ge(summed, 2)
            dve.tensor_copy(var[:, :, :], shaped(1)).then_inc(to_sum, 1)
            dve.wait_ge(std_ready, 1)
            steps.link(dve.reciprocal(tmp[:, :, :], var[:, :, :]))
            scales = sc[:, :].rearrange("p (o c) -> p o c", o=1).broadcast_to([P, B, CH])
            biases = bi[:, :].rearrange("p (o c) -> p o c", o=1).broadcast_to([P, B, CH])
            steps.link(dve.tensor_tensor(ab[:, :, :, 0], tmp[:, :, :], scales, ALU.mult))
            steps.link(dve.tensor_tensor(tmp[:, :, :], mean[:, :, :], ab[:, :, :, 0], ALU.mult))
            dve.tensor_tensor(ab[:, :, :, 1], biases, tmp[:, :, :], ALU.subtract).then_inc(ab_ready, 1)


NF = 33
U0 = H - NF
SHRINK = 0.01
FEW = 4


def fourier_matrices():
    n = np.arange(64)
    v = np.arange(NF)
    phase = 2 * np.pi * np.outer(n, v) / W
    fwd = np.concatenate([np.cos(phase), -np.sin(phase[:, 1:NF - 1])], 1) / 8
    twice = np.where((v == 0) | (v == NF - 1), 1.0, 2.0)
    inv = np.concatenate([twice * np.cos(phase), -(twice * np.sin(phase))[:, 1:NF - 1]], 1).T / 8
    both = lambda m: np.kron(np.eye(B), m).astype(np.float32)
    ph = 2 * np.pi * np.outer(n, U0 + v) / H
    c, s = np.cos(ph) / 8, np.sin(ph) / 8
    fwd_h = np.block([[c, -s], [s, c]]).astype(np.float32)
    inv_h = np.block([[c.T, s.T], [-s.T, c.T]]).astype(np.float32)
    return both(fwd), both(inv), fwd_h, inv_h


def block_diagonal(w1, w2):
    n = P // 32
    out = np.zeros((2, 2, CH, n, 32, n, 32), np.float32)
    for layer, w in enumerate((w1, w2)):
        blocks = np.asarray(w).reshape(2, CH, n, 32, 32)
        for k in range(n):
            out[layer, :, :, k, :, k, :] = blocks[:, :, k]
    return out.reshape(2, 2, CH, P, P)


def mix_biases(b1, b2):
    cols = [np.asarray(b).reshape(2, CH, P).transpose(2, 0, 1).reshape(P, 2 * CH) for b in (b1, b2)]
    return np.stack(cols)


def w_transform_phase(nc, name, x, matrix, out, residual=None):
    inverse = residual is not None
    STEPS = H // FEW
    with Phase(nc, name) as ph:
        m = ph.sb("m", [P, P])
        x_in = [ph.sb(f"x{u}", [P, FEW, C]) for u in range(2)]
        r_in = [ph.sb(f"r{u}", [P, FEW, C]) for u in range(2)]
        y = [ph.sb(f"y{u}", [P, FEW, C]) for u in range(2)]
        pr = [ph.ps(f"p{k}", [P, 512]) for k in range(4)]
        m_loaded = ph.sem("m_loaded")
        loaded = ph.sems("loaded", 2)
        done = ph.sem("done")
        copied = ph.sem("copied")
        stored = ph.sems("stored", 2)
        block = ph.block()
        per = 16 * (1 + B if inverse else B)
        n_out = B if inverse else 1

        def lines(ap, i, u, b):
            return ap.rearrange("b (s n) w c -> b s w n c", n=FEW)[b:b + 1, bass.ds(2 * i + u, 1)].rearrange("b s w n c -> (b s w) n c")

        def packed(ap, i, u):
            return ap.rearrange("b k (s n) c -> (b k) s n c", n=FEW)[:, bass.ds(2 * i + u, 1)].rearrange("p s n c -> p (s n) c")

        @block.sync
        def _(sp):
            def load(i, u):
                if inverse:
                    sp.dma_start(x_in[u][:, :, :], packed(x, i, u)).then_inc(loaded[u], 16)
                for b in range(B):
                    dst = (r_in if inverse else x_in)[u][b * W:(b + 1) * W, :, :]
                    sp.dma_start(dst, lines(residual if inverse else x, i, u, b)).then_inc(loaded[u], 16)

            def store(i, u):
                sp.wait_ge(copied, 2 * (2 * i + u) + 2)
                if inverse:
                    for b in range(B):
                        sp.dma_start(lines(out, i, u, b), y[u][b * W:(b + 1) * W, :, :]).then_inc(stored[u], 16)
                else:
                    sp.dma_start(packed(out, i, u), y[u][:, :, :]).then_inc(stored[u], 16)

            sp.dma_start(m[:, :], matrix).then_inc(m_loaded, 16)
            for u in range(2):
                load(0, u)
            with sp.Fori(0, STEPS // 2 - 1) as i:
                for u in range(2):
                    store(i, u)
                    load(i + 1, u)
            for u in range(2):
                store(STEPS // 2 - 1, u)
            for u in range(2):
                sp.wait_ge(stored[u], 16 * n_out * (STEPS // 2) + FREE)

        @block.tensor
        def _(pe):
            pe.wait_ge(m_loaded, 16)
            with pe.Fori(0, STEPS // 2) as i:
                for u in range(2):
                    pe.wait_ge(loaded[u], per * (i + 1))
                    for k in range(2):
                        pe.matmul(pr[2 * u + k][:, :], m[:, :], x_in[u][:, 2 * k:2 * k + 2, :].rearrange("p n c -> p (n c)"),
                                  start=True, stop=True).then_inc(done, 1)

        @block.vector
        def _(dve):
            for u in range(2):
                dve.sem_inc(stored[u], FREE)
            with dve.Fori(0, STEPS // 2) as i:
                for u in range(2):
                    dve.wait_ge(stored[u], 16 * n_out * i + FREE)
                    for k in range(2):
                        part = lambda t: t[u][:, 2 * k:2 * k + 2, :].rearrange("p n c -> p (n c)")
                        dve.wait_ge(done, 2 * (2 * i + u) + k + 1)
                        if inverse:
                            ins = dve.tensor_tensor(part(y), pr[2 * u + k][:, :], part(r_in), ALU.add)
                        else:
                            ins = dve.tensor_copy(part(y), pr[2 * u + k][:, :])
                        ins.then_inc(copied, 1)


def frequency_phase(nc, name, a, ident, fwd_h, inv_h, w_mix, b_mix, g):
    V2 = 7
    CHUNKS = [(v, min(V2, NF - v)) for v in range(0, NF, V2)]
    VM = NF // 3
    NM = VM * NF
    VT = 4
    TURNS = [(v, min(VT, NF - v)) for v in range(0, NF, VT)]
    N2 = 2 * NF
    with Phase(nc, name) as ph:
        idt = ph.sb("ident", [P, P])
        fh = ph.sb("fh", [P, N2])
        ih = ph.sb("ih", [N2, P])
        wm = ph.sb("wm", [P, 2, 2, CH, P])
        wn = ph.sb("wn", [P, 2, CH, P])
        bm = ph.sb("bm", [P, 2, 2, CH])
        b_up = ph.sb("b_up", [P, 2, CH])
        b_dn = ph.sb("b_dn", [P, 2, CH])
        at = [ph.sb(f"a{u}", [P, NF, P]) for u in range(2)]
        z = ph.sb("z", [P, 2, NF * NF])
        o1 = ph.sb("o1", [P, 2, NF * NF])
        o2 = ph.sb("o2", [P, NF, 2, NF])
        up = [ph.sb(f"up{x}", [P, NM]) for x in range(2)]
        dn = [ph.sb(f"dn{x}", [P, NM]) for x in range(2)]
        d = ph.sb("d", [N2, NF, P])
        go = [ph.sb(f"g{x}", [P, VT, P]) for x in range(2)]
        zp = [ph.ps(f"zp{x}", [P, 512]) for x in range(2)]
        mp = [ph.ps(f"mp{x}", [P, 512]) for x in range(2)]
        tp = [ph.ps(f"tp{x}", [P, 512]) for x in range(2)]
        gp = [ph.ps(f"gp{x}", [P, 512]) for x in range(2)]

        consts_in = ph.sem("consts_in")
        zeroed = ph.sem("zeroed")
        consts = ph.sem("consts")
        a_loaded = ph.sems("a_loaded", CH)
        z_made = ph.sem("z_made")
        z_ready = ph.sem("z_ready")
        mixed = ph.sem("mixed")
        mix_read = ph.sem("mix_read")
        shrunk = ph.sem("shrunk")
        turned = ph.sem("turned")
        d_ready = ph.sem("d_ready")
        g_made = ph.sem("g_made")
        g_ready = ph.sem("g_ready")
        stored = ph.sems("stored", 2)
        block = ph.block()
        MIX = 12
        CONSTS = 5
        PER_STORE = [sum(1 + (max(v, 1) < min(v + nv, NF - 1)) for k, (v, nv) in enumerate(TURNS) if k % 2 == x)
                     for x in range(2)]
        units = [(b, j) for b in range(B) for j in range(CH)]

        @block.sync
        def _(sp):
            def load(n):
                b, j = units[n]
                cols = slice(j * P, (j + 1) * P)
                sp.dma_start(at[j][0:H, :, :], a[b, 0:NF, :, cols].rearrange("v h c -> h v c")).then_inc(a_loaded[j], 16)
                sp.dma_start(at[j][H:2 * H, 1:NF - 1, :], a[b, NF:2 * NF - 2, :, cols].rearrange("v h c -> h v c")).then_inc(a_loaded[j], 16)

            srcs = [(idt[:, :], ident), (fh[:, :], fwd_h), (ih[:, :], inv_h),
                    (wm[:, :, :, :, :].rearrange("p l r j n -> p (l r j) n"), w_mix.rearrange("l r j p n -> p (l r j) n")),
                    (bm[:, :, :, :].rearrange("p l r j -> p l (r j)"), b_mix.rearrange("l p n -> p l n"))]
            assert len(srcs) == CONSTS
            for dst, src in srcs:
                sp.dma_start(dst, src).then_inc(consts_in, 16)
            for n in range(2):
                load(n)
            for n, (b, j) in enumerate(units):
                for k, (v, nv) in enumerate(TURNS):
                    sp.wait_ge(g_ready, n * len(TURNS) + k + 1 + FREE)
                    if k == 0 and 1 <= n and n + 1 < len(units):
                        load(n + 1)
                    cols = slice(j * P, (j + 1) * P)
                    sp.dma_start(g[b, v:v + nv, :, cols].rearrange("v h c -> h v c"), go[k % 2][0:H, 0:nv, :]).then_inc(stored[k % 2], 16)
                    lo, hi = max(v, 1), min(v + nv, NF - 1)
                    if lo < hi:
                        sp.dma_start(g[b, NF - 1 + lo:NF - 1 + hi, :, cols].rearrange("v h c -> h v c"),
                                     go[k % 2][H:2 * H, lo - v:hi - v, :]).then_inc(stored[k % 2], 16)
            for x in range(2):
                sp.wait_ge(stored[x], 16 * PER_STORE[x] * len(units) + FREE)

        def unit_loop(eng):
            with eng.Fori(0, B) as i:
                for j in range(CH):
                    yield i * CH + j, j, i

        @block.tensor
        def _(pe):
            pe.wait_ge(consts_in, 16 * CONSTS)
            pe.wait_ge(consts, 3)
            for n, j, i in unit_loop(pe):
                pe.wait_ge(a_loaded[j], 32 * (i + 1))
                for k, (v, nv) in enumerate(CHUNKS):
                    pe.wait_ge(z_ready, n * len(CHUNKS) + max(k - 1, 0) + FREE)
                    for x in range(nv):
                        last = pe.matmul(zp[k % 2][:, x * N2:(x + 1) * N2], at[j][:, v + x, :], fh[:, :],
                                         start=True, stop=True)
                    last.then_inc(z_made, 1)
                for layer, src in enumerate((z, o1)):
                    for c in range(3):
                        if layer == 0:
                            done = sum(v < VM * (c + 1) for v, _ in CHUNKS)
                            pe.wait_ge(z_ready, n * len(CHUNKS) + done + FREE)
                        else:
                            pe.wait_ge(mix_read, n * MIX + 2 * c + 2 + FREE)
                        cols = slice(c * NM, (c + 1) * NM)
                        for part in range(2):
                            m = 6 * layer + 2 * c + part
                            pe.wait_ge(mix_read, n * MIX + max(m - 1, 0) + FREE)
                            w_im = wn[:, layer, j, :] if part == 0 else wm[:, layer, 1, j, :]
                            pe.matmul(mp[m % 2][:, 0:NM], wm[:, layer, 0, j, :], src[:, part, cols], start=True, stop=False)
                            pe.matmul(mp[m % 2][:, 0:NM], w_im, src[:, 1 - part, cols], start=False, stop=True).then_inc(mixed, 1)
                for k, (v, nv) in enumerate(TURNS):
                    c = min((v + nv - 1) // VM, 2)
                    pe.wait_ge(shrunk, n * 6 + 2 * (c + 1) + FREE)
                    pe.wait_ge(d_ready, n * len(TURNS) + max(k - 1, 0) + FREE)
                    for x in range(nv):
                        last = pe.transpose(tp[k % 2][0:N2, x * P:(x + 1) * P], o2[:, v + x, :, :].rearrange("p r u -> p (r u)"), idt[:, :])
                    last.then_inc(turned, 1)
                for k, (v, nv) in enumerate(TURNS):
                    pe.wait_ge(d_ready, n * len(TURNS) + k + 1 + FREE)
                    pe.wait_ge(g_ready, n * len(TURNS) + max(k - 1, 0) + FREE)
                    pe.matmul(gp[k % 2][:, 0:nv * P], ih[:, :], d[:, v:v + nv, :].rearrange("p v c -> p (v c)"),
                              start=True, stop=True).then_inc(g_made, 1)

        @block.scalar
        def _(act):
            act.sem_inc(mix_read, FREE)
            act.sem_inc(g_ready, FREE)
            for u in range(2):
                act.sem_inc(stored[u], FREE)
            act.wait_ge(consts_in, 16 * CONSTS)
            act.mul(wn[:, :, :, :], wm[:, :, 1, :, :], -1.0).then_inc(consts, 1)
            act.wait_ge(consts, 3)
            for n, j, i in unit_loop(act):
                for m in range(MIX):
                    layer, c, part = m // 6, m % 6 // 2, m % 2
                    act.wait_ge(mixed, n * MIX + m + 1)
                    if layer == 0:
                        act.activation(o1[:, part, c * NM:(c + 1) * NM], mp[m % 2][:, 0:NM], ACT.Relu,
                                       bias=bm[:, 0, part, j:j + 1]).then_inc(mix_read, 1)
                    else:
                        act.wait_ge(shrunk, n * 6 + max(m - 6 - 1, 0) + FREE)
                        act.activation(up[m % 2][:, :], mp[m % 2][:, 0:NM], ACT.Relu, bias=b_up[:, part, j:j + 1])
                        act.activation(dn[m % 2][:, :], mp[m % 2][:, 0:NM], ACT.Relu, bias=b_dn[:, part, j:j + 1],
                                       scale=-1.0).then_inc(mix_read, 1)
                for k, (v, nv) in enumerate(TURNS):
                    act.wait_ge(g_made, n * len(TURNS) + k + 1)
                    if k >= 2:
                        before = sum(1 + (max(a, 1) < min(a + b, NF - 1)) for q, (a, b) in enumerate(TURNS) if q % 2 == k % 2 and q < k)
                    else:
                        before = 0
                    act.wait_ge(stored[k % 2], (n * PER_STORE[k % 2] + before) * 16 + FREE)
                    act.activation(go[k % 2][:, 0:nv, :], gp[k % 2][:, 0:nv * P].rearrange("p (v c) -> p v c", c=P),
                                   ACT.Copy).then_inc(g_ready, 1)

        @block.vector
        def _(dve):
            dve.sem_inc(z_ready, FREE)
            dve.sem_inc(d_ready, FREE)
            dve.sem_inc(shrunk, FREE)
            for u in range(2):
                dve.memset(at[u][H:2 * H, 0:NF:NF - 1, :], 0.0).then_inc(zeroed, 1)
            dve.wait_ge(consts_in, 16 * CONSTS)
            dve.wait_ge(zeroed, 2)
            dve.tensor_scalar(b_up[:, :, :], bm[:, 1, :, :], SHRINK, None, ALU.subtract).then_inc(consts, 1)
            dve.tensor_scalar(b_dn[:, :, :], bm[:, 1, :, :], -1.0, SHRINK, ALU.mult, ALU.subtract).then_inc(consts, 1)
            for n, j, i in unit_loop(dve):
                zv = z[:, :, :].rearrange("p r (v u) -> p v r u", u=NF)
                for k, (v, nv) in enumerate(CHUNKS):
                    dve.wait_ge(z_made, n * len(CHUNKS) + k + 1)
                    dve.tensor_copy(zv[:, v:v + nv, :, :],
                                    zp[k % 2][:, 0:nv * N2].rearrange("p (v r u) -> p v r u", r=2, u=NF)).then_inc(z_ready, 1)
                for m in range(6):
                    c, part = m // 2, m % 2
                    dve.wait_ge(mix_read, n * MIX + 6 + m + 1 + FREE)
                    dve.tensor_tensor(o2[:, c * VM:(c + 1) * VM, part, :], up[m % 2][:, :].rearrange("p (v u) -> p v u", u=NF),
                                      dn[m % 2][:, :].rearrange("p (v u) -> p v u", u=NF), ALU.subtract).then_inc(shrunk, 1)
                for k, (v, nv) in enumerate(TURNS):
                    dve.wait_ge(turned, n * len(TURNS) + k + 1)
                    dve.tensor_copy(d[:, v:v + nv, :].rearrange("p v c -> p (v c)"), tp[k % 2][0:N2, 0:nv * P]).then_inc(d_ready, 1)


def build(nc, a, out):
    def scratch(name, shape, dt=F32):
        return nc.dram_tensor(name, shape, dt).ap()

    tokens = lambda ap: ap.rearrange("b h w c -> (b h w) c")
    image = lambda ap: ap.rearrange("(b h w) c -> b h w c", b=B, h=H)
    ident = a["ident"]
    x0 = tokens(a["x"])
    NHL, HDL, NHG, HDG = 8, C // 8, 4, C // 4

    qk_l = scratch("qk_local", (2, NHL, 2, HDL, T), F16)
    v_l = scratch("v_local", (T, NHL * (2 * HDL + 1)), F16)
    att_l = scratch("att_local", (B, PATCHES, P, C))
    x1 = scratch("x1", (T, C))
    front_phase(nc, "f0", "layer", x0, ident, a["w_qkv0"], a["b_qk0"], a["b_v0"], a["g10"], a["be10"],
                qk_l, v_l, NHL, True)
    local_attention_phase(nc, "l0", qk_l, v_l, ident, a["masks7"], att_l, NHL, 7, HDL ** -0.5)
    tail_phase(nc, "t0", "layer", att_l, x0, ident, a["w_proj0"], a["b_proj0"], x1, True,
               a["g20"], a["be20"], a["w10"], a["b10"], a["w20"], a["b20"])

    spec_a = scratch("spec_a", (B, 2 * NF - 2, H, C))
    spec_g = scratch("spec_g", (B, 2 * NF - 2, H, C))
    x2 = scratch("x2", (T, C))
    w_transform_phase(nc, "wf", image(x1), a["fwd_w"], spec_a)
    frequency_phase(nc, "fq", spec_a, ident, a["fwd_h"], a["inv_h"], a["w_mix"], a["b_mix"], spec_g)
    w_transform_phase(nc, "wi", spec_g, a["inv_w"], image(x2), image(x1))

    qk_2 = scratch("qk_local2", (2, NHL, 2, HDL, T), F16)
    v_2 = scratch("v_local2", (T, NHL * (2 * HDL + 1)), F16)
    att_2 = scratch("att_local2", (B, PATCHES, P, C))
    x3 = scratch("x3", (T, C))
    front_phase(nc, "f2", "arsinh", x2, ident, a["w_qkv2"], a["b_qk2"], a["b_v2"], a["g12"], a["be12"],
                qk_2, v_2, NHL, True)
    local_attention_phase(nc, "l2", qk_2, v_2, ident, a["masks3"], att_2, NHL, 3, HDL ** -0.5)
    tail_phase(nc, "t2", "arsinh", att_2, x2, ident, a["w_proj2"], a["b_proj2"], x3, True,
               a["g22"], a["be22"], a["w12"], a["b12"], a["w22"], a["b22"])

    affine = scratch("affine", (GROUPS, 2, C))
    xn = scratch("xn", (T, C))
    qk_g = scratch("qk_global", (2, NHG, 2, HDG, T), F16)
    v_g = scratch("v_global", (T, NHG * (2 * HDG + 1)), F16)
    att_g = scratch("att_global", (T, C))
    group_stats_phase(nc, "gs", x3, ident, a["ones_blocks"], a["g3"], a["be3"], affine)
    front_phase(nc, "f3", "group", x3, ident, a["w_qkv3"], None, None, None, None, qk_g, v_g, NHG, False,
                affine, xn)
    global_attention_phase(nc, "ga", qk_g, v_g, ident, att_g, NHG, C ** -0.5)
    tail_phase(nc, "t3", "none", att_g, xn, ident, a["w_out3"], a["b_out3"], tokens(out), False)


def lay_out(p):
    p = {k: np.asarray(v) for k, v in p.items()}
    col = lambda v: np.ascontiguousarray(v.reshape(-1, P).T)
    fwd_w, inv_w, fwd_h, inv_h = fourier_matrices()
    a = {
        "x": p["x"], "ident": np.eye(P, dtype=np.float32), "masks7": neighbour_masks(7), "masks3": neighbour_masks(3),
        "ones_blocks": np.kron(np.eye(P // 32), np.full((32, 32), 1 / 32)).astype(np.float32),
        "fwd_w": fwd_w, "inv_w": inv_w, "fwd_h": fwd_h, "inv_h": inv_h,
        "w_mix": block_diagonal(p["L1_conv_w1"], p["L1_conv_w2"]), "b_mix": mix_biases(p["L1_conv_b1"], p["L1_conv_b2"]),
    }
    l0, l2, l3 = (lambda n: p["L0_conv_" + n]), (lambda n: p["L2_conv_" + n]), (lambda n: p["L3_conv_" + n])
    names = {"w_qkv": l0("qkv_w").T, "w_proj": l0("proj_w").T, "b_proj": l0("proj_b"), "w1": l0("fc1_w").T,
             "b1": col(l0("fc1_b")), "w2": l0("fc2_w").T, "b2": l0("fc2_b"),
             "g1": col(l0("ln1_w")), "be1": col(l0("ln1_b")), "g2": col(l0("ln2_w")), "be2": col(l0("ln2_b")),
             "b_qk": col(l0("qkv_b")[:2 * C]), "b_v": l0("qkv_b")[2 * C:]}
    a.update({k + "0": v for k, v in names.items()})
    names = {"w_qkv": l2("qkv_w"), "w_proj": l2("proj_w"), "b_proj": l2("proj_b"), "w1": l2("mlp_w1"),
             "b1": col(l2("mlp_b1")), "w2": l2("mlp_w2"), "b2": l2("mlp_b2"),
             "g1": col(l2("n1_w")), "be1": col(l2("n1_b")), "g2": col(l2("n2_w")), "be2": col(l2("n2_b")),
             "b_qk": col(l2("qkv_b")[:2 * C]), "b_v": l2("qkv_b")[2 * C:]}
    a.update({k + "2": v for k, v in names.items()})
    a.update({"w_qkv3": l3("w_qkv").reshape(C, 4, 3, C // 4).transpose(0, 2, 1, 3).reshape(C, 3 * C),
              "w_out3": l3("w_out"), "b_out3": l3("b_out"), "g3": col(l3("gn_scale")), "be3": col(l3("gn_bias"))})
    return {k: np.ascontiguousarray(v) for k, v in a.items()}


def kernel(**inputs):
    import concourse.bacc as bacc
    from concourse.bass_utils import run_bass_kernel_spmd

    arrays = lay_out(inputs)
    nc = bacc.Bacc("TRN2", target_bir_lowering=False, num_devices=1)
    args = {k: nc.dram_tensor(f"in_{k}", v.shape, mybir.dt.from_np(v.dtype), kind="ExternalInput").ap()
            for k, v in arrays.items()}
    out = nc.dram_tensor("out_image", (B, H, W, C), F32, kind="ExternalOutput").ap()
    build(nc, args, out)
    r = run_bass_kernel_spmd(nc, [{f"in_{k}": v for k, v in arrays.items()}], core_ids=[0])
    return r.results[0]["out_image"]
```

```python
import math
from contextlib import ExitStack

import numpy as np
import concourse.bass as bass
from concourse import mybir

F32 = mybir.dt.float32
F16 = mybir.dt.float16
BF16 = mybir.dt.bfloat16
ALU = mybir.AluOpType
ACT = mybir.ActivationFunctionType
AX = mybir.AxisListType

P = 128
B, H, W, C = 2, 64, 64, 256
T = B * H * W
GT = 512
GROUPS = T // GT
TPG = GT // P
CH = C // P
PR, PC = 8, 16
LN_EPS = 1e-5
OPERAND_SCALE = 16.0
WEIGHT_SCALE = 64.0
PROB_SCALE = 1024.0
FREE = 1


class Phase:

    def __init__(self, nc, name):
        self.nc, self.name, self.stack = nc, name, ExitStack()
        self.used = []

    def __enter__(self):
        self.stack.__enter__()
        return self

    def __exit__(self, *e):
        self.blocks.__exit__(*e)
        for sem in self.used:
            self.nc.sync.sem_clear(sem)
        self.nc.all_engine_barrier()
        return self.stack.__exit__(*e)

    def sb(self, name, shape, dt=F32):
        return self.stack.enter_context(self.nc.sbuf_tensor(f"{self.name}_{name}", shape, dt))

    def ps(self, name, shape, dt=F32):
        return self.stack.enter_context(self.nc.psum_tensor(f"{self.name}_{name}", shape, dt))

    def sem(self, name):
        self.used.append(self.stack.enter_context(self.nc.semaphore(f"{self.name}_{name}")))
        return self.used[-1]

    def sems(self, name, n):
        return [self.sem(f"{name}{k}") for k in range(n)]

    def block(self):
        self.blocks = self.nc.Block()
        return self.blocks.__enter__()


def passed(eng, marker):
    eng.sem_inc(marker, 1)


class Chain:

    def __init__(self, eng, sem, start=0):
        self.eng, self.sem, self.start, self.n = eng, sem, start, 0

    def step(self, ins):
        ins.then_inc(self.sem, 1)
        self.n += 1

    def settle(self):
        self.eng.wait_ge(self.sem, self.start + self.n)

    def link(self, ins):
        self.step(ins)
        self.settle()


def row(ap):
    return ap.rearrange("(o n) -> o n", o=1).broadcast_to([P, ap.shape[0]])



def front_phase(nc, name, kind, x, ident, w_qkv, b_qk, b_v, gamma, beta, qk_out, v_out, heads,
                q_patches, group_affine=None, xn_out=None):
    hd = C // heads
    vw = 2 * hd + 1
    V_UNITS, QK_UNITS = 2, 4
    UNITS = V_UNITS + QK_UNITS
    START = CH + 1
    with Phase(nc, name) as ph:
        idt = ph.sb("ident", [P, P])
        w = ph.sb("w", [P, CH, 3 * C])
        w_hi = ph.sb("w_hi", [P, CH, 3 * C], F16)
        w_lo = ph.sb("w_lo", [P, CH, 3 * C], F16)
        x_in = [ph.sb(f"x{u}", [P, TPG, C]) for u in range(2)]
        xn = [ph.sb(f"xn{u}", [P, TPG, C]) for u in range(2)]
        aux = ph.sb("aux", [P, TPG, C])
        root = ph.sb("root", [P, TPG, C])
        stats = ph.sb("stats", [P, TPG, 6])
        mv = ph.sb("mv", [P, TPG, 2])
        std = ph.sb("std", [P, TPG])
        rstd = ph.sb("rstd", [P, TPG])
        eps = ph.sb("eps", [P, 1])
        ab = [ph.sb(f"ab{u}", [P, 2, C]) for u in range(2)]
        gcol = ph.sb("gamma", [P, CH])
        bcol = ph.sb("beta", [P, CH])
        qkb = ph.sb("qkb", [P, 4])
        vb = ph.sb("vb", [P, C])
        xT = [ph.sb(f"xT{u}", [P, CH, GT]) for u in range(2)]
        xT_hi = [ph.sb(f"xT_hi{u}", [P, CH, GT], F16) for u in range(2)]
        xT_lo = [ph.sb(f"xT_lo{u}", [P, CH, GT], F16) for u in range(2)]
        lin = ph.sb("lin", [P, QK_UNITS, 512])
        vlin = ph.sb("vlin", [P, V_UNITS, 512])
        qks = [ph.sb(f"qks{u}", [P, 4, 2, GT], F16) for u in range(2)]
        vs = [ph.sb(f"vs{u}", [P, TPG, heads * vw], F16) for u in range(2)]
        tp = [ph.ps(f"tp{c}", [P, GT]) for c in range(CH)]
        mm = [ph.ps(f"mm{k}", [P, 512]) for k in range(UNITS)]

        vectors_in = ph.sem("vectors_in")
        w_in = ph.sem("w_in")
        w_split = ph.sem("w_split")
        xt_lo = ph.sem("xt_lo")
        sp_marker = ph.sem("sp_marker")
        consts = ph.sem("consts")
        bias_ready = ph.sem("bias_ready")
        scaled = ph.sem("scaled")
        x_loaded = ph.sems("x_loaded", 2)
        x_used = ph.sems("x_used", 2)
        act_steps = ph.sem("act_steps")
        norm_steps = ph.sem("norm_steps")
        split_steps = ph.sem("split_steps")
        marker = ph.sem("marker")
        var_ready = ph.sem("var_ready")
        std_ready = ph.sem("std_ready")
        square_ready = ph.sem("square_ready")
        root_ready = ph.sem("root_ready")
        sum_ready = ph.sem("sum_ready")
        log_ready = ph.sem("log_ready")
        xn_ready = ph.sem("xn_ready")
        tp_ready = ph.sem("tp_ready")
        xt_ready = ph.sem("xt_ready")
        mm_ready = ph.sem("mm_ready")
        qk_hi = ph.sem("qk_hi")
        qk_lo = ph.sem("qk_lo")
        v_split = ph.sem("v_split")
        qk_stored = ph.sems("qk_stored", 2)
        v_stored = ph.sems("v_stored", 2)
        xn_stored = ph.sems("xn_stored", 2)
        block = ph.block()

        loads = [(idt[:, :], ident)]
        if gamma is not None:
            loads += [(gcol[:, :], gamma), (bcol[:, :], beta)]
        if b_qk is not None:
            loads += [(qkb[:, :], b_qk), (vb[:, :], row(b_v))]
        per_x = 16 * (1 + (group_affine is not None))

        def groups(eng):
            with eng.Fori(0, GROUPS // 2 - 1) as i:
                for u in range(2):
                    yield i, u, True
            for u in range(2):
                yield GROUPS // 2 - 1, u, u == 0

        @block.sync
        def _(sp):
            def load(g, u):
                sp.dma_start(x_in[u][:, :, :],
                             x[bass.ds(g * GT, GT)].rearrange("(t p) c -> p t c", p=P)).then_inc(x_loaded[u], 16)
                if group_affine is not None:
                    sp.dma_start(ab[u][:, :, :], group_affine[bass.ds(g, 1)].broadcast_to([P, 2, C])).then_inc(x_loaded[u], 16)

            def store(g, u):
                if xn_out is not None:
                    sp.wait_ge(xn_ready, g + 1 + FREE)
                    sp.dma_start(xn_out[bass.ds(g * GT, GT)].rearrange("(t p) f -> p t f", p=P),
                                 xn[u][:, :, :]).then_inc(xn_stored[u], 16)
                sp.wait_ge(v_split, g + 1 + FREE)
                sp.dma_start(v_out[bass.ds(g * GT, GT)].rearrange("(t p) f -> p t f", p=P),
                             vs[u][:, :, :]).then_inc(v_stored[u], 16)
                for m in range(QK_UNITS):
                    sp.wait_ge(qk_lo, QK_UNITS * g + m + 1 + FREE)
                    passed(sp, sp_marker)
                    some = slice((m % 2) * (heads // 2), (m % 2 + 1) * (heads // 2))
                    for s in range(2):
                        sp.dma_start(qk_out[m // 2, some, s, :, bass.ds(g * GT, GT)],
                                     qks[u][:, m, s, :]).then_inc(qk_stored[u], 16)

            for u in range(2):
                load(u, u)
            for dst, src in loads:
                sp.dma_start(dst, src).then_inc(vectors_in, 16)
            sp.dma_start(w[:, :, :], w_qkv.rearrange("(c p) n -> p c n", p=P)).then_inc(w_in, 16)
            with sp.Fori(0, GROUPS // 2 - 1) as i:
                for u in range(2):
                    sp.wait_ge(x_used[u], i + 1)
                    load(2 * i + 2 + u, u)
                    store(2 * i + u, u)
            for u in range(2):
                store(GROUPS - 2 + u, u)
            for u in range(2):
                sp.wait_ge(qk_stored[u], 32 * QK_UNITS * (GROUPS // 2) + FREE)
                sp.wait_ge(v_stored[u], 16 * (GROUPS // 2) + FREE)
                if xn_out is not None:
                    sp.wait_ge(xn_stored[u], 16 * (GROUPS // 2) + FREE)

        @block.gpsimd
        def _(pool):
            pool.sem_inc(qk_lo, FREE)
            pool.sem_inc(xt_lo, FREE)
            pool.memset(eps[:, :], LN_EPS).then_inc(consts, 1)
            for u in range(2):
                v = vs[u][:, :, :].rearrange("p t (h f) -> p (t h) f", f=vw)
                pool.memset(v[:, :, hd:hd + 1], OPERAND_SCALE).then_inc(consts, 1)
            with pool.Fori(0, GROUPS // 2) as i:
                for u in range(2):
                    g = 2 * i + u
                    for c in range(CH):
                        pool.wait_ge(xt_ready, CH * g + c + 1 + START)
                        pool.tensor_tensor(xT_lo[u][:, c, :], xT[u][:, c, :], xT_hi[u][:, c, :],
                                           ALU.subtract).then_inc(xt_lo, 1)
                    for m in range(QK_UNITS):
                        pool.wait_ge(qk_hi, QK_UNITS * g + m + 1)
                        pool.tensor_tensor(qks[u][:, m, 1, :], lin[:, m, :], qks[u][:, m, 0, :],
                                           ALU.subtract).then_inc(qk_lo, 1)

        @block.tensor
        def _(pe):
            HH, HL, LH = ((0, 0), (0, 1), (1, 0))
            x_parts, w_parts = (xT_hi, xT_lo), (w_hi, w_lo)
            passes = [(*parts, c) for parts in (HH, HL, LH) for c in range(CH)]
            pe.wait_ge(vectors_in, 16 * len(loads))

            def turn(i, u):
                pe.wait_ge(xn_ready, 2 * i + u + 1 + FREE)
                for c in range(CH):
                    for t in range(TPG):
                        last = pe.transpose(tp[c][:, t * P:(t + 1) * P], xn[u][:, t, c * P:(c + 1) * P], idt[:, :])
                    last.then_inc(tp_ready, 1)

            turn(0, 0)
            pe.wait_ge(w_split, 2)
            for i, u, more in groups(pe):
                g = 2 * i + u
                pe.wait_ge(xt_ready, CH * (g + 1) + START)
                for m in range(QK_UNITS):
                    for n, (xp, wp, c) in enumerate(passes):
                        if m == 0 and n == passes.index((*LH, 0)):
                            pe.wait_ge(xt_lo, CH * (g + 1) + FREE)
                        last = pe.matmul(mm[m][:, :], w_parts[wp][:, c, m * P:(m + 1) * P], x_parts[xp][u][:, c, :],
                                         start=(n == 0), stop=(n == len(passes) - 1))
                    last.then_inc(mm_ready, 1)
                if more:
                    turn(i + u, 1 - u)
                pe.wait_ge(v_split, g + FREE)
                for k in range(V_UNITS):
                    for t in range(2):
                        tt = 2 * k + t
                        for n, (xp, wp, c) in enumerate(passes):
                            last = pe.matmul(mm[QK_UNITS + k][:, t * C:(t + 1) * C],
                                             x_parts[xp][u][:, c, tt * P:(tt + 1) * P],
                                             w_parts[wp][:, c, 2 * C:3 * C],
                                             start=(n == 0), stop=(n == len(passes) - 1))
                    last.then_inc(mm_ready, 1)
        @block.scalar
        def _(act):
            act.sem_inc(xt_ready, START)
            for u in range(2):
                act.sem_inc(qk_stored[u], FREE)
            act.wait_ge(vectors_in, 16 * len(loads))
            act.wait_ge(consts, 3)
            if gamma is not None:
                act.mul(gcol[:, :], gcol[:, :], OPERAND_SCALE).then_inc(scaled, 1)
                act.mul(bcol[:, :], bcol[:, :], OPERAND_SCALE).then_inc(scaled, 1)
                act.wait_ge(scaled, 2)
            if b_qk is not None:
                act.mul(qkb[:, :], qkb[:, :], OPERAND_SCALE).then_inc(bias_ready, 1)
                act.mul(vb[:, :], vb[:, :], OPERAND_SCALE).then_inc(bias_ready, 1)
                act.wait_ge(bias_ready, 2)

            def root_part(i, u):
                g = 2 * i + u
                if kind == "layer":
                    act.wait_ge(var_ready, g + 1)
                    act.activation(std[:, :], mv[:, :, 1], ACT.Sqrt, bias=eps[:, :]).then_inc(std_ready, 1)
                if kind == "arsinh":
                    act.wait_ge(square_ready, g + 1)
                    act.activation(root[:, :, :], root[:, :, :], ACT.Sqrt, bias=1.0).then_inc(root_ready, 1)

            def log_part(i, u):
                if kind == "arsinh":
                    g = 2 * i + u
                    act.wait_ge(sum_ready, g + 1)
                    act.activation(aux[:, :, :], aux[:, :, :], ACT.Ln).then_inc(act_steps, 1)
                    act.wait_ge(act_steps, g + 1)
                    act.activation(root[:, :, :], x_in[u][:, :, :], ACT.Sign).then_inc(log_ready, 1)

            def split(g, m, u):
                act.wait_ge(mm_ready, UNITS * g + m + 1)
                bank = mm[m]
                bias = qkb[:, m:m + 1] if b_qk is not None else 0.0
                src, whole, high = bank[:, :], lin[:, m, :], qks[u][:, m, 0, :]
                if q_patches and m < 2:
                    src = src.rearrange("p (r t c) -> p t r c", r=PR, c=PC)
                    whole, high = (y.rearrange("p (t r c) -> p t r c", r=PR, c=PC) for y in (whole, high))
                act.activation(whole, src, ACT.Identity, bias=bias, scale=1 / WEIGHT_SCALE)
                act.activation(high, src, ACT.Identity, bias=bias, scale=1 / WEIGHT_SCALE).then_inc(qk_hi, 1)

            root_part(0, 0)
            log_part(0, 0)
            for i, u, more in groups(act):
                g = 2 * i + u
                for c in range(CH):
                    act.wait_ge(tp_ready, CH * g + c + 1)
                    gain = OPERAND_SCALE if gamma is None else gcol[:, c:c + 1]
                    shift = 0.0 if gamma is None else bcol[:, c:c + 1]
                    act.activation(xT[u][:, c, :], tp[c][:, :], ACT.Identity, bias=shift, scale=gain)
                    act.activation(xT_hi[u][:, c, :], tp[c][:, :], ACT.Identity, bias=shift,
                                   scale=gain).then_inc(xt_ready, 1)
                if more:
                    root_part(i + u, 1 - u)
                    log_part(i + u, 1 - u)
                act.wait_ge(qk_stored[u], 32 * QK_UNITS * i + FREE)
                act.wait_ge(qk_lo, QK_UNITS * g + FREE)
                for m in range(QK_UNITS):
                    split(g, m, u)

        @block.vector
        def _(dve):
            dve.sem_inc(xn_ready, FREE)
            dve.sem_inc(v_split, FREE)
            for u in range(2):
                dve.sem_inc(xn_stored[u], FREE)
            for u in range(2):
                dve.sem_inc(v_stored[u], FREE)
            if b_qk is not None:
                dve.wait_ge(bias_ready, 2)
            dve.wait_ge(consts, 3)

            def norm(i, u):
                g = 2 * i + u
                steps = Chain(dve, norm_steps, {"layer": 2, "arsinh": 1, "group": 1}[kind] * g)
                dve.wait_ge(x_loaded[u], per_x * (i + 1))
                if kind != "arsinh":
                    dve.wait_ge(xt_ready, CH * g - CH + START)
                if xn_out is not None:
                    dve.wait_ge(xn_stored[u], 16 * i + FREE)
                if kind == "layer":
                    for t in range(TPG):
                        last = dve.bn_stats(stats[:, t, :], x_in[u][:, t, :])
                    steps.link(last)
                    passed(dve, marker)
                    for t in range(TPG):
                        last = dve.bn_aggr(mv[:, t, :], stats[:, t, :])
                    last.then_inc(var_ready, 1)
                    dve.wait_ge(var_ready, g + 1)
                    dve.wait_ge(std_ready, g + 1)
                    steps.link(dve.reciprocal(rstd[:, :], std[:, :]))
                    for t in range(TPG):
                        last = dve.tensor_scalar(xn[u][:, t, :], x_in[u][:, t, :], mv[:, t, 0:1],
                                                 rstd[:, t:t + 1], ALU.subtract, ALU.mult)
                if kind == "arsinh":
                    dve.tensor_tensor(root[:, :, :], x_in[u][:, :, :], x_in[u][:, :, :],
                                      ALU.mult).then_inc(square_ready, 1)
                    steps.link(dve.scalar_tensor_tensor(aux[:, :, :], x_in[u][:, :, :], -1.0, x_in[u][:, :, :],
                                                        ALU.mult, ALU.max))
                    dve.wait_ge(root_ready, g + 1)
                    dve.tensor_tensor(aux[:, :, :], aux[:, :, :], root[:, :, :], ALU.add).then_inc(sum_ready, 1)
                    dve.wait_ge(xt_ready, CH * g - CH + START)
                    dve.wait_ge(log_ready, g + 1)
                    last = dve.tensor_tensor(xn[u][:, :, :], aux[:, :, :], root[:, :, :], ALU.mult)
                if kind == "group":
                    a = ab[u][:, 0:1, :].broadcast_to([P, TPG, C])
                    b = ab[u][:, 1:2, :].broadcast_to([P, TPG, C])
                    steps.link(dve.tensor_tensor(aux[:, :, :], x_in[u][:, :, :], a, ALU.mult))
                    last = dve.tensor_tensor(xn[u][:, :, :], aux[:, :, :], b, ALU.add)
                last.then_inc(xn_ready, 1)
                dve.wait_ge(xn_ready, g + 1 + FREE)
                dve.sem_inc(x_used[u], 1)

            def split(i, u):
                g = 2 * i + u
                steps = Chain(dve, split_steps, 2 * V_UNITS * g)
                dve.wait_ge(v_stored[u], 16 * i + FREE)
                for k in range(V_UNITS):
                    dve.wait_ge(mm_ready, UNITS * g + QK_UNITS + k + 1)
                    src = mm[QK_UNITS + k][:, :].rearrange("p (t c) -> p t c", c=C)
                    dst = vlin[:, k, :].rearrange("p (t c) -> p t c", c=C)
                    if b_qk is not None:
                        bias = vb[:, :].rearrange("p (o c) -> p o c", o=1).broadcast_to([P, 2, C])
                        ins = dve.scalar_tensor_tensor(dst, src, 1 / WEIGHT_SCALE, bias, ALU.mult, ALU.add)
                    else:
                        ins = dve.tensor_scalar(dst, src, 1 / WEIGHT_SCALE, None, ALU.mult)
                    steps.link(ins)
                    whole = vlin[:, k, :].rearrange("p (h f) -> p h f", f=hd)
                    parts = vs[u][:, 2 * k:2 * k + 2, :].rearrange("p t (h f) -> p (t h) f", f=vw)
                    steps.link(dve.tensor_copy(parts[:, :, 0:hd], whole))
                    last = dve.tensor_tensor(parts[:, :, hd + 1:vw], whole, parts[:, :, 0:hd], ALU.subtract)
                last.then_inc(v_split, 1)
                dve.wait_ge(v_split, g + 1 + FREE)

            norm(0, 0)
            dve.wait_ge(w_in, 16)
            dve.tensor_scalar(w_hi[:, :, :], w[:, :, :], WEIGHT_SCALE, None, ALU.mult).then_inc(w_split, 1)
            dve.wait_ge(w_split, 1)
            dve.scalar_tensor_tensor(w_lo[:, :, :], w[:, :, :], WEIGHT_SCALE, w_hi[:, :, :],
                                     ALU.mult, ALU.subtract).then_inc(w_split, 1)
            for i, u, more in groups(dve):
                if more:
                    norm(i + u, 1 - u)
                split(i, u)


def global_attention_phase(nc, name, qk, v, ident, out, heads, scale):
    S = H * W
    hd = C // heads
    vw = 2 * hd + 1
    assert 2 * hd == P
    QB = S // GT
    KT = S // P
    QT = GT // P
    KC = S // 512
    UNITS = QT * KC
    AHEAD = 3
    EARLY = 3
    MAX_STEPS = 26
    COL_STEP, ROW_STEP, COPY_STEP = 25, 27, 28
    LOW_START = 3
    HEADS = B * heads
    STAT = 256.0
    exp_scale = scale / OPERAND_SCALE ** 2

    def units_of(kt):
        if kt >= KT - EARLY:
            return [(2, kt - (KT - EARLY))]
        upto = lambda x: EARLY + min(x * (UNITS - EARLY) // MAX_STEPS, UNITS - EARLY)
        return [(1, k) for k in range(upto(kt), upto(kt + 1))]

    def by_pool(kt):
        return kt % 2 == 0

    def lows(kt):
        n = sum(by_pool(x) for x in range(kt + 1))
        return kt + 1 - n, n

    D_LOWS, P_LOWS = lows(KT - 1)
    assert by_pool(0)

    with Phase(nc, name) as ph:
        idf = ph.sb("ident", [P, P])
        id16 = ph.sb("ident16", [P, P], F16)
        q_hl = [ph.sb(f"q_hl{u}", [P, S], F16) for u in range(2)]
        q_hm = [ph.sb(f"q_hm{u}", [P, S], F16) for u in range(2)]
        k_hh = [ph.sb(f"k_hh{u}", [P, S], F16) for u in range(2)]
        k_ll = [ph.sb(f"k_ll{u}", [P, S], F16) for u in range(2)]
        k_lc = [ph.sb(f"k_lc{u}", [P, S], F16) for u in range(2)]
        vt = [ph.sb(f"v{u}", [P, KT, vw], F16) for u in range(2)]
        o_head = [ph.sb(f"o{u}", [P, S // P, hd]) for u in range(2)]
        part_max = ph.sb("part_max", [P, QT, KC])
        neg_max = ph.sb("neg_max", [P, QT])
        max_cols = ph.sb("max_cols", [P, QT, P], F16)
        shift = ph.sb("shift", [P, 1])
        p32 = [ph.sb(f"p32_{k}", [P, GT]) for k in range(4)]
        p_hi = [ph.sb(f"p_hi{k}", [P, GT], F16) for k in range(4)]
        p_lo = [ph.sb(f"p_lo{k}", [P, GT], F16) for k in range(4)]
        o_low = ph.sb("o_low", [P, QT, hd])
        o_sum = ph.sb("o_sum", [P, QT, hd])
        rden = ph.sb("rden", [P, QT])
        st = [ph.ps(f"st{k}", [P, GT]) for k in range(4)]
        mx = [ph.ps(f"mx{k}", [P, 512]) for k in range(2)]
        o_ps = ph.ps("o_ps", [P, 2, 512])
        row_ps = mx[0]

        consts_in = ph.sem("consts_in")
        zeroed = ph.sem("zeroed")
        consts = ph.sem("consts")
        head_loaded = ph.sems("head_loaded", 2)
        st_ready = ph.sem("st_ready")
        exp_done = ph.sem("exp_done")
        low_dve = ph.sem("low_dve")
        low_pool = ph.sem("low_pool")
        mx_ready = ph.sem("mx_ready")
        mx_read = ph.sem("mx_read")
        dve_steps = ph.sem("dve_steps")
        cols_ready = ph.sem("cols_ready")
        rows_ready = ph.sem("rows_ready")
        q_ready = ph.sem("q_ready")
        block_done = ph.sem("block_done")
        block_out = ph.sem("block_out")
        head_stored = ph.sems("head_stored", 2)
        block = ph.block()
        LOADS = 8

        @block.sync
        def _(sp):
            def load(n, u):
                b, h = n // heads % B, n % heads
                toks = slice(b * S, (b + 1) * S)
                parts = [(q_hl[u][:, :], qk[0, h, :, :, toks].rearrange("s d n -> (s d) n")),
                         (q_hm[u][0:hd, :], qk[0, h, 0, :, toks]),
                         (k_hh[u][0:hd, :], qk[1, h, 0, :, toks]), (k_hh[u][hd:P, :], qk[1, h, 0, :, toks]),
                         (k_ll[u][0:hd, :], qk[1, h, 1, :, toks]), (k_ll[u][hd:P, :], qk[1, h, 1, :, toks]),
                         (k_lc[u][0:hd, :], qk[1, h, 1, :, toks]),
                         (vt[u][:, :, :], v[toks, h * vw:(h + 1) * vw].rearrange("(t p) f -> p t f", p=P))]
                assert len(parts) == LOADS
                for dst, src in parts:
                    sp.dma_start(dst, src).then_inc(head_loaded[u], 16)

            sp.dma_start(idf[:, :], ident).then_inc(consts_in, 16)
            for n in range(2):
                load(n, n)
            for n in range(HEADS):
                u = n % 2
                b, h = n // heads, n % heads
                sp.wait_ge(block_out, QB * (n + 1) + FREE)
                sp.dma_start(out[b * S:(b + 1) * S, h * hd:(h + 1) * hd].rearrange("(t p) f -> p t f", p=P),
                             o_head[u][:, :, :]).then_inc(head_stored[u], 16)
                if n + 2 <= HEADS:
                    load(n + 2, u)
            for u in range(2):
                sp.wait_ge(head_stored[u], 16 * (HEADS // 2) + FREE)

        @block.gpsimd
        def _(pool):
            pool.sem_inc(low_pool, LOW_START)
            with pool.Fori(0, HEADS // 2) as a:
                for u in range(2):
                    with pool.Fori(0, QB) as qb:
                        j = a * (2 * QB) + u * QB + qb
                        for kt in range(KT):
                            if by_pool(kt):
                                pool.wait_ge(exp_done, j * KT + kt + 5)
                                pool.tensor_tensor(p_lo[kt % 4][:, :], p32[kt % 4][:, :], p_hi[kt % 4][:, :],
                                                   ALU.subtract).then_inc(low_pool, 1)

        @block.tensor
        def _(pe):
            def max_unit(base, k, u, q0):
                tq, c = k // KC, k % KC
                if not (isinstance(base, int) and base + k < 2):
                    pe.wait_ge(mx_read, base + k - 1)
                lhs = q_hl[u][:, bass.ds(q0 + tq * P, P)]
                pe.matmul(mx[k % 2][:, :], lhs, k_hh[u][:, c * 512:(c + 1) * 512], start=True, stop=False)
                pe.matmul(mx[k % 2][:, :], lhs, k_ll[u][:, c * 512:(c + 1) * 512], start=False,
                          stop=True).then_inc(mx_ready, 1)

            def max_rows(mj):
                pe.wait_ge(cols_ready, mj + 1)
                for tq in range(QT):
                    last = pe.matmul(row_ps[:, tq * P:(tq + 1) * P], max_cols[:, tq, :], id16[:, :],
                                     start=(tq == 0), stop=(tq == QT - 1), skip_group_check=True)
                last.then_inc(rows_ready, 1)

            def values(j, kt, u):
                d, p = lows(kt)
                if by_pool(kt):
                    pe.wait_ge(low_pool, j * P_LOWS + p + LOW_START)
                else:
                    pe.wait_ge(low_dve, j * D_LOWS + d + LOW_START)
                if kt == 0:
                    pe.wait_ge(block_out, j + FREE)
                for tq in range(QT):
                    o = o_ps[:, tq // 2, (tq % 2) * vw:(tq % 2 + 1) * vw]
                    pe.matmul(o, p_hi[kt % 4][:, tq * P:(tq + 1) * P], vt[u][:, kt, :],
                              start=(kt == 0 and tq % 2 == 0), stop=(kt == KT - 1), skip_group_check=True)
                    last = pe.matmul(o[:, 0:hd + 1], p_lo[kt % 4][:, tq * P:(tq + 1) * P], vt[u][:, kt, 0:hd + 1],
                                     start=False, stop=(kt == KT - 1), skip_group_check=True)
                if kt == KT - 1:
                    last.then_inc(block_done, 1)

            def scores(base, kt, u, q0):
                pe.wait_ge(exp_done, base + kt + 1)
                pe.matmul(st[kt % 4][:, :], k_hh[u][:, kt * P:(kt + 1) * P],
                          q_hl[u][:, bass.ds(q0, GT)], start=True, stop=False)
                pe.matmul(st[kt % 4][:, :], k_lc[u][:, kt * P:(kt + 1) * P],
                          q_hm[u][:, bass.ds(q0, GT)], start=False, stop=True).then_inc(st_ready, 1)

            def attend(j, u, qb, ahead):
                for kt in range(KT):
                    if kt + AHEAD < KT:
                        scores(j * KT, kt + AHEAD, u, qb * GT)
                    else:
                        if kt + AHEAD == KT:
                            pe.wait_ge(q_ready, j + 2)
                        scores((j + 1) * KT, kt + AHEAD - KT, *ahead[0])
                    for n, k in units_of(kt):
                        max_unit((j + n) * UNITS, k, *ahead[n - 1])
                    if kt == ROW_STEP:
                        max_rows(j + 1)
                    values(j, kt, u)

            pe.wait_ge(consts, 5)
            pe.wait_ge(head_loaded[0], 16 * LOADS)
            for k in range(UNITS):
                max_unit(0, k, 0, 0)
            max_rows(0)
            pe.wait_ge(q_ready, 1)
            for k in range(EARLY):
                max_unit(UNITS, k, 0, GT)
            for kt in range(AHEAD):
                scores(0, kt, 0, 0)
            with pe.Fori(0, HEADS // 2) as a:
                for u in range(2):
                    first = a * (2 * QB) + u * QB
                    with pe.Fori(0, QB - 2) as qb:
                        attend(first + qb, u, qb, [(u, (qb + 1) * GT), (u, (qb + 2) * GT)])
                    pe.wait_ge(head_loaded[1 - u], 16 * LOADS * (a + 1 + u))
                    attend(first + QB - 2, u, QB - 2, [(u, (QB - 1) * GT), (1 - u, 0)])
                    attend(first + QB - 1, u, QB - 1, [(1 - u, 0), (1 - u, GT)])

        @block.scalar
        def _(act):
            act.sem_inc(exp_done, 4)
            act.wait_ge(consts_in, 16)
            act.activation(id16[:, :], idf[:, :], ACT.Copy).then_inc(consts, 1)
            act.wait_ge(consts, 5)
            with act.Fori(0, HEADS // 2) as a:
                for u in range(2):
                    with act.Fori(0, QB) as qb:
                        j = a * (2 * QB) + u * QB + qb
                        for kt in range(KT):
                            before = (kt - 4) % KT
                            d, p = lows(before)
                            if by_pool(before):
                                act.wait_ge(low_pool, j * P_LOWS + (p if kt >= 4 else p - P_LOWS) + LOW_START)
                            else:
                                act.wait_ge(low_dve, j * D_LOWS + (d if kt >= 4 else d - D_LOWS) + LOW_START)
                            act.wait_ge(st_ready, j * KT + kt + 1)
                            act.activation(p32[kt % 4][:, :], st[kt % 4][:, :], ACT.Exp, bias=shift[:, :],
                                           scale=exp_scale)
                            act.activation(p_hi[kt % 4][:, :], st[kt % 4][:, :], ACT.Exp, bias=shift[:, :],
                                           scale=exp_scale).then_inc(exp_done, 1)

        @block.vector
        def _(dve):
            dve.sem_inc(low_dve, LOW_START)
            for u in range(2):
                dve.sem_inc(head_stored[u], FREE)
            dve.sem_inc(block_out, FREE)
            OWN = 4

            def reduce_unit(base, k):
                dve.wait_ge(mx_ready, base + k + 1)
                dve.tensor_reduce(part_max[:, k // KC, k % KC:k % KC + 1], mx[k % 2][:, :], AX.X,
                                  ALU.max).then_inc(mx_read, 1)

            def max_to_cols(mj, steps):
                dve.wait_ge(mx_read, (mj + 1) * UNITS)
                steps.link(dve.tensor_reduce(neg_max[:, :], part_max[:, :, :], AX.X, ALU.max, negate=True))
                steps.link(dve.tensor_scalar(max_cols[:, :, hd], neg_max[:, :], 1.0 / STAT, None, ALU.mult))
                dve.scalar_tensor_tensor(max_cols[:, :, hd + 1], neg_max[:, :], 1.0 / STAT, max_cols[:, :, hd],
                                         ALU.mult, ALU.subtract).then_inc(cols_ready, 1)

            def rows_to_q(mj, u, q0):
                dve.wait_ge(rows_ready, mj + 1)
                dve.tensor_copy(q_hm[u][hd:P, bass.ds(q0, GT)], row_ps[hd:P, :]).then_inc(q_ready, 1)

            def low(j, kt):
                if by_pool(kt):
                    return
                dve.wait_ge(exp_done, j * KT + kt + 5)
                dve.tensor_tensor(p_lo[kt % 4][:, :], p32[kt % 4][:, :], p_hi[kt % 4][:, :],
                                  ALU.subtract).then_inc(low_dve, 1)

            def attend(a, j, u, qb, u_next, q_next):
                steps = Chain(dve, dve_steps, 2 + OWN * j)
                for kt in range(KT):
                    if kt + 1 < KT:
                        low(j, kt + 1)
                    for n, k in units_of(kt):
                        reduce_unit((j + n) * UNITS, k)
                    if kt == COL_STEP:
                        max_to_cols(j + 1, steps)
                    if kt == COPY_STEP:
                        rows_to_q(j + 1, u_next, q_next)
                dve.wait_ge(block_done, j + 1)
                sums = o_ps[:, :, 0:2 * vw].rearrange("p b (t f) -> p b t f", f=vw)
                four = lambda x: x[:, :, :].rearrange("p (b t) f -> p b t f", t=2)
                dve.tensor_copy(four(o_low), sums[:, :, :, hd + 1:vw])
                steps.link(dve.reciprocal(rden[:, :].rearrange("p (b t) -> p b t", t=2), sums[:, :, :, hd]))
                steps.link(dve.tensor_tensor(four(o_sum), sums[:, :, :, 0:hd], four(o_low), ALU.add))
                den = rden[:, :].rearrange("p (t o) -> p t o", o=1).broadcast_to([P, QT, hd])
                dve.wait_ge(head_stored[u], 16 * a + FREE)
                dve.tensor_tensor(o_head[u][:, bass.ds(qb * QT, QT), :], o_sum[:, :, :], den,
                                  ALU.mult).then_inc(block_out, 1)
                assert steps.n == OWN

            for u in range(2):
                dve.memset(k_lc[u][hd:P, :], 0.0).then_inc(zeroed, 1)
            dve.memset(max_cols[:, :, :], 0.0).then_inc(consts, 1)
            dve.memset(shift[:, :], math.log(PROB_SCALE)).then_inc(consts, 1)
            dve.wait_ge(zeroed, 2)
            for u in range(2):
                dve.memset(k_lc[u][hd:hd + 2, :], STAT).then_inc(consts, 1)
            dve.wait_ge(consts, 5)
            for k in range(UNITS):
                reduce_unit(0, k)
            max_to_cols(0, Chain(dve, dve_steps, 0))
            rows_to_q(0, 0, 0)
            for k in range(EARLY):
                reduce_unit(UNITS, k)
            with dve.Fori(0, HEADS // 2) as a:
                for u in range(2):
                    with dve.Fori(0, QB - 1) as qb:
                        attend(a, a * (2 * QB) + u * QB + qb, u, qb, u, (qb + 1) * GT)
                    attend(a, a * (2 * QB) + u * QB + QB - 1, u, QB - 1, 1 - u, 0)


PATCHES = (H // PR) * (W // PC)
MASKED = -1e30


def window(k):
    wr, wc = PR + k - 1, PC + k - 1
    rows = P // wc
    return wr, wc, rows, -(-wr // rows)


def patch_origin(t, k):
    half = k // 2
    r, c = PR * (t // (W // PC)), PC * (t % (W // PC))
    wr, wc, _, _ = window(k)
    return r, c, min(max(r - half, 0), H - wr), min(max(c - half, 0), W - wc)


def neighbour_masks(k):
    wr, wc, _, _ = window(k)
    out = np.full((3, 3, PR, PC, wr, wc), MASKED, np.float32)
    for vr, tr in enumerate((0, 1, H // PR - 1)):
        for vc, tc in enumerate((0, 1, W // PC - 1)):
            r0, c0, kr0, kc0 = patch_origin(tr * (W // PC) + tc, k)
            for r in range(PR):
                a = min(max(r0 + r - k // 2, 0), H - k) - kr0
                for c in range(PC):
                    b = min(max(c0 + c - k // 2, 0), W - k) - kc0
                    out[vr, vc, r, c, a:a + k, b:b + k] = 0.0
    return (out.reshape(9, P, wr * wc).view(np.uint32) >> 16).astype(np.uint16)


def local_attention_phase(nc, name, qk, v, ident, masks, out, heads, k, scale):
    S = H * W
    hd = C // heads
    vw = 2 * hd + 1
    assert 4 * hd == P
    wr, wc, cr, NC = window(k)
    keys, ck = wr * wc, cr * wc
    HG = 4
    NHG = heads // HG
    N = 2 * PATCHES
    SB = 4
    QUADS = N // 4
    PARTS = 4
    TWO = 2
    exp_scale = scale / OPERAND_SCALE ** 2

    def rows_of(ch):
        return min(cr, wr - cr * ch)

    with Phase(nc, name) as ph:
        idt = ph.sb("ident", [P, P])
        idb = ph.sb("identb", [P, P], BF16)
        mask = ph.sb("mask", [P, 9, keys], BF16)
        q4 = [ph.sb(f"q{u}", [P, S], F16) for u in range(2)]
        k4 = [ph.sb(f"k{u}", [P, H, W], F16) for u in range(2)]
        vwin = [ph.sb(f"v{x}", [P, PATCHES * NC, HG * vw], F16) for x in range(NHG)]
        o_head = [ph.sb(f"o{u}", [P, PATCHES, hd]) for u in range(2)]
        neg_max = ph.sb("neg_max", [P, SB])
        bias = ph.sb("bias", [P, SB])
        p32 = [ph.sb(f"p{x}", [P, NC * ck]) for x in range(SB)]
        p_hi = [ph.sb(f"ph{x}", [P, NC * P], F16) for x in range(SB)]
        p_lo = [ph.sb(f"pl{x}", [P, NC * P], F16) for x in range(SB)]
        o_low = [ph.sb(f"o_low{x}", [P, 4, hd]) for x in range(2)]
        o_sum = [ph.sb(f"o_sum{x}", [P, 4, hd]) for x in range(2)]
        rden = [ph.sb(f"rden{x}", [P, 4]) for x in range(2)]
        sc = [ph.ps(f"sc{x}", [P, 512]) for x in range(SB)]
        pt = [ph.ps(f"pt{x}", [P, 512]) for x in range(2)]
        ov = [ph.ps(f"ov{x}", [P, 512]) for x in range(2)]

        consts_in = ph.sem("consts_in")
        consts = ph.sem("consts")
        head_loaded = ph.sems("head_loaded", 2)
        v_loaded = [ph.sems(f"v_loaded{x}_", PARTS) for x in range(NHG)]
        sc_ready = ph.sem("sc_ready")
        max_ready = ph.sem("max_ready")
        bias_ready = ph.sem("bias_ready")
        exp_done = ph.sem("exp_done")
        pt_ready = ph.sem("pt_ready")
        hi_ready = ph.sem("hi_ready")
        lo_ready = ph.sem("lo_ready")
        pv_done = ph.sem("pv_done")
        low_copied = ph.sem("low_copied")
        marker = ph.sem("marker")
        sums_read = ph.sem("sums_read")
        out_ready = ph.sem("out_ready")
        head_stored = ph.sems("head_stored", 2)
        block = ph.block()
        PAIRS = HG // 2
        CONSTS = 1 + SB + NHG

        @block.sync
        def _(sp):
            def load_head(n, u):
                b, h = n // heads % B, n % heads
                toks = slice(b * S, (b + 1) * S)
                flat = lambda x: x[:, :, :].rearrange("p r c -> p (r c)")
                for x in range(2):
                    sp.dma_start(q4[u][2 * hd * x:2 * hd * (x + 1), :],
                                 qk[0, h, :, :, toks].rearrange("s d n -> (s d) n")).then_inc(head_loaded[u], 16)
                for x in range(4):
                    sp.dma_start(flat(k4[u])[hd * x:hd * (x + 1), :],
                                 qk[1, h, x // 2, :, toks]).then_inc(head_loaded[u], 16)

            def load_v(b, x, parts=range(PARTS)):
                img = v[b * S:(b + 1) * S, x * HG * vw:(x + 1) * HG * vw].rearrange("(r c) f -> r c f", c=W)
                for t in range(PATCHES):
                    if t * PARTS // PATCHES not in parts:
                        continue
                    _, _, r0, c0 = patch_origin(t, k)
                    for ch in range(NC):
                        n = rows_of(ch)
                        a = r0 + cr * ch
                        sp.dma_start(vwin[x][0:n * wc, t * NC + ch, :],
                                     img[a:a + n, c0:c0 + wc, :]).then_inc(v_loaded[x][t * PARTS // PATCHES], 16)

            load_head(0, 0)
            sp.dma_start(idt[:, :], ident).then_inc(consts_in, 16)
            sp.dma_start(mask[:, :, :], masks.rearrange("v p n -> p v n").bitcast(BF16)).then_inc(consts_in, 16)
            sp.wait_ge(consts, CONSTS)
            load_v(0, 0)
            load_head(1, 1)
            for n in range(B * heads):
                u = n % 2
                sp.wait_ge(out_ready, (n + 1) * QUADS // 2 + TWO)
                sp.dma_start(out[n // heads, :, :, n % heads * hd:(n % heads + 1) * hd].rearrange("t p f -> p t f"),
                             o_head[u][:, :, :]).then_inc(head_stored[u], 16)
                if n + 2 <= B * heads:
                    load_head(n + 2, u)
                for half in range(2):
                    last = n - half
                    parts = range(half * PARTS // 2, (half + 1) * PARTS // 2)
                    if last == 0:
                        for x in range(1, NHG):
                            load_v(0, x, parts)
                    elif last > 0 and (last + 1) % HG == 0 and last + 1 + heads - HG < B * heads:
                        load_v(last // heads + 1, last % heads // HG, parts)
            for u in range(2):
                sp.wait_ge(head_stored[u], 16 * (B * heads // 2) + FREE)

        def bodies(eng):
            with eng.Fori(0, B) as b:
                for x in range(NHG):
                    with eng.Fori(0, PAIRS) as a:
                        yield b * (NHG * PAIRS) + x * PAIRS + a, b, x, a

        @block.tensor
        def _(pe):
            pe.wait_ge(consts_in, 32)
            pe.wait_ge(consts, CONSTS)

            def scores(pair, n):
                u, t = n // PATCHES, n % PATCHES
                if t == 0:
                    pe.wait_ge(head_loaded[u], 96 * (pair + 1))
                pe.wait_ge(exp_done, pair * N + n + 1)
                r, c, kr, kc = patch_origin(t, k)
                vr = 0 if r == 0 else 2 if r == H - PR else 1
                vc = 0 if c == 0 else 2 if c == W - PC else 1
                dst = sc[n % SB][:, 0:keys]
                pe.matmul(dst, q4[u][:, t * P:(t + 1) * P], k4[u][:, kr:kr + wr, kc:kc + wc],
                          start=True, stop=False)
                pe.matmul(dst, idb[:, :], mask[:, 3 * vr + vc, :], start=False, stop=True).then_inc(sc_ready, 1)

            def turn(pair, n):
                pe.wait_ge(exp_done, pair * N + n + 1 + SB)
                pe.wait_ge(lo_ready, pair * N + n - 1 + TWO)
                for ch in range(NC):
                    last = pe.transpose(pt[n % 2][0:ck, ch * P:(ch + 1) * P], p32[n % SB][:, ch * ck:(ch + 1) * ck],
                                        idt[:, :])
                last.then_inc(pt_ready, 1)

            def values(pair, n, b, x, a):
                u, t = n // PATCHES, n % PATCHES
                if t % (PATCHES // PARTS) == 0:
                    pe.wait_ge(v_loaded[x][t * PARTS // PATCHES], 16 * PATCHES * NC // PARTS * (b + 1))
                pe.wait_ge(lo_ready, pair * N + n + 1 + TWO)
                quad = n // 4
                if n % 4 == 0:
                    pe.wait_ge(sums_read, pair * QUADS + quad - 1 + TWO)
                o = ov[quad % 2][:, (n % 4) * vw:(n % 4 + 1) * vw]
                for ch in range(NC):
                    vv = vwin[x][0:ck, t * NC + ch, bass.ds(a * (2 * vw) + u * vw, vw)]
                    first = n % 4 == 0 and ch == 0
                    pe.matmul(o, p_hi[n % SB][0:ck, ch * P:(ch + 1) * P], vv,
                              start=first, stop=(ch == NC - 1), skip_group_check=True)
                    vv = vwin[x][0:ck, t * NC + ch, bass.ds(a * (2 * vw) + u * vw, hd + 1)]
                    last = pe.matmul(o[:, 0:hd + 1], p_lo[n % SB][0:ck, ch * P:(ch + 1) * P], vv,
                                     start=False, stop=(ch == NC - 1), skip_group_check=True)
                if n % 4 == 3:
                    last.then_inc(pv_done, 1)

            for n in range(3):
                scores(0, n)
            for pair, b, x, a in bodies(pe):
                for s in range(N + 2):
                    if s + 3 < N:
                        scores(pair, s + 3)
                    elif s < N:
                        scores(pair + 1, s + 3 - N)
                    if s < N:
                        turn(pair, s)
                    if s >= 2:
                        values(pair, s - 2, b, x, a)

        @block.scalar
        def _(act):
            act.sem_inc(exp_done, SB)
            act.wait_ge(consts_in, 32)
            act.activation(idb[:, :], idt[:, :], ACT.Copy).then_inc(consts, 1)
            for pair, b, x, a in bodies(act):
                for s in range(N + 3):
                    if s < N:
                        act.wait_ge(bias_ready, pair * N + s + 1)
                        act.activation(p32[s % SB][:, 0:keys], sc[s % SB][:, 0:keys], ACT.Exp,
                                       bias=bias[:, s % SB:s % SB + 1], scale=exp_scale).then_inc(exp_done, 1)
                    if 1 <= s <= N:
                        m = s - 1
                        act.wait_ge(pt_ready, pair * N + m + 1)
                        act.activation(p_hi[m % SB][0:ck, :], pt[m % 2][0:ck, 0:NC * P], ACT.Copy).then_inc(hi_ready, 1)
                    if s >= 6 and s % 4 == 2:
                        quad = s // 4 - 1
                        act.wait_ge(pv_done, pair * QUADS + quad + 1)
                        sums = ov[quad % 2][:, 0:4 * vw].rearrange("p (t f) -> p t f", f=vw)
                        act.activation(o_low[quad % 2][:, :, :], sums[:, :, hd + 1:vw], ACT.Copy).then_inc(low_copied, 1)

        @block.vector
        def _(dve):
            dve.sem_inc(lo_ready, TWO)
            dve.sem_inc(sums_read, TWO)
            for x in range(NHG):
                dve.memset(vwin[x][:, NC - 1:PATCHES * NC:NC, :], 0.0).then_inc(consts, 1)
            for x in range(SB):
                dve.memset(p32[x][:, :], 0.0).then_inc(consts, 1)
            dve.wait_ge(consts, CONSTS)

            def maxima(pair, n):
                dve.wait_ge(sc_ready, pair * N + n + 1)
                dve.tensor_reduce(neg_max[:, n % SB:n % SB + 1], sc[n % SB][:, 0:keys], AX.X, ALU.max,
                                  negate=True).then_inc(max_ready, 1)

            def low(pair, n):
                dve.wait_ge(hi_ready, pair * N + n + 1)
                dve.tensor_tensor(p_lo[n % SB][0:ck, :], pt[n % 2][0:ck, 0:NC * P], p_hi[n % SB][0:ck, :],
                                  ALU.subtract).then_inc(lo_ready, 1)

            def add_up(pair, quad):
                x = quad % 2
                sums = ov[x][:, 0:4 * vw].rearrange("p (t f) -> p t f", f=vw)
                dve.wait_ge(out_ready, pair * QUADS + quad - 1 + TWO)
                dve.wait_ge(low_copied, pair * QUADS + quad + 1)
                dve.reciprocal(rden[x][:, :], sums[:, :, hd])
                dve.tensor_tensor(o_sum[x][:, :, :], sums[:, :, 0:hd], o_low[x][:, :, :],
                                  ALU.add).then_inc(sums_read, 1)

            for n in range(2):
                maxima(0, n)
            for pair, b, x, a in bodies(dve):
                for s in range(N + 3):
                    if s + 2 < N:
                        maxima(pair, s + 2)
                    elif s < N:
                        maxima(pair + 1, s + 2 - N)
                    if 1 <= s <= N:
                        low(pair, s - 1)
                    if s >= 6 and s % 4 == 2:
                        add_up(pair, s // 4 - 1)

        @block.gpsimd
        def _(pool):
            pool.sem_inc(out_ready, TWO)
            for u in range(2):
                pool.sem_inc(head_stored[u], FREE)

            def biases(pair, n):
                pool.wait_ge(max_ready, pair * N + n + 1)
                passed(pool, marker)
                pool.tensor_scalar(bias[:, n % SB:n % SB + 1], neg_max[:, n % SB:n % SB + 1], exp_scale,
                                   math.log(PROB_SCALE), ALU.mult, ALU.add).then_inc(bias_ready, 1)

            def normalise(pair, quad):
                u, x, t = quad // (QUADS // 2), quad % 2, quad * 4 % PATCHES
                pool.wait_ge(sums_read, pair * QUADS + quad + 1 + TWO)
                if t == 0:
                    pool.wait_ge(head_stored[u], 16 * pair + FREE)
                den = rden[x][:, :].rearrange("p (t o) -> p t o", o=1).broadcast_to([P, 4, hd])
                pool.tensor_tensor(o_head[u][:, t:t + 4, :], o_sum[x][:, :, :], den,
                                   ALU.mult).then_inc(out_ready, 1)

            for n in range(2):
                biases(0, n)
            for pair, b, x, a in bodies(pool):
                for s in range(N + 3):
                    if s + 2 < N:
                        biases(pair, s + 2)
                    elif s < N:
                        biases(pair + 1, s + 2 - N)
                    if s >= 7 and s % 4 == 3:
                        normalise(pair, s // 4 - 1)
                normalise(pair, QUADS - 1)


def tail_phase(nc, name, kind, att, x, ident, w_proj, b_proj, out, patches,
               gamma=None, beta=None, w1=None, b1=None, w2=None, b2=None):
    mlp = kind != "none"
    FT = w1.shape[1] // P if mlp else 0
    TURN_AT = 0
    FIRST = kind == "arsinh"
    with Phase(nc, name) as ph:
        idt = ph.sb("ident", [P, P])
        wp = ph.sb("wp", [P, CH, C])
        bp = ph.sb("bp", [P, C])
        a_in = [ph.sb(f"a{u}", [P, TPG, C]) for u in range(2)]
        x_in = [ph.sb(f"x{u}", [P, TPG, C]) for u in range(2)]
        res = ph.sb("res", [P, TPG, C])
        y = [ph.sb(f"y{u}", [P, TPG, C]) for u in range(2)]
        aT = ph.sb("aT", [P, CH, GT])
        xn = ph.sb("xn", [P, TPG, C])
        aux = ph.sb("aux", [P, TPG, C])
        root = ph.sb("root", [P, TPG, C])
        res2 = ph.sb("res2", [P, TPG, C])
        stats = ph.sb("stats", [P, TPG, 6])
        mv = ph.sb("mv", [P, TPG, 2])
        std = ph.sb("std", [P, TPG])
        rstd = ph.sb("rstd", [P, TPG])
        eps = ph.sb("eps", [P, 1])
        tp = [ph.ps(f"tp{c}", [P, GT]) for c in range(CH)]
        pp = [ph.ps(f"pp{c}", [P, 512]) for c in range(2)]
        op = [ph.ps(f"op{c}", [P, 512]) for c in range(2)]
        fp = [ph.ps(f"fp{c}", [P, 512]) for c in range(2)]
        if mlp:
            gcol, bcol = ph.sb("gamma", [P, CH]), ph.sb("beta", [P, CH])
            w1s, b1s = ph.sb("w1", [P, CH, FT * P]), ph.sb("b1", [P, FT])
            w2s, b2s = ph.sb("w2", [P, FT, C]), ph.sb("b2", [P, C])
            w1_hi, w1_lo = (ph.sb(f"w1_{x}", [P, CH, FT * P], F16) for x in ("hi", "lo"))
            xT = ph.sb("xT", [P, CH, GT])
            xT_hi, xT_lo = (ph.sb(f"xT_{x}", [P, CH, GT], F16) for x in ("hi", "lo"))
            hT = ph.sb("hT", [P, FT, GT])

        proj_in = ph.sem("proj_in")
        weights_in = ph.sem("weights_in")
        consts = ph.sem("consts")
        scaled = ph.sem("scaled")
        w1_split = ph.sem("w1_split")
        xt_lo = ph.sem("xt_lo")
        loaded = ph.sems("loaded", 2)
        a_turned = ph.sem("a_turned")
        at_ready = ph.sem("at_ready")
        proj_ready = ph.sem("proj_ready")
        res_ready = ph.sem("res_ready")
        y_ready = ph.sem("y_ready")
        dve_steps = ph.sem("dve_steps")
        act_steps = ph.sem("act_steps")
        marker = ph.sem("marker")
        var_ready = ph.sem("var_ready")
        std_ready = ph.sem("std_ready")
        square_ready = ph.sem("square_ready")
        root_ready = ph.sem("root_ready")
        sum_ready = ph.sem("sum_ready")
        log_ready = ph.sem("log_ready")
        xn_ready = ph.sem("xn_ready")
        x_turned = ph.sem("x_turned")
        xt_ready = ph.sem("xt_ready")
        fc1_ready = ph.sem("fc1_ready")
        h_ready = ph.sem("h_ready")
        fc2_ready = ph.sem("fc2_ready")
        res2_ready = ph.sem("res2_ready")
        out_ready = ph.sem("out_ready")
        stored = ph.sems("stored", 2)
        block = ph.block()

        proj_loads = [(idt[:, :], ident), (wp[:, :, :], w_proj.rearrange("(c p) n -> p c n", p=P)),
                      (bp[:, :], row(b_proj))]
        loads = []
        if mlp:
            loads += [(gcol[:, :], gamma), (bcol[:, :], beta), (w1s[:, :, :], w1.rearrange("(c p) n -> p c n", p=P)),
                      (b1s[:, :], b1), (w2s[:, :, :], w2.rearrange("(c p) n -> p c n", p=P)), (b2s[:, :], row(b2))]
        n_x = TPG if patches else 1

        def token_parts(dram, g, tile):
            if not patches:
                return [(dram[bass.ds(g * GT, GT)].rearrange("(t p) c -> p t c", p=P), tile[:, :, :])]
            band = dram.rearrange("(g r t c) f -> g r t c f", r=PR, t=TPG, c=PC)[bass.ds(g, 1)]
            return [(band[:, :, t, :, :].rearrange("g r c f -> (g r) c f"), tile[:, t, :]) for t in range(TPG)]

        @block.sync
        def _(sp):
            def load(g, u):
                if patches:
                    src = att.rearrange("b t p f -> (b t) p f")[bass.ds(g * TPG, TPG)].rearrange("t p f -> p t f")
                else:
                    src = att[bass.ds(g * GT, GT)].rearrange("(t p) c -> p t c", p=P)
                sp.dma_start(a_in[u][:, :, :], src).then_inc(loaded[u], 16)
                for dram, tile in token_parts(x, g, x_in[u]):
                    sp.dma_start(tile, dram).then_inc(loaded[u], 16)

            def store(g, u):
                sp.wait_ge(out_ready, g + 1 + FREE)
                for dram, tile in token_parts(out, g, y[u]):
                    sp.dma_start(dram, tile).then_inc(stored[u], 16)

            load(0, 0)
            for dst, src in proj_loads:
                sp.dma_start(dst, src).then_inc(proj_in, 16)
            load(1, 1)
            for dst, src in loads:
                sp.dma_start(dst, src).then_inc(weights_in, 16)
            with sp.Fori(0, GROUPS // 2 - 1) as i:
                for u in range(2):
                    g = 2 * i + u
                    sp.wait_ge(a_turned, CH * (g + 1))
                    sp.wait_ge(res_ready, g + 1)
                    load(g + 2, u)
                    store(g, u)
            for u in range(2):
                store(GROUPS - 2 + u, u)
            for u in range(2):
                sp.wait_ge(stored[u], 16 * n_x * (GROUPS // 2) + FREE)

        def groups(eng):
            with eng.Fori(0, GROUPS // 2 - 1) as i:
                for u in range(2):
                    yield i, u, True
            for u in range(2):
                yield GROUPS // 2 - 1, u, u == 0

        @block.gpsimd
        def _(pool):
            def add_bias(dst, src, bias, done):
                pool.tensor_tensor(dst[:, :, :], src[:, :, :],
                                   bias[:, :].rearrange("p (o c) -> p o c", o=1).broadcast_to([P, TPG, C]),
                                   ALU.add).then_inc(done, 1)

            def residual(i, u):
                pool.wait_ge(loaded[u], 16 * (1 + n_x) * (i + 1))
                pool.wait_ge(y_ready, 2 * i + u + FREE)
                add_bias(res, x_in[u], bp, res_ready)

            pool.wait_ge(proj_in, 16 * len(proj_loads))
            pool.memset(eps[:, :], LN_EPS).then_inc(consts, 1)
            residual(0, 0)
            if mlp:
                pool.wait_ge(weights_in, 16 * len(loads))
            for i, u, more in groups(pool):
                if more:
                    residual(i + u, 1 - u)
                if mlp:
                    for c in range(CH):
                        pool.wait_ge(xt_ready, CH * (2 * i + u) + c + 1)
                        pool.tensor_tensor(xT_lo[:, c, :], xT[:, c, :], xT_hi[:, c, :],
                                           ALU.subtract).then_inc(xt_lo, 1)
                if mlp:
                    pool.wait_ge(y_ready, 2 * i + u + 1 + FREE)
                    pool.wait_ge(out_ready, 2 * i + u + FREE)
                    add_bias(res2, y[u], b2s, res2_ready)

        @block.tensor
        def _(pe):
            pe.wait_ge(proj_in, 16 * len(proj_loads))

            def turn(src, done):
                for c in range(CH):
                    for t in range(TPG):
                        last = pe.transpose(tp[c][:, t * P:(t + 1) * P], src[:, t, c * P:(c + 1) * P], idt[:, :])
                    last.then_inc(done, 1)

            def token_major(half, banks, lhs, w, tiles, done, before_last=None):
                for t in range(2):
                    tt = 2 * half + t
                    for c in range(tiles):
                        if before_last is not None and t == 0 and c == tiles - 1:
                            pe.wait_ge(h_ready, before_last)
                        last = pe.matmul(banks[half][:, t * C:(t + 1) * C], lhs[:, c, tt * P:(tt + 1) * P],
                                         w[:, c, :], start=(c == 0), stop=(c == tiles - 1))
                last.then_inc(done, 1)

            def turn_norm(g):
                pe.wait_ge(xn_ready, g + 1)
                turn(xn, x_turned)

            def turn_in(i, u):
                pe.wait_ge(loaded[u], 16 * (1 + n_x) * (i + 1))
                if not mlp:
                    pe.wait_ge(at_ready, CH * (2 * i + u) + FREE)
                turn(a_in[u], a_turned)

            def project(i, u):
                pe.wait_ge(at_ready, CH * (2 * i + u + 1) + (0 if mlp else FREE))
                pe.wait_ge(y_ready, 2 * i + u + FREE)
                for half in range(2):
                    token_major(half, pp, aT, wp, CH, proj_ready)

            HH, HL, LH = ((0, 0), (0, 1), (1, 0))
            passes = [(*parts, c) for parts in (HH, HL, LH) for c in range(CH)]
            turn_in(0, 0)
            project(0, 0)
            if mlp:
                pe.wait_ge(weights_in, 16 * len(loads))
                pe.wait_ge(w1_split, 2)
                if not FIRST:
                    turn_norm(0)
            for i, u, more in groups(pe):
                g = 2 * i + u
                if FIRST:
                    if more:
                        turn_in(i + u, 1 - u)
                        pe.wait_ge(at_ready, CH * (g + 2))
                    turn_norm(g)
                    if more:
                        project(i + u, 1 - u)
                if mlp:
                    pe.wait_ge(xt_ready, CH * (g + 1))
                for m in range(FT):
                    if m >= 2:
                        pe.wait_ge(h_ready, FT * g + m - 1)
                    for n, (xp, wp1, c) in enumerate(passes):
                        if m == 0 and n == passes.index((*LH, 0)):
                            pe.wait_ge(xt_lo, CH * (g + 1))
                        last = pe.matmul(fp[m % 2][:, :], (w1_hi, w1_lo)[wp1][:, c, m * P:(m + 1) * P],
                                         (xT_hi, xT_lo)[xp][:, c, :], start=(n == 0), stop=(n == len(passes) - 1))
                    last.then_inc(fc1_ready, 1)
                    if more and m == TURN_AT and not FIRST:
                        turn_in(i + u, 1 - u)
                    if more and m == TURN_AT + 1 and not FIRST:
                        project(i + u, 1 - u)
                if mlp:
                    pe.wait_ge(h_ready, FT * (g + 1) - 1)
                    pe.wait_ge(out_ready, g + FREE)
                    token_major(0, op, hT, w2s, FT, fc2_ready, before_last=FT * (g + 1))
                    if more and not FIRST:
                        turn_norm(g + 1)
                    token_major(1, op, hT, w2s, FT, fc2_ready)
                elif more:
                    turn_in(i + u, 1 - u)
                    project(i + u, 1 - u)

        @block.scalar
        def _(act):
            def copy_in(i, u):
                for c in range(CH):
                    act.wait_ge(a_turned, CH * (2 * i + u) + c + 1)
                    act.activation(aT[:, c, :], tp[c][:, :], ACT.Copy).then_inc(at_ready, 1)

            def norm(i, u):
                g = 2 * i + u
                if kind == "layer":
                    act.wait_ge(var_ready, g + 1)
                    act.activation(std[:, :], mv[:, :, 1], ACT.Sqrt, bias=eps[:, :]).then_inc(std_ready, 1)
                elif kind == "arsinh":
                    steps = Chain(act, act_steps, g)
                    act.wait_ge(square_ready, g + 1)
                    act.activation(root[:, :, :], root[:, :, :], ACT.Sqrt, bias=1.0).then_inc(root_ready, 1)
                    act.wait_ge(sum_ready, g + 1)
                    steps.link(act.activation(aux[:, :, :], aux[:, :, :], ACT.Ln))
                    act.activation(root[:, :, :], y[u][:, :, :], ACT.Sign).then_inc(log_ready, 1)

            if not mlp:
                act.sem_inc(at_ready, FREE)
            act.wait_ge(consts, 1)
            copy_in(0, 0)
            norm(0, 0)
            if mlp:
                act.wait_ge(weights_in, 16 * len(loads))
                act.mul(gcol[:, :], gcol[:, :], OPERAND_SCALE).then_inc(scaled, 1)
                act.mul(bcol[:, :], bcol[:, :], OPERAND_SCALE).then_inc(scaled, 1)
                act.wait_ge(scaled, 2)
            for i, u, more in groups(act):
                g = 2 * i + u
                if more and FIRST:
                    copy_in(i + u, 1 - u)
                if mlp:
                    for c in range(CH):
                        act.wait_ge(x_turned, CH * g + c + 1)
                        for dst in (xT, xT_hi):
                            last = act.activation(dst[:, c, :], tp[c][:, :], ACT.Identity, bias=bcol[:, c:c + 1],
                                                  scale=gcol[:, c:c + 1])
                        last.then_inc(xt_ready, 1)
                for m in range(FT):
                    act.wait_ge(fc1_ready, FT * g + m + 1)
                    act.activation(hT[:, m, :], fp[m % 2][:, :], ACT.Gelu, bias=b1s[:, m:m + 1],
                                   scale=1 / (OPERAND_SCALE * WEIGHT_SCALE)).then_inc(h_ready, 1)
                    if more and m == TURN_AT and not FIRST:
                        copy_in(i + u, 1 - u)
                if more and mlp:
                    norm(i + u, 1 - u)
                elif more:
                    copy_in(i + u, 1 - u)

        @block.vector
        def _(dve):
            dve.sem_inc(y_ready, FREE)
            dve.sem_inc(out_ready, FREE)
            for u in range(2):
                dve.sem_inc(stored[u], FREE)
            own = {"layer": 2, "arsinh": 1, "none": 0}[kind]
            flat = lambda x, half: x[:, 2 * half:2 * half + 2, :].rearrange("p t c -> p (t c)")

            def first_stage(i, u):
                g = 2 * i + u
                steps = Chain(dve, dve_steps, own * g)
                dve.wait_ge(stored[u], 16 * n_x * i + FREE)
                dve.wait_ge(res_ready, g + 1)
                for half in range(2):
                    dve.wait_ge(proj_ready, 2 * g + half + 1)
                    last = dve.tensor_tensor(flat(y[u], half), pp[half][:, :], flat(res, half), ALU.add)
                last.then_inc(y_ready, 1)
                dve.wait_ge(y_ready, g + 1 + FREE)
                if kind == "none":
                    dve.sem_inc(out_ready, 1)
                    return
                if kind == "layer":
                    for t in range(TPG):
                        last = dve.bn_stats(stats[:, t, :], y[u][:, t, :])
                    steps.link(last)
                    passed(dve, marker)
                    for t in range(TPG):
                        last = dve.bn_aggr(mv[:, t, :], stats[:, t, :])
                    last.then_inc(var_ready, 1)
                    dve.wait_ge(var_ready, g + 1)
                    dve.wait_ge(std_ready, g + 1)
                    steps.link(dve.reciprocal(rstd[:, :], std[:, :]))
                    for t in range(TPG):
                        last = dve.tensor_scalar(xn[:, t, :], y[u][:, t, :], mv[:, t, 0:1], rstd[:, t:t + 1],
                                                 ALU.subtract, ALU.mult)
                else:
                    dve.tensor_tensor(root[:, :, :], y[u][:, :, :], y[u][:, :, :], ALU.mult).then_inc(square_ready, 1)
                    steps.link(dve.scalar_tensor_tensor(aux[:, :, :], y[u][:, :, :], -1.0, y[u][:, :, :],
                                                        ALU.mult, ALU.max))
                    dve.wait_ge(root_ready, g + 1)
                    dve.tensor_tensor(aux[:, :, :], aux[:, :, :], root[:, :, :], ALU.add).then_inc(sum_ready, 1)
                    dve.wait_ge(log_ready, g + 1)
                    last = dve.tensor_tensor(xn[:, :, :], aux[:, :, :], root[:, :, :], ALU.mult)
                last.then_inc(xn_ready, 1)
                assert steps.n == own

            first_stage(0, 0)
            if mlp:
                dve.wait_ge(weights_in, 16 * len(loads))
                dve.tensor_scalar(w1_hi[:, :, :], w1s[:, :, :], WEIGHT_SCALE, None, ALU.mult).then_inc(w1_split, 1)
                dve.wait_ge(w1_split, 1)
                dve.scalar_tensor_tensor(w1_lo[:, :, :], w1s[:, :, :], WEIGHT_SCALE, w1_hi[:, :, :],
                                         ALU.mult, ALU.subtract).then_inc(w1_split, 1)
            for i, u, more in groups(dve):
                g = 2 * i + u
                if more:
                    first_stage(i + u, 1 - u)
                if not mlp:
                    continue
                dve.wait_ge(res2_ready, g + 1)
                for half in range(2):
                    dve.wait_ge(fc2_ready, 2 * g + half + 1)
                    last = dve.tensor_tensor(flat(y[u], half), op[half][:, :], flat(res2, half), ALU.add)
                last.then_inc(out_ready, 1)


GN_GROUPS = 8


def group_stats_phase(nc, name, x, ident, ones_blocks, scale, bias, affine):
    PER = GROUPS // B
    with Phase(nc, name) as ph:
        idt = ph.sb("ident", [P, P])
        ones = ph.sb("ones", [P, P])
        sc = ph.sb("scale", [P, CH])
        bi = ph.sb("bias", [P, CH])
        x_in = [ph.sb(f"x{u}", [P, TPG, C]) for u in range(2)]
        stats = ph.sb("stats", [P, B, CH, PER, 6])
        mv = ph.sb("mv", [P, B, CH, 2])
        mean = ph.sb("mean", [P, B, CH])
        dev = ph.sb("dev", [P, B, CH])
        var = ph.sb("var", [P, B, CH])
        eps = ph.sb("eps", [P, 1])
        ab = ph.sb("ab", [P, B, 2, CH])
        ab_rows = ph.sb("ab_rows", [B * 2 * CH, P])
        tmp = ph.sb("tmp", [P, B, CH])
        tp = [ph.ps(f"tp{c}", [P, GT]) for c in range(2 * CH)]
        sums = ph.ps("sums", [P, 512])

        consts_in = ph.sem("consts_in")
        consts = ph.sem("consts")
        loaded = ph.sems("loaded", 2)
        turned = ph.sem("turned")
        counted = ph.sem("counted")
        steps_done = ph.sem("steps_done")
        to_sum = ph.sem("to_sum")
        summed = ph.sem("summed")
        std_ready = ph.sem("std_ready")
        ab_ready = ph.sem("ab_ready")
        ab_turned = ph.sem("ab_turned")
        rows_ready = ph.sem("rows_ready")
        stored = ph.sem("stored")
        block = ph.block()

        @block.sync
        def _(sp):
            for dst, src in ((idt[:, :], ident), (ones[:, :], ones_blocks), (sc[:, :], scale), (bi[:, :], bias)):
                sp.dma_start(dst, src).then_inc(consts_in, 16)
            for g in range(GROUPS):
                u = g % 2
                if g >= 2:
                    sp.wait_ge(turned, CH * (g - 1))
                sp.dma_start(x_in[u][:, :, :], x[g * GT:(g + 1) * GT].rearrange("(t p) c -> p t c", p=P)).then_inc(loaded[u], 16)
            sp.wait_ge(rows_ready, 1)
            rows = 2 * CH
            for g in range(GROUPS):
                b = g // PER
                sp.dma_start(affine[g].rearrange("k (c p) -> (k c) p", p=P),
                             ab_rows[b * rows:(b + 1) * rows, :]).then_inc(stored, 16)
            sp.wait_ge(stored, 16 * GROUPS)

        @block.gpsimd
        def _(pool):
            pool.memset(eps[:, :], LN_EPS).then_inc(consts, 1)

        @block.tensor
        def _(pe):
            pe.wait_ge(consts_in, 64)
            for g in range(GROUPS):
                u = g % 2
                pe.wait_ge(loaded[u], 16 * (g // 2 + 1))
                if g >= 2:
                    pe.wait_ge(counted, CH * (g - 1))
                for c in range(CH):
                    for t in range(TPG):
                        last = pe.transpose(tp[CH * u + c][:, t * P:(t + 1) * P], x_in[u][:, t, c * P:(c + 1) * P], idt[:, :])
                    last.then_inc(turned, 1)
            n = B * CH
            flat = lambda v: v[:, :, :].rearrange("p b c -> p (b c)")
            for k, src in enumerate((mean, dev)):
                pe.wait_ge(to_sum, k + 1)
                pe.matmul(sums[:, k * n:(k + 1) * n], ones[:, :], flat(src), start=True, stop=True).then_inc(summed, 1)
            pe.wait_ge(ab_ready, 1)
            pe.transpose(sums[0:2 * n, P:2 * P], ab[:, :, :, :].rearrange("p b k c -> p (b k c)"),
                         idt[:, :]).then_inc(ab_turned, 1)

        @block.scalar
        def _(act):
            act.wait_ge(consts, 1)
            act.wait_ge(to_sum, 3)
            act.activation(var[:, :, :], var[:, :, :], ACT.Sqrt, bias=eps[:, :]).then_inc(std_ready, 1)

        @block.vector
        def _(dve):
            steps = Chain(dve, steps_done)
            dve.wait_ge(consts_in, 64)
            for g in range(GROUPS):
                for c in range(CH):
                    dve.wait_ge(turned, CH * g + c + 1)
                    dve.bn_stats(stats[:, g // PER, c, g % PER, :], tp[CH * (g % 2) + c][:, :]).then_inc(counted, 1)
            dve.wait_ge(counted, CH * GROUPS)
            for b in range(B):
                for c in range(CH):
                    steps.step(dve.bn_aggr(mv[:, b, c, :], stats[:, b, c, :, :]))
            steps.settle()
            n = B * CH
            shaped = lambda k: sums[:, k * n:(k + 1) * n].rearrange("p (b c) -> p b c", b=B)
            dve.tensor_copy(mean[:, :, :], mv[:, :, :, 0]).then_inc(to_sum, 1)
            dve.wait_ge(summed, 1)
            steps.link(dve.tensor_copy(mean[:, :, :], shaped(0)))
            steps.link(dve.tensor_tensor(dev[:, :, :], mv[:, :, :, 0], mean[:, :, :], ALU.subtract))
            steps.link(dve.tensor_tensor(dev[:, :, :], dev[:, :, :], dev[:, :, :], ALU.mult))
            dve.tensor_tensor(dev[:, :, :], dev[:, :, :], mv[:, :, :, 1], ALU.add).then_inc(to_sum, 1)
            dve.wait_ge(summed, 2)
            dve.tensor_copy(var[:, :, :], shaped(1)).then_inc(to_sum, 1)
            dve.wait_ge(std_ready, 1)
            steps.link(dve.reciprocal(tmp[:, :, :], var[:, :, :]))
            scales = sc[:, :].rearrange("p (o c) -> p o c", o=1).broadcast_to([P, B, CH])
            biases = bi[:, :].rearrange("p (o c) -> p o c", o=1).broadcast_to([P, B, CH])
            steps.link(dve.tensor_tensor(ab[:, :, 0, :], tmp[:, :, :], scales, ALU.mult))
            steps.link(dve.tensor_tensor(tmp[:, :, :], mean[:, :, :], ab[:, :, 0, :], ALU.mult))
            dve.tensor_tensor(ab[:, :, 1, :], biases, tmp[:, :, :], ALU.subtract).then_inc(ab_ready, 1)
            dve.wait_ge(ab_turned, 1)
            dve.tensor_copy(ab_rows[:, :], sums[0:2 * n, P:2 * P]).then_inc(rows_ready, 1)


NF = 33
U0 = H - NF
SHRINK = 0.01
FEW = 4


def fourier_matrices():
    n = np.arange(64)
    v = np.arange(NF)
    phase = 2 * np.pi * np.outer(n, v) / W
    fwd = np.concatenate([np.cos(phase), -np.sin(phase[:, 1:NF - 1])], 1) / 8
    twice = np.where((v == 0) | (v == NF - 1), 1.0, 2.0)
    inv = np.concatenate([twice * np.cos(phase), -(twice * np.sin(phase))[:, 1:NF - 1]], 1).T / 8
    both = lambda m: np.kron(np.eye(B), m).astype(np.float32)
    ph = 2 * np.pi * np.outer(n, U0 + v) / H
    c, s = np.cos(ph) / 8, np.sin(ph) / 8
    fwd_h = np.block([[c, -s], [s, c]]).astype(np.float32)
    inv_h = np.block([[c.T, s.T], [-s.T, c.T]]).astype(np.float32)
    return both(fwd), both(inv), fwd_h, inv_h


def block_diagonal(w1, w2):
    n = P // 32
    out = np.zeros((2, 2, CH, n, 32, n, 32), np.float32)
    for layer, w in enumerate((w1, w2)):
        blocks = np.asarray(w).reshape(2, CH, n, 32, 32)
        for k in range(n):
            out[layer, :, :, k, :, k, :] = blocks[:, :, k]
    return out.reshape(2, 2, CH, P, P)


def mix_biases(b1, b2):
    cols = [np.asarray(b).reshape(2, CH, P).transpose(2, 0, 1).reshape(P, 2 * CH) for b in (b1, b2)]
    return np.stack(cols)


def w_transform_phase(nc, name, x, matrix, out, residual=None):
    inverse = residual is not None
    STEPS = H // FEW
    with Phase(nc, name) as ph:
        m = ph.sb("m", [P, P])
        x_in = [ph.sb(f"x{u}", [P, FEW, C]) for u in range(2)]
        r_in = [ph.sb(f"r{u}", [P, FEW, C]) for u in range(2)]
        y = [ph.sb(f"y{u}", [P, FEW, C]) for u in range(2)]
        pr = [ph.ps(f"p{k}", [P, 512]) for k in range(4)]
        m_loaded = ph.sem("m_loaded")
        loaded = ph.sems("loaded", 2)
        done = ph.sem("done")
        copied = ph.sem("copied")
        stored = ph.sems("stored", 2)
        block = ph.block()
        per = 16 * (1 + B if inverse else B)
        n_out = B if inverse else 1

        def lines(ap, i, u, b):
            return ap.rearrange("b (s n) w c -> b s w n c", n=FEW)[b:b + 1, bass.ds(2 * i + u, 1)].rearrange("b s w n c -> (b s w) n c")

        def packed(ap, i, u):
            return ap.rearrange("b k (s n) c -> (b k) s n c", n=FEW)[:, bass.ds(2 * i + u, 1)].rearrange("p s n c -> p (s n) c")

        @block.sync
        def _(sp):
            def load(i, u):
                if inverse:
                    sp.dma_start(x_in[u][:, :, :], packed(x, i, u)).then_inc(loaded[u], 16)
                for b in range(B):
                    dst = (r_in if inverse else x_in)[u][b * W:(b + 1) * W, :, :]
                    sp.dma_start(dst, lines(residual if inverse else x, i, u, b)).then_inc(loaded[u], 16)

            def store(i, u):
                sp.wait_ge(copied, 2 * (2 * i + u) + 2)
                if inverse:
                    for b in range(B):
                        sp.dma_start(lines(out, i, u, b), y[u][b * W:(b + 1) * W, :, :]).then_inc(stored[u], 16)
                else:
                    sp.dma_start(packed(out, i, u), y[u][:, :, :]).then_inc(stored[u], 16)

            sp.dma_start(m[:, :], matrix).then_inc(m_loaded, 16)
            for u in range(2):
                load(0, u)
            with sp.Fori(0, STEPS // 2 - 1) as i:
                for u in range(2):
                    store(i, u)
                    load(i + 1, u)
            for u in range(2):
                store(STEPS // 2 - 1, u)
            for u in range(2):
                sp.wait_ge(stored[u], 16 * n_out * (STEPS // 2) + FREE)

        @block.tensor
        def _(pe):
            pe.wait_ge(m_loaded, 16)
            with pe.Fori(0, STEPS // 2) as i:
                for u in range(2):
                    pe.wait_ge(loaded[u], per * (i + 1))
                    for k in range(2):
                        pe.matmul(pr[2 * u + k][:, :], m[:, :], x_in[u][:, 2 * k:2 * k + 2, :].rearrange("p n c -> p (n c)"),
                                  start=True, stop=True).then_inc(done, 1)

        @block.vector
        def _(dve):
            for u in range(2):
                dve.sem_inc(stored[u], FREE)
            with dve.Fori(0, STEPS // 2) as i:
                for u in range(2):
                    dve.wait_ge(stored[u], 16 * n_out * i + FREE)
                    for k in range(2):
                        part = lambda t: t[u][:, 2 * k:2 * k + 2, :].rearrange("p n c -> p (n c)")
                        dve.wait_ge(done, 2 * (2 * i + u) + k + 1)
                        if inverse:
                            ins = dve.tensor_tensor(part(y), pr[2 * u + k][:, :], part(r_in), ALU.add)
                        else:
                            ins = dve.tensor_copy(part(y), pr[2 * u + k][:, :])
                        ins.then_inc(copied, 1)


def frequency_phase(nc, name, a, ident, fwd_h, inv_h, w_mix, b_mix, g):
    V2 = 7
    CHUNKS = [(v, min(V2, NF - v)) for v in range(0, NF, V2)]
    VM = NF // 3
    NM = VM * NF
    VT = 4
    TURNS = [(v, min(VT, NF - v)) for v in range(0, NF, VT)]
    N2 = 2 * NF
    with Phase(nc, name) as ph:
        idt = ph.sb("ident", [P, P])
        fh = ph.sb("fh", [P, N2])
        ih = ph.sb("ih", [N2, P])
        wm = ph.sb("wm", [P, 2, 2, CH, P])
        wn = ph.sb("wn", [P, 2, CH, P])
        bm = ph.sb("bm", [P, 2, 2, CH])
        b_up = ph.sb("b_up", [P, 2, CH])
        b_dn = ph.sb("b_dn", [P, 2, CH])
        at = [ph.sb(f"a{u}", [P, NF, P]) for u in range(2)]
        z = ph.sb("z", [P, 2, NF * NF])
        o1 = ph.sb("o1", [P, 2, NF * NF])
        o2 = ph.sb("o2", [P, NF, 2, NF])
        up = [ph.sb(f"up{x}", [P, NM]) for x in range(2)]
        dn = [ph.sb(f"dn{x}", [P, NM]) for x in range(2)]
        d = ph.sb("d", [N2, NF, P])
        go = [ph.sb(f"g{x}", [P, VT, P]) for x in range(2)]
        zp = [ph.ps(f"zp{x}", [P, 512]) for x in range(2)]
        mp = [ph.ps(f"mp{x}", [P, 512]) for x in range(2)]
        tp = [ph.ps(f"tp{x}", [P, 512]) for x in range(2)]
        gp = [ph.ps(f"gp{x}", [P, 512]) for x in range(2)]

        consts_in = ph.sem("consts_in")
        zeroed = ph.sem("zeroed")
        consts = ph.sem("consts")
        a_loaded = ph.sems("a_loaded", CH)
        z_made = ph.sem("z_made")
        z_ready = ph.sem("z_ready")
        mixed = ph.sem("mixed")
        mix_read = ph.sem("mix_read")
        shrunk = ph.sem("shrunk")
        turned = ph.sem("turned")
        d_ready = ph.sem("d_ready")
        g_made = ph.sem("g_made")
        g_ready = ph.sem("g_ready")
        stored = ph.sems("stored", 2)
        block = ph.block()
        MIX = 12
        CONSTS = 5
        PER_STORE = [sum(1 + (max(v, 1) < min(v + nv, NF - 1)) for k, (v, nv) in enumerate(TURNS) if k % 2 == x)
                     for x in range(2)]
        units = [(b, j) for b in range(B) for j in range(CH)]

        @block.sync
        def _(sp):
            def load(n):
                b, j = units[n]
                cols = slice(j * P, (j + 1) * P)
                sp.dma_start(at[j][0:H, :, :], a[b, 0:NF, :, cols].rearrange("v h c -> h v c")).then_inc(a_loaded[j], 16)
                sp.dma_start(at[j][H:2 * H, 1:NF - 1, :], a[b, NF:2 * NF - 2, :, cols].rearrange("v h c -> h v c")).then_inc(a_loaded[j], 16)

            srcs = [(idt[:, :], ident), (fh[:, :], fwd_h), (ih[:, :], inv_h),
                    (wm[:, :, :, :, :].rearrange("p l r j n -> p (l r j) n"), w_mix.rearrange("l r j p n -> p (l r j) n")),
                    (bm[:, :, :, :].rearrange("p l r j -> p l (r j)"), b_mix.rearrange("l p n -> p l n"))]
            assert len(srcs) == CONSTS
            for dst, src in srcs:
                sp.dma_start(dst, src).then_inc(consts_in, 16)
            for n in range(2):
                load(n)
            for n, (b, j) in enumerate(units):
                for k, (v, nv) in enumerate(TURNS):
                    sp.wait_ge(g_ready, n * len(TURNS) + k + 1 + FREE)
                    if k == 0 and 1 <= n and n + 1 < len(units):
                        load(n + 1)
                    cols = slice(j * P, (j + 1) * P)
                    sp.dma_start(g[b, v:v + nv, :, cols].rearrange("v h c -> h v c"), go[k % 2][0:H, 0:nv, :]).then_inc(stored[k % 2], 16)
                    lo, hi = max(v, 1), min(v + nv, NF - 1)
                    if lo < hi:
                        sp.dma_start(g[b, NF - 1 + lo:NF - 1 + hi, :, cols].rearrange("v h c -> h v c"),
                                     go[k % 2][H:2 * H, lo - v:hi - v, :]).then_inc(stored[k % 2], 16)
            for x in range(2):
                sp.wait_ge(stored[x], 16 * PER_STORE[x] * len(units) + FREE)

        def unit_loop(eng):
            with eng.Fori(0, B) as i:
                for j in range(CH):
                    yield i * CH + j, j, i

        @block.tensor
        def _(pe):
            pe.wait_ge(consts_in, 16 * CONSTS)
            pe.wait_ge(consts, 3)
            for n, j, i in unit_loop(pe):
                pe.wait_ge(a_loaded[j], 32 * (i + 1))
                for k, (v, nv) in enumerate(CHUNKS):
                    pe.wait_ge(z_ready, n * len(CHUNKS) + max(k - 1, 0) + FREE)
                    for x in range(nv):
                        last = pe.matmul(zp[k % 2][:, x * N2:(x + 1) * N2], at[j][:, v + x, :], fh[:, :],
                                         start=True, stop=True)
                    last.then_inc(z_made, 1)
                for layer, src in enumerate((z, o1)):
                    for c in range(3):
                        if layer == 0:
                            done = sum(v < VM * (c + 1) for v, _ in CHUNKS)
                            pe.wait_ge(z_ready, n * len(CHUNKS) + done + FREE)
                        else:
                            pe.wait_ge(mix_read, n * MIX + 2 * c + 2 + FREE)
                        cols = slice(c * NM, (c + 1) * NM)
                        for part in range(2):
                            m = 6 * layer + 2 * c + part
                            pe.wait_ge(mix_read, n * MIX + max(m - 1, 0) + FREE)
                            w_im = wn[:, layer, j, :] if part == 0 else wm[:, layer, 1, j, :]
                            pe.matmul(mp[m % 2][:, 0:NM], wm[:, layer, 0, j, :], src[:, part, cols], start=True, stop=False)
                            pe.matmul(mp[m % 2][:, 0:NM], w_im, src[:, 1 - part, cols], start=False, stop=True).then_inc(mixed, 1)
                for k, (v, nv) in enumerate(TURNS):
                    c = min((v + nv - 1) // VM, 2)
                    pe.wait_ge(shrunk, n * 6 + 2 * (c + 1) + FREE)
                    pe.wait_ge(d_ready, n * len(TURNS) + max(k - 1, 0) + FREE)
                    for x in range(nv):
                        last = pe.transpose(tp[k % 2][0:N2, x * P:(x + 1) * P], o2[:, v + x, :, :].rearrange("p r u -> p (r u)"), idt[:, :])
                    last.then_inc(turned, 1)
                for k, (v, nv) in enumerate(TURNS):
                    pe.wait_ge(d_ready, n * len(TURNS) + k + 1 + FREE)
                    pe.wait_ge(g_ready, n * len(TURNS) + max(k - 1, 0) + FREE)
                    pe.matmul(gp[k % 2][:, 0:nv * P], ih[:, :], d[:, v:v + nv, :].rearrange("p v c -> p (v c)"),
                              start=True, stop=True).then_inc(g_made, 1)

        @block.scalar
        def _(act):
            act.sem_inc(mix_read, FREE)
            act.sem_inc(g_ready, FREE)
            for u in range(2):
                act.sem_inc(stored[u], FREE)
            act.wait_ge(consts_in, 16 * CONSTS)
            act.mul(wn[:, :, :, :], wm[:, :, 1, :, :], -1.0).then_inc(consts, 1)
            act.wait_ge(consts, 3)
            for n, j, i in unit_loop(act):
                for m in range(MIX):
                    layer, c, part = m // 6, m % 6 // 2, m % 2
                    act.wait_ge(mixed, n * MIX + m + 1)
                    if layer == 0:
                        act.activation(o1[:, part, c * NM:(c + 1) * NM], mp[m % 2][:, 0:NM], ACT.Relu,
                                       bias=bm[:, 0, part, j:j + 1]).then_inc(mix_read, 1)
                    else:
                        act.wait_ge(shrunk, n * 6 + max(m - 6 - 1, 0) + FREE)
                        act.activation(up[m % 2][:, :], mp[m % 2][:, 0:NM], ACT.Relu, bias=b_up[:, part, j:j + 1])
                        act.activation(dn[m % 2][:, :], mp[m % 2][:, 0:NM], ACT.Relu, bias=b_dn[:, part, j:j + 1],
                                       scale=-1.0).then_inc(mix_read, 1)
                for k, (v, nv) in enumerate(TURNS):
                    act.wait_ge(g_made, n * len(TURNS) + k + 1)
                    if k >= 2:
                        before = sum(1 + (max(a, 1) < min(a + b, NF - 1)) for q, (a, b) in enumerate(TURNS) if q % 2 == k % 2 and q < k)
                    else:
                        before = 0
                    act.wait_ge(stored[k % 2], (n * PER_STORE[k % 2] + before) * 16 + FREE)
                    act.activation(go[k % 2][:, 0:nv, :], gp[k % 2][:, 0:nv * P].rearrange("p (v c) -> p v c", c=P),
                                   ACT.Copy).then_inc(g_ready, 1)

        @block.vector
        def _(dve):
            dve.sem_inc(z_ready, FREE)
            dve.sem_inc(d_ready, FREE)
            dve.sem_inc(shrunk, FREE)
            for u in range(2):
                dve.memset(at[u][H:2 * H, 0:NF:NF - 1, :], 0.0).then_inc(zeroed, 1)
            dve.wait_ge(consts_in, 16 * CONSTS)
            dve.wait_ge(zeroed, 2)
            dve.tensor_scalar(b_up[:, :, :], bm[:, 1, :, :], SHRINK, None, ALU.subtract).then_inc(consts, 1)
            dve.tensor_scalar(b_dn[:, :, :], bm[:, 1, :, :], -1.0, SHRINK, ALU.mult, ALU.subtract).then_inc(consts, 1)
            for n, j, i in unit_loop(dve):
                zv = z[:, :, :].rearrange("p r (v u) -> p v r u", u=NF)
                for k, (v, nv) in enumerate(CHUNKS):
                    dve.wait_ge(z_made, n * len(CHUNKS) + k + 1)
                    dve.tensor_copy(zv[:, v:v + nv, :, :],
                                    zp[k % 2][:, 0:nv * N2].rearrange("p (v r u) -> p v r u", r=2, u=NF)).then_inc(z_ready, 1)
                for m in range(6):
                    c, part = m // 2, m % 2
                    dve.wait_ge(mix_read, n * MIX + 6 + m + 1 + FREE)
                    dve.tensor_tensor(o2[:, c * VM:(c + 1) * VM, part, :], up[m % 2][:, :].rearrange("p (v u) -> p v u", u=NF),
                                      dn[m % 2][:, :].rearrange("p (v u) -> p v u", u=NF), ALU.subtract).then_inc(shrunk, 1)
                for k, (v, nv) in enumerate(TURNS):
                    dve.wait_ge(turned, n * len(TURNS) + k + 1)
                    dve.tensor_copy(d[:, v:v + nv, :].rearrange("p v c -> p (v c)"), tp[k % 2][0:N2, 0:nv * P]).then_inc(d_ready, 1)


def build(nc, a, out):
    def scratch(name, shape, dt=F32):
        return nc.dram_tensor(name, shape, dt).ap()

    tokens = lambda ap: ap.rearrange("b h w c -> (b h w) c")
    image = lambda ap: ap.rearrange("(b h w) c -> b h w c", b=B, h=H)
    ident = a["ident"]
    x0 = tokens(a["x"])
    NHL, HDL, NHG, HDG = 8, C // 8, 4, C // 4

    qk_l = scratch("qk_local", (2, NHL, 2, HDL, T), F16)
    v_l = scratch("v_local", (T, NHL * (2 * HDL + 1)), F16)
    att_l = scratch("att_local", (B, PATCHES, P, C))
    x1 = scratch("x1", (T, C))
    front_phase(nc, "f0", "layer", x0, ident, a["w_qkv0"], a["b_qk0"], a["b_v0"], a["g10"], a["be10"],
                qk_l, v_l, NHL, True)
    local_attention_phase(nc, "l0", qk_l, v_l, ident, a["masks7"], att_l, NHL, 7, HDL ** -0.5)
    tail_phase(nc, "t0", "layer", att_l, x0, ident, a["w_proj0"], a["b_proj0"], x1, True,
               a["g20"], a["be20"], a["w10"], a["b10"], a["w20"], a["b20"])

    spec_a = scratch("spec_a", (B, 2 * NF - 2, H, C))
    spec_g = scratch("spec_g", (B, 2 * NF - 2, H, C))
    x2 = scratch("x2", (T, C))
    w_transform_phase(nc, "wf", image(x1), a["fwd_w"], spec_a)
    frequency_phase(nc, "fq", spec_a, ident, a["fwd_h"], a["inv_h"], a["w_mix"], a["b_mix"], spec_g)
    w_transform_phase(nc, "wi", spec_g, a["inv_w"], image(x2), image(x1))

    qk_2 = scratch("qk_local2", (2, NHL, 2, HDL, T), F16)
    v_2 = scratch("v_local2", (T, NHL * (2 * HDL + 1)), F16)
    att_2 = scratch("att_local2", (B, PATCHES, P, C))
    x3 = scratch("x3", (T, C))
    front_phase(nc, "f2", "arsinh", x2, ident, a["w_qkv2"], a["b_qk2"], a["b_v2"], a["g12"], a["be12"],
                qk_2, v_2, NHL, True)
    local_attention_phase(nc, "l2", qk_2, v_2, ident, a["masks3"], att_2, NHL, 3, HDL ** -0.5)
    tail_phase(nc, "t2", "arsinh", att_2, x2, ident, a["w_proj2"], a["b_proj2"], x3, True,
               a["g22"], a["be22"], a["w12"], a["b12"], a["w22"], a["b22"])

    affine = scratch("affine", (GROUPS, 2, C))
    xn = scratch("xn", (T, C))
    qk_g = scratch("qk_global", (2, NHG, 2, HDG, T), F16)
    v_g = scratch("v_global", (T, NHG * (2 * HDG + 1)), F16)
    att_g = scratch("att_global", (T, C))
    group_stats_phase(nc, "gs", x3, ident, a["ones_blocks"], a["g3"], a["be3"], affine)
    front_phase(nc, "f3", "group", x3, ident, a["w_qkv3"], None, None, None, None, qk_g, v_g, NHG, False,
                affine, xn)
    global_attention_phase(nc, "ga", qk_g, v_g, ident, att_g, NHG, C ** -0.5)
    tail_phase(nc, "t3", "none", att_g, xn, ident, a["w_out3"], a["b_out3"], tokens(out), False)


def lay_out(p):
    p = {k: np.asarray(v) for k, v in p.items()}
    col = lambda v: np.ascontiguousarray(v.reshape(-1, P).T)
    fwd_w, inv_w, fwd_h, inv_h = fourier_matrices()
    a = {
        "x": p["x"], "ident": np.eye(P, dtype=np.float32), "masks7": neighbour_masks(7), "masks3": neighbour_masks(3),
        "ones_blocks": np.kron(np.eye(P // 32), np.full((32, 32), 1 / 32)).astype(np.float32),
        "fwd_w": fwd_w, "inv_w": inv_w, "fwd_h": fwd_h, "inv_h": inv_h,
        "w_mix": block_diagonal(p["L1_conv_w1"], p["L1_conv_w2"]), "b_mix": mix_biases(p["L1_conv_b1"], p["L1_conv_b2"]),
    }
    l0, l2, l3 = (lambda n: p["L0_conv_" + n]), (lambda n: p["L2_conv_" + n]), (lambda n: p["L3_conv_" + n])
    names = {"w_qkv": l0("qkv_w").T, "w_proj": l0("proj_w").T, "b_proj": l0("proj_b"), "w1": l0("fc1_w").T,
             "b1": col(l0("fc1_b")), "w2": l0("fc2_w").T, "b2": l0("fc2_b"),
             "g1": col(l0("ln1_w")), "be1": col(l0("ln1_b")), "g2": col(l0("ln2_w")), "be2": col(l0("ln2_b")),
             "b_qk": col(l0("qkv_b")[:2 * C]), "b_v": l0("qkv_b")[2 * C:]}
    a.update({k + "0": v for k, v in names.items()})
    names = {"w_qkv": l2("qkv_w"), "w_proj": l2("proj_w"), "b_proj": l2("proj_b"), "w1": l2("mlp_w1"),
             "b1": col(l2("mlp_b1")), "w2": l2("mlp_w2"), "b2": l2("mlp_b2"),
             "g1": col(l2("n1_w")), "be1": col(l2("n1_b")), "g2": col(l2("n2_w")), "be2": col(l2("n2_b")),
             "b_qk": col(l2("qkv_b")[:2 * C]), "b_v": l2("qkv_b")[2 * C:]}
    a.update({k + "2": v for k, v in names.items()})
    a.update({"w_qkv3": l3("w_qkv").reshape(C, 4, 3, C // 4).transpose(0, 2, 1, 3).reshape(C, 3 * C),
              "w_out3": l3("w_out"), "b_out3": l3("b_out"), "g3": col(l3("gn_scale")), "be3": col(l3("gn_bias"))})
    return {k: np.ascontiguousarray(v) for k, v in a.items()}


def kernel(**inputs):
    import concourse.bacc as bacc
    from concourse.bass_utils import run_bass_kernel_spmd

    arrays = lay_out(inputs)
    nc = bacc.Bacc("TRN2", target_bir_lowering=False, num_devices=1)
    args = {k: nc.dram_tensor(f"in_{k}", v.shape, mybir.dt.from_np(v.dtype), kind="ExternalInput").ap()
            for k, v in arrays.items()}
    out = nc.dram_tensor("out_image", (B, H, W, C), F32, kind="ExternalOutput").ap()
    build(nc, args, out)
    r = run_bass_kernel_spmd(nc, [{f"in_{k}": v for k, v in arrays.items()}], core_ids=[0])
    return r.results[0]["out_image"]
```
